# Optimizing a Trainium2 kernel written in Bass

```python
import numpy as np
import jax
import jax.numpy as jnp

def _softmax(x, axis=-1):
    return jax.nn.softmax(x, axis=axis)

def _gelu(x):
    return jax.nn.gelu(x, approximate=True)

def _silu(x):
    return jax.nn.silu(x)

def _sigmoid(x):
    return jax.nn.sigmoid(x)

def _layernorm(x, axis=-1, eps=1e-05):
    m = jnp.mean(x, axis=axis, keepdims=True)
    v = jnp.var(x, axis=axis, keepdims=True)
    return (x - m) / jnp.sqrt(v + eps)

def _scatter_add(tgt, idx, src, axis=0):
    return tgt.at[idx].add(src)

def _segment_sum(src, seg, n):
    return jax.ops.segment_sum(src, seg, n)
kernel_name = 'mk_decoder_postln_d2_seqx_r8_d9bbfc'

def setup_inputs(seed: int=0):
    np.random.seed(seed)
    _w = jnp.asarray

    def _rec_inputs():
        import jax
        import jax.numpy as jnp
        _rk = jax.random.key(seed)
        x = -0.0002928 + 1 * jax.random.normal(jax.random.fold_in(_rk, 1), (4, 512, 128), jnp.float32)
        _lenS = 512 - jax.random.randint(jax.random.fold_in(_rk, 7), (4,), 0, max(1, 512 // 4) + 1, jnp.int32)
        _lenS2 = 77 - jax.random.randint(jax.random.fold_in(_rk, 8), (4,), 0, max(1, 77 // 4) + 1, jnp.int32)
        _ctx_1024P = jax.random.normal(jax.random.fold_in(_rk, 11), (4, 16, 128), jnp.float32)
        _ctx_1024c = jax.random.dirichlet(jax.random.fold_in(_rk, 511), 0.3 * jnp.ones((16,), jnp.float32), (4, 77))
        _ctx_1024t = jnp.einsum('bsk,bkd->bsd', _ctx_1024c, _ctx_1024P)
        _ctx_1024t = _ctx_1024t * jax.lax.rsqrt(jnp.mean(jnp.square(_ctx_1024t)) + 1e-12) * 0.953939
        ctx_1024 = -1.39393e-06 + 0.999914 * (_ctx_1024t + 0.3 * jax.random.normal(jax.random.fold_in(_rk, 611), (4, 77, 128), jnp.float32))
        return (x, ctx_1024)
    x, ctx_1024 = _rec_inputs()

    def _L0_attn_setup():
        import jax, jax.numpy as jnp
        import numpy as np
        NUM_HEADS = 16
        CLIP = 16
        key = jax.random.key(seed)
        ks = jax.random.split(key, 7)
        d = 128
        return {'x': jax.random.normal(ks[0], (2, 256, d), dtype=jnp.float32), 'Wq': jax.random.normal(ks[1], (d, d), dtype=jnp.float32) / np.sqrt(d), 'Wk': jax.random.normal(ks[2], (d, d), dtype=jnp.float32) / np.sqrt(d), 'Wv': jax.random.normal(ks[3], (d, d), dtype=jnp.float32) / np.sqrt(d), 'Wo': jax.random.normal(ks[4], (d, d), dtype=jnp.float32) / np.sqrt(d), 'bo': jax.random.normal(ks[5], (d,), dtype=jnp.float32) * 0.01, 'rel_emb': jax.random.normal(ks[6], (CLIP + 1,), dtype=jnp.float32)}
    _L0_attn_all = _L0_attn_setup()
    _L0_attn_in = {k: v for k, v in _L0_attn_all.items() if k in ('Wq', 'Wk', 'Wv', 'Wo', 'bo', 'rel_emb')}
    del _L0_attn_all

    def _L0_xattn_setup():
        import jax, jax.numpy as jnp
        import numpy as np
        D_MODEL = 128
        HEADS = 16
        DK = D_MODEL // HEADS
        B, S = (1, 512)
        key = jax.random.key(seed)
        ks = jax.random.split(key, 11)
        sd = 1.0 / np.sqrt(D_MODEL)
        return {'q': jax.random.normal(ks[0], (B, S, D_MODEL), jnp.float32), 'k': jax.random.normal(ks[1], (B, S, D_MODEL), jnp.float32), 'v': jax.random.normal(ks[2], (B, S, D_MODEL), jnp.float32), 'Wq': jax.random.uniform(ks[3], (D_MODEL, D_MODEL), jnp.float32, -sd, sd), 'bq': jax.random.uniform(ks[4], (D_MODEL,), jnp.float32, -sd, sd), 'Wk': jax.random.uniform(ks[5], (D_MODEL, DK), jnp.float32, -sd, sd), 'bk': jax.random.uniform(ks[6], (DK,), jnp.float32, -sd, sd), 'Wv': jax.random.uniform(ks[7], (D_MODEL, DK), jnp.float32, -sd, sd), 'bv': jax.random.uniform(ks[8], (DK,), jnp.float32, -sd, sd), 'Wo': jax.random.uniform(ks[9], (D_MODEL, D_MODEL), jnp.float32, -sd, sd), 'bo': jax.random.uniform(ks[10], (D_MODEL,), jnp.float32, -sd, sd)}
    _L0_xattn_all = _L0_xattn_setup()
    _L0_xattn_in = {k: v for k, v in _L0_xattn_all.items() if k in ('Wq', 'bq', 'Wk', 'bk', 'Wv', 'bv', 'Wo', 'bo')}
    del _L0_xattn_all

    def _L0_ffn_setup():
        import jax, jax.numpy as jnp
        import numpy as np
        from jax import lax
        N_HEADS = 16
        TOP_K = 2
        N_EXPERTS = 8

        def layer_norm(x, w, b, eps=1e-05):
            mu = jnp.mean(x, axis=-1, keepdims=True)
            var = jnp.mean(jnp.square(x - mu), axis=-1, keepdims=True)
            return (x - mu) * lax.rsqrt(var + eps) * w + b

        def attention(x, w_qkv, b_qkv, w_o, b_o):
            B, T, D = x.shape
            dh = D // N_HEADS
            qkv = x @ w_qkv + b_qkv
            q, k, v = jnp.split(qkv, 3, axis=-1)
            q = q.reshape(B, T, N_HEADS, dh)
            k = k.reshape(B, T, N_HEADS, dh)
            v = v.reshape(B, T, N_HEADS, dh)
            scores = jnp.einsum('bqhd,bkhd->bhqk', q, k) / jnp.sqrt(jnp.float32(dh)).astype(x.dtype)
            probs = jax.nn.softmax(scores, axis=-1)
            ctx = jnp.einsum('bhqk,bkhd->bqhd', probs, v).reshape(B, T, D)
            return ctx @ w_o + b_o

        def moe_ff(x, w_gate, w1, b1, w2, b2):
            B, T, D = x.shape
            t = x.reshape(B * T, D)
            probs = jax.nn.softmax(t @ w_gate, axis=-1)
            tw, ti = lax.top_k(probs, TOP_K)
            tw = tw / jnp.sum(tw, axis=-1, keepdims=True)
            out = jnp.zeros_like(t)
            for e in range(N_EXPERTS):
                we = jnp.sum(jnp.where(ti == e, tw, 0.0), axis=-1)
                h = jax.nn.gelu(t @ w1[e] + b1[e]) @ w2[e] + b2[e]
                out = out + we[:, None] * h
            return out.reshape(B, T, D)
        key = jax.random.key(seed)
        ks = jax.random.split(key, 8)
        B, T, D, H, E = (4, 64, 128, 512, 8)
        s = lambda d: 1.0 / np.sqrt(d)
        return {'x': jax.random.normal(ks[0], (B, T, D), jnp.float32), 'ln1_w': jnp.ones((D,), jnp.float32), 'ln1_b': jnp.zeros((D,), jnp.float32), 'ln2_w': jnp.ones((D,), jnp.float32), 'ln2_b': jnp.zeros((D,), jnp.float32), 'w_qkv': jax.random.normal(ks[1], (D, 3 * D), jnp.float32) * s(D), 'b_qkv': jnp.zeros((3 * D,), jnp.float32), 'w_o': jax.random.normal(ks[2], (D, D), jnp.float32) * s(D), 'b_o': jnp.zeros((D,), jnp.float32), 'w_gate': jax.random.normal(ks[3], (D, E), jnp.float32) * s(D), 'w1': jax.random.normal(ks[4], (E, D, H), jnp.float32) * s(D), 'b1': jnp.zeros((E, H), jnp.float32), 'w2': jax.random.normal(ks[5], (E, H, D), jnp.float32) * s(H), 'b2': jnp.zeros((E, D), jnp.float32)}
    _L0_ffn_all = _L0_ffn_setup()
    _L0_ffn_in = {k: v for k, v in _L0_ffn_all.items() if k in ('ln1_w', 'ln1_b', 'ln2_w', 'ln2_b', 'w_qkv', 'b_qkv', 'w_o', 'b_o', 'w_gate', 'w1', 'b1', 'w2', 'b2')}
    del _L0_ffn_all

    def _L1_attn_setup():
        import jax, jax.numpy as jnp
        import numpy as np
        DIM = 128
        DIM_HEAD = 64
        N_HEADS = 16
        INNER = DIM_HEAD * N_HEADS
        LN_EPS = 1e-05

        def layer_norm(x, gamma, beta):
            mu = jnp.mean(x, axis=-1, keepdims=True)
            var = jnp.var(x, axis=-1, keepdims=True)
            return (x - mu) * jax.lax.rsqrt(var + LN_EPS) * gamma + beta

        def alibi_bias(seq, n_heads):
            n_sequence = jnp.arange(n_heads, 0, -1).astype(jnp.float32)
            head_scalars = 2.0 ** (-8.0 / n_sequence)
            idx = jnp.arange(seq)
            dist = -jnp.abs(idx[:, None] - idx[None, :]).astype(jnp.float32)
            return head_scalars[:, None, None] * dist
        key = jax.random.key(seed)
        ks = jax.random.split(key, 6)
        B, S = (2, 256)
        scale = 0.02
        return {'x': jax.random.normal(ks[0], (B, S, DIM), dtype=jnp.float32), 'ln_gamma': jnp.ones((DIM,), dtype=jnp.float32), 'ln_beta': jnp.zeros((DIM,), dtype=jnp.float32), 'Wq': jax.random.normal(ks[1], (DIM, INNER), dtype=jnp.float32) * scale, 'Wk': jax.random.normal(ks[2], (DIM, INNER), dtype=jnp.float32) * scale, 'Wv': jax.random.normal(ks[3], (DIM, INNER), dtype=jnp.float32) * scale, 'Wo': jax.random.normal(ks[4], (INNER, DIM), dtype=jnp.float32) * scale}
    _L1_attn_all = _L1_attn_setup()
    _L1_attn_in = {k: v for k, v in _L1_attn_all.items() if k in ('ln_gamma', 'ln_beta', 'Wq', 'Wk', 'Wv', 'Wo')}
    del _L1_attn_all

    def _L1_xattn_setup():
        import jax, jax.numpy as jnp
        import numpy as np
        B, Q, K, D = (4, 1500, 1500, 128)
        H, HD = (16, 64)
        key = jax.random.key(seed)
        ks = jax.random.split(key, 10)
        s = 0.02
        return {'inputs_q': jax.random.normal(ks[0], (B, Q, D), jnp.float32), 'inputs_kv': jax.random.normal(ks[1], (B, K, D), jnp.float32), 'Wq': jax.random.normal(ks[2], (D, H, HD), jnp.float32) * s, 'bq': jnp.zeros((H, HD), jnp.float32), 'Wk': jax.random.normal(ks[3], (D, H, HD), jnp.float32) * s, 'bk': jnp.zeros((H, HD), jnp.float32), 'Wv': jax.random.normal(ks[4], (D, H, HD), jnp.float32) * s, 'bv': jnp.zeros((H, HD), jnp.float32), 'Wo': jax.random.normal(ks[5], (H, HD, D), jnp.float32) * s, 'bo': jnp.zeros((D,), jnp.float32)}
    _L1_xattn_all = _L1_xattn_setup()
    _L1_xattn_in = {k: v for k, v in _L1_xattn_all.items() if k in ('Wq', 'bq', 'Wk', 'bk', 'Wv', 'bv', 'Wo', 'bo')}
    del _L1_xattn_all

    def _L1_ffn_setup():
        import jax, jax.numpy as jnp
        import numpy as np
        D_MODEL = 128
        HIDDEN = 256
        N_EXPERTS = 8
        TOP_K = 2
        BATCH = 2
        SEQ = 256
        key = jax.random.key(seed)
        ks = jax.random.split(key, 9)
        s = 0.02
        return {'x': jax.random.normal(ks[0], (BATCH, SEQ, D_MODEL), dtype=jnp.float32), 'w_router': jax.random.normal(ks[1], (D_MODEL, N_EXPERTS), dtype=jnp.float32) * s, 'w1': jax.random.normal(ks[2], (N_EXPERTS, D_MODEL, HIDDEN), dtype=jnp.float32) * s, 'w3': jax.random.normal(ks[3], (N_EXPERTS, D_MODEL, HIDDEN), dtype=jnp.float32) * s, 'w2': jax.random.normal(ks[4], (N_EXPERTS, HIDDEN, D_MODEL), dtype=jnp.float32) * s, 'sw1': jax.random.normal(ks[5], (D_MODEL, HIDDEN), dtype=jnp.float32) * s, 'sw3': jax.random.normal(ks[6], (D_MODEL, HIDDEN), dtype=jnp.float32) * s, 'sw2': jax.random.normal(ks[7], (HIDDEN, D_MODEL), dtype=jnp.float32) * s}
    _L1_ffn_all = _L1_ffn_setup()
    _L1_ffn_in = {k: v for k, v in _L1_ffn_all.items() if k in ('w_router', 'w1', 'w3', 'w2', 'sw1', 'sw3', 'sw2')}
    del _L1_ffn_all
    return {'x': x, 'ctx_1024': ctx_1024, 'L0_attn_Wq': _L0_attn_in['Wq'], 'L0_attn_Wk': _L0_attn_in['Wk'], 'L0_attn_Wv': _L0_attn_in['Wv'], 'L0_attn_Wo': _L0_attn_in['Wo'], 'L0_attn_bo': _L0_attn_in['bo'], 'L0_attn_rel_emb': _L0_attn_in['rel_emb'], 'L0_xattn_Wq': _L0_xattn_in['Wq'], 'L0_xattn_bq': _L0_xattn_in['bq'], 'L0_xattn_Wk': _L0_xattn_in['Wk'], 'L0_xattn_bk': _L0_xattn_in['bk'], 'L0_xattn_Wv': _L0_xattn_in['Wv'], 'L0_xattn_bv': _L0_xattn_in['bv'], 'L0_xattn_Wo': _L0_xattn_in['Wo'], 'L0_xattn_bo': _L0_xattn_in['bo'], 'L0_ffn_ln1_w': _L0_ffn_in['ln1_w'], 'L0_ffn_ln1_b': _L0_ffn_in['ln1_b'], 'L0_ffn_ln2_w': _L0_ffn_in['ln2_w'], 'L0_ffn_ln2_b': _L0_ffn_in['ln2_b'], 'L0_ffn_w_qkv': _L0_ffn_in['w_qkv'], 'L0_ffn_b_qkv': _L0_ffn_in['b_qkv'], 'L0_ffn_w_o': _L0_ffn_in['w_o'], 'L0_ffn_b_o': _L0_ffn_in['b_o'], 'L0_ffn_w_gate': _L0_ffn_in['w_gate'], 'L0_ffn_w1': _L0_ffn_in['w1'], 'L0_ffn_b1': _L0_ffn_in['b1'], 'L0_ffn_w2': _L0_ffn_in['w2'], 'L0_ffn_b2': _L0_ffn_in['b2'], 'L1_attn_ln_gamma': _L1_attn_in['ln_gamma'], 'L1_attn_ln_beta': _L1_attn_in['ln_beta'], 'L1_attn_Wq': _L1_attn_in['Wq'], 'L1_attn_Wk': _L1_attn_in['Wk'], 'L1_attn_Wv': _L1_attn_in['Wv'], 'L1_attn_Wo': _L1_attn_in['Wo'], 'L1_xattn_Wq': _L1_xattn_in['Wq'], 'L1_xattn_bq': _L1_xattn_in['bq'], 'L1_xattn_Wk': _L1_xattn_in['Wk'], 'L1_xattn_bk': _L1_xattn_in['bk'], 'L1_xattn_Wv': _L1_xattn_in['Wv'], 'L1_xattn_bv': _L1_xattn_in['bv'], 'L1_xattn_Wo': _L1_xattn_in['Wo'], 'L1_xattn_bo': _L1_xattn_in['bo'], 'L1_ffn_w_router': _L1_ffn_in['w_router'], 'L1_ffn_w1': _L1_ffn_in['w1'], 'L1_ffn_w3': _L1_ffn_in['w3'], 'L1_ffn_w2': _L1_ffn_in['w2'], 'L1_ffn_sw1': _L1_ffn_in['sw1'], 'L1_ffn_sw3': _L1_ffn_in['sw3'], 'L1_ffn_sw2': _L1_ffn_in['sw2']}

def reference(x, ctx_1024, L0_attn_Wq, L0_attn_Wk, L0_attn_Wv, L0_attn_Wo, L0_attn_bo, L0_attn_rel_emb, L0_xattn_Wq, L0_xattn_bq, L0_xattn_Wk, L0_xattn_bk, L0_xattn_Wv, L0_xattn_bv, L0_xattn_Wo, L0_xattn_bo, L0_ffn_ln1_w, L0_ffn_ln1_b, L0_ffn_ln2_w, L0_ffn_ln2_b, L0_ffn_w_qkv, L0_ffn_b_qkv, L0_ffn_w_o, L0_ffn_b_o, L0_ffn_w_gate, L0_ffn_w1, L0_ffn_b1, L0_ffn_w2, L0_ffn_b2, L1_attn_ln_gamma, L1_attn_ln_beta, L1_attn_Wq, L1_attn_Wk, L1_attn_Wv, L1_attn_Wo, L1_xattn_Wq, L1_xattn_bq, L1_xattn_Wk, L1_xattn_bk, L1_xattn_Wv, L1_xattn_bv, L1_xattn_Wo, L1_xattn_bo, L1_ffn_w_router, L1_ffn_w1, L1_ffn_w3, L1_ffn_w2, L1_ffn_sw1, L1_ffn_sw3, L1_ffn_sw2):
    import jax
    import jax.numpy as jnp

    def _L0_attn_ref(x, Wq, Wk, Wv, Wo, bo, rel_emb):
        import jax, jax.numpy as jnp
        import numpy as np
        NUM_HEADS = 16
        CLIP = 16
        b, s, d_in = x.shape
        h, hd = (NUM_HEADS, x.shape[-1] // NUM_HEADS)
        q = (x @ Wq).reshape(b, s, h, hd).transpose(0, 2, 1, 3)
        k = (x @ Wk).reshape(b, s, h, hd).transpose(0, 2, 1, 3)
        v = (x @ Wv).reshape(b, s, h, hd).transpose(0, 2, 1, 3)
        r = jnp.arange(s)
        dist = jnp.clip(jnp.abs(r[None, :] - r[:, None]), 0, CLIP)
        a_k = rel_emb[dist]
        scores = jnp.einsum('bhqd,bhkd->bhqk', q, k) * a_k
        causal = jnp.triu(jnp.ones((s, s), dtype=bool), k=1)
        scores = jnp.where(causal, -jnp.inf, scores)
        attn = jax.nn.softmax(scores / np.sqrt(hd), axis=-1)
        ctx = jnp.einsum('bhqk,bhkd->bhqd', attn, v)
        ctx = ctx.transpose(0, 2, 1, 3).reshape(b, s, h * hd)
        return ctx @ Wo + bo

    def _L0_xattn_ref(q, k, v, Wq, bq, Wk, bk, Wv, bv, Wo, bo):
        import jax, jax.numpy as jnp
        import numpy as np
        D_MODEL = 128
        HEADS = 16
        DK = D_MODEL // HEADS
        B, S = (1, 512)
        b, s, d = q.shape
        qp = (q @ Wq + bq).reshape(b, s, HEADS, DK).transpose(0, 2, 1, 3)
        kp = k @ Wk + bk
        vp = v @ Wv + bv
        scores = jnp.einsum('bhqd,bkd->bhqk', qp, kp)
        attn = jax.nn.softmax(scores, axis=-1)
        out = jnp.einsum('bhqk,bkd->bhqd', attn, vp)
        out = out.transpose(0, 2, 1, 3).reshape(b, s, d)
        return out @ Wo + bo

    def _L0_ffn_ref(x, ln1_w, ln1_b, ln2_w, ln2_b, w_qkv, b_qkv, w_o, b_o, w_gate, w1, b1, w2, b2):
        import jax, jax.numpy as jnp
        import numpy as np
        from jax import lax
        N_HEADS = 16
        TOP_K = 2
        N_EXPERTS = 8

        def layer_norm(x, w, b, eps=1e-05):
            mu = jnp.mean(x, axis=-1, keepdims=True)
            var = jnp.mean(jnp.square(x - mu), axis=-1, keepdims=True)
            return (x - mu) * lax.rsqrt(var + eps) * w + b

        def attention(x, w_qkv, b_qkv, w_o, b_o):
            B, T, D = x.shape
            dh = D // N_HEADS
            qkv = x @ w_qkv + b_qkv
            q, k, v = jnp.split(qkv, 3, axis=-1)
            q = q.reshape(B, T, N_HEADS, dh)
            k = k.reshape(B, T, N_HEADS, dh)
            v = v.reshape(B, T, N_HEADS, dh)
            scores = jnp.einsum('bqhd,bkhd->bhqk', q, k) / jnp.sqrt(jnp.float32(dh)).astype(x.dtype)
            probs = jax.nn.softmax(scores, axis=-1)
            ctx = jnp.einsum('bhqk,bkhd->bqhd', probs, v).reshape(B, T, D)
            return ctx @ w_o + b_o

        def moe_ff(x, w_gate, w1, b1, w2, b2):
            B, T, D = x.shape
            t = x.reshape(B * T, D)
            probs = jax.nn.softmax(t @ w_gate, axis=-1)
            tw, ti = lax.top_k(probs, TOP_K)
            tw = tw / jnp.sum(tw, axis=-1, keepdims=True)
            out = jnp.zeros_like(t)
            for e in range(N_EXPERTS):
                we = jnp.sum(jnp.where(ti == e, tw, 0.0), axis=-1)
                h = jax.nn.gelu(t @ w1[e] + b1[e]) @ w2[e] + b2[e]
                out = out + we[:, None] * h
            return out.reshape(B, T, D)
        h = x + attention(layer_norm(x, ln1_w, ln1_b), w_qkv, b_qkv, w_o, b_o)
        return h + moe_ff(layer_norm(h, ln2_w, ln2_b), w_gate, w1, b1, w2, b2)

    def _L1_attn_ref(x, ln_gamma, ln_beta, Wq, Wk, Wv, Wo):
        import jax, jax.numpy as jnp
        import numpy as np
        DIM = 128
        DIM_HEAD = 64
        N_HEADS = 16
        INNER = DIM_HEAD * N_HEADS
        LN_EPS = 1e-05

        def layer_norm(x, gamma, beta):
            mu = jnp.mean(x, axis=-1, keepdims=True)
            var = jnp.var(x, axis=-1, keepdims=True)
            return (x - mu) * jax.lax.rsqrt(var + LN_EPS) * gamma + beta

        def alibi_bias(seq, n_heads):
            n_sequence = jnp.arange(n_heads, 0, -1).astype(jnp.float32)
            head_scalars = 2.0 ** (-8.0 / n_sequence)
            idx = jnp.arange(seq)
            dist = -jnp.abs(idx[:, None] - idx[None, :]).astype(jnp.float32)
            return head_scalars[:, None, None] * dist
        B, S, _ = x.shape
        xn = layer_norm(x, ln_gamma, ln_beta)

        def heads(t):
            return t.reshape(B, S, N_HEADS, DIM_HEAD).transpose(0, 2, 1, 3)
        q = heads(xn @ Wq)
        k = heads(xn @ Wk)
        v = heads(xn @ Wv)
        att = jnp.einsum('bhid,bhjd->bhij', q, k) / DIM_HEAD ** 0.5
        att = att + alibi_bias(S, N_HEADS)[None]
        p = jax.nn.softmax(att, axis=-1)
        out = jnp.einsum('bhij,bhjd->bhid', p, v)
        out = out.transpose(0, 2, 1, 3).reshape(B, S, INNER)
        return out @ Wo

    def _L1_xattn_ref(inputs_q, inputs_kv, Wq, bq, Wk, bk, Wv, bv, Wo, bo):
        import jax, jax.numpy as jnp
        import numpy as np
        B, Q, K, D = (4, 1500, 1500, 128)
        H, HD = (16, 64)
        q = jnp.einsum('bqm,mhd->bqhd', inputs_q, Wq) + bq
        k = jnp.einsum('bkm,mhd->bkhd', inputs_kv, Wk) + bk
        v = jnp.einsum('bkm,mhd->bkhd', inputs_kv, Wv) + bv
        q = q / jnp.sqrt(jnp.asarray(HD, q.dtype))
        attn = jnp.einsum('bqhd,bkhd->bhqk', q, k)
        attn = jax.nn.softmax(attn, axis=-1)
        out = jnp.einsum('bhqk,bkhd->bqhd', attn, v)
        return jnp.einsum('bqhd,hdm->bqm', out, Wo) + bo

    def _L1_ffn_ref(x, w_router, w1, w3, w2, sw1, sw3, sw2):
        import jax, jax.numpy as jnp
        import numpy as np
        D_MODEL = 128
        HIDDEN = 256
        N_EXPERTS = 8
        TOP_K = 2
        BATCH = 2
        SEQ = 256
        b, s, d = x.shape
        xf = x.reshape(b * s, d)
        probs = jax.nn.softmax(xf @ w_router, axis=-1)
        top_vals, top_idx = jax.lax.top_k(probs, TOP_K)
        gates = top_vals / jnp.sum(top_vals, axis=-1, keepdims=True)
        onehot = jax.nn.one_hot(top_idx, N_EXPERTS, dtype=xf.dtype)
        cw = jnp.einsum('tk,tke->te', gates, onehot)
        h1 = jnp.einsum('td,edh->eth', xf, w1)
        h3 = jnp.einsum('td,edh->eth', xf, w3)
        y = jnp.einsum('eth,ehd->etd', jax.nn.silu(h1) * h3, w2)
        out = jnp.einsum('etd,te->td', y, cw)
        out = out + jax.nn.silu(xf @ sw1) * (xf @ sw3) @ sw2
        return out.reshape(b, s, d)
    x = _layernorm(x + _L0_attn_ref(x, L0_attn_Wq, L0_attn_Wk, L0_attn_Wv, L0_attn_Wo, L0_attn_bo, L0_attn_rel_emb), axis=-1)
    x = _layernorm(x + _L0_xattn_ref(x, ctx_1024, ctx_1024, L0_xattn_Wq, L0_xattn_bq, L0_xattn_Wk, L0_xattn_bk, L0_xattn_Wv, L0_xattn_bv, L0_xattn_Wo, L0_xattn_bo), axis=-1)
    x = _layernorm(x + _L0_ffn_ref(x, L0_ffn_ln1_w, L0_ffn_ln1_b, L0_ffn_ln2_w, L0_ffn_ln2_b, L0_ffn_w_qkv, L0_ffn_b_qkv, L0_ffn_w_o, L0_ffn_b_o, L0_ffn_w_gate, L0_ffn_w1, L0_ffn_b1, L0_ffn_w2, L0_ffn_b2), axis=-1)
    x = _layernorm(x + _L1_attn_ref(x, L1_attn_ln_gamma, L1_attn_ln_beta, L1_attn_Wq, L1_attn_Wk, L1_attn_Wv, L1_attn_Wo), axis=-1)
    x = _layernorm(x + _L1_xattn_ref(x, ctx_1024, L1_xattn_Wq, L1_xattn_bq, L1_xattn_Wk, L1_xattn_bk, L1_xattn_Wv, L1_xattn_bv, L1_xattn_Wo, L1_xattn_bo), axis=-1)
    x = _layernorm(x + _L1_ffn_ref(x, L1_ffn_w_router, L1_ffn_w1, L1_ffn_w3, L1_ffn_w2, L1_ffn_sw1, L1_ffn_sw3, L1_ffn_sw2), axis=-1)
    return x

_drawn_inputs = setup_inputs


def setup_inputs(seed=0):
    import zlib

    import numpy as np

    out = dict(_drawn_inputs(seed))
    spreads = {'L0_ffn_ln1_w': (1.0, 0.2),
     'L0_ffn_ln1_b': (0.0, 0.1),
     'L0_ffn_ln2_w': (1.0, 0.2),
     'L0_ffn_ln2_b': (0.0, 0.1),
     'L0_ffn_b_qkv': (0.0, 0.1),
     'L0_ffn_b_o': (0.0, 0.1),
     'L0_ffn_b1': (0.0, 0.339),
     'L0_ffn_b2': (0.0, 0.1),
     'L1_attn_ln_gamma': (1.0, 0.6),
     'L1_attn_ln_beta': (0.0, 0.555),
     'L1_xattn_bq': (0.0, 0.8),
     'L1_xattn_bk': (0.0, 0.8),
     'L1_xattn_bv': (0.0, 0.1),
     'L1_xattn_bo': (0.0, 0.1)}
    factors = {'L0_attn_bo': 2.72,
     'L0_xattn_bq': 2.804,
     'L0_xattn_bk': 8.0,
     'L1_attn_Wq': 8.0,
     'L1_attn_Wk': 8.0,
     'L1_xattn_Wq': 8.0,
     'L1_xattn_Wk': 8.0,
     'L1_ffn_w_router': 8.0,
     'L1_ffn_w1': 8.0,
     'L1_ffn_w3': 8.0,
     'L1_ffn_w2': 8.0,
     'L1_ffn_sw1': 6.99,
     'L1_ffn_sw3': 6.843,
     'L1_ffn_sw2': 6.878}
    for name, (base, spread) in spreads.items():
        noise = np.random.default_rng([zlib.crc32(name.encode()), seed]).standard_normal(out[name].shape)
        drawn = base * np.exp(spread * noise) if base else spread * noise
        out[name] = jnp.asarray(drawn.astype(out[name].dtype))
    for name, factor in factors.items():
        out[name] = (out[name] * factor).astype(out[name].dtype)
    return out
```

```python
import concourse.bass as bass
from concourse import mybir
from contextlib import ExitStack

F32 = mybir.dt.float32
BF16 = mybir.dt.bfloat16
ALU = mybir.AluOpType
ACT = mybir.ActivationFunctionType
AX = mybir.AxisListType

P = 128
B = 4
S = 512
QT = S // P
NT = B * QT
TOK = B * S
KC = 77
H = 16
HD8 = P // H
HD64 = 64
PAIRS = H // 2
GH = 4
GROUPS = H // GH
STEPS = B * GROUPS
CW = P // GH
NPART = 3
SROWS = 96
NE = 8
HID0 = 512
HID1 = 256
CLIP = 16
EPS = 1e-5
MASKED = -1e30
LOWEST = -3e38
ISQ8 = float(HD8) ** -0.5
ISQ64 = float(HD64) ** -0.5


class Chain:

    def __init__(self, sem, base=0):
        self.sem, self.base, self.n = sem, base, 0

    def inc(self, instruction):
        instruction.then_inc(self.sem, 1)
        self.n += 1

    def value(self):
        return self.base + self.n

    def wait(self, engine):
        engine.wait_ge(self.sem, self.base + self.n)


def peeled(engine, count, body):
    body(0, True, False)
    with engine.Fori(1, count - 1) as t:
        body(t, False, False)
    body(count - 1, False, True)


def first_then_loop(engine, count, body):
    body(0)
    with engine.Fori(1, count) as t:
        body(t)


def wait(engine, sem, value):
    if not isinstance(value, int) or value > 0:
        engine.wait_ge(sem, value)


class Core:

    def __init__(self, nc, ctx):
        self.nc, self.ctx, self.sems = nc, ctx, []
        self.X = self.sb("X", [P, NT, P], F32)
        self.XT = self.sb("XT", [P, TOK], F32)
        self.CTX = self.sb("CTX", [P, NT, P], F32)
        self.CTT = self.sb("CTT", [P, B * KC], F32)
        self.ident = self.sb("ident", [P, P], F32)
        self.VG = self.sb("VG", [P, QT, GH, CW], F32)
        self.neghalf = self.sb("neghalf", [P, 4], F32)
        self.ps_s = ctx.enter_context(nc.psum_tensor("ps_s", [P, 4, 512], F32))
        self.ps_t = ctx.enter_context(nc.psum_tensor("ps_t", [P, 2, 512], F32))
        self.ps_v = ctx.enter_context(nc.psum_tensor("ps_v", [P, 512], F32))
        self.ps_f = ctx.enter_context(nc.psum_tensor("ps_f", [P, 512], F32))

    def sb(self, name, shape, dt, ctx=None):
        return (ctx or self.ctx).enter_context(self.nc.sbuf_tensor(name, shape, dt))

    def sem(self, name):
        self.sems.append(self.nc.alloc_semaphore(name=name))
        return self.sems[-1]

    def recycle_semaphores(self):
        self.nc.clear_and_free_semaphores(self.sems)
        self.nc.all_engine_barrier()
        self.sems = []


def row(ap, parts=P):
    n = ap.shape[0]
    return ap.rearrange("(a n) -> a n", a=1).broadcast_to([parts, n])


def col(ap):
    return ap.rearrange("(p a) -> p a", a=1)


def setup(c, x, ctx_in):
    nc = c.nc
    with ExitStack() as own:
        CR = c.sb("CR", [KC, B, P], F32, own)
        loaded, made, turned, copied = (c.sem(f"setup_{n}") for n in ("loaded", "made", "turned", "copied"))
        with nc.Block() as block:
            @block.sync
            def _(sp):
                for b in range(B):
                    sp.dma_start(c.X[:, b * QT:(b + 1) * QT, :],
                                 x[b].rearrange("(n p) d -> p n d", p=P)).then_inc(loaded, 16)
                sp.dma_start(CR[:, :, :], ctx_in.rearrange("b k d -> k b d")).then_inc(loaded, 16)

            @block.gpsimd
            def _(pool):
                nc.gpsimd.memset(c.ident[:, :], 0.0).then_inc(made, 1)
                pool.wait_ge(made, 1)
                nc.gpsimd.affine_select(out=c.ident[:, :], in_=c.ident[:, :], compare_op=ALU.not_equal, fill=1.0,
                                        base=0, pattern=[[-1, P]], channel_multiplier=1).then_inc(made, 1)
                nc.gpsimd.memset(c.VG[:, :, :, :], 1.0)
                nc.gpsimd.memset(c.neghalf[:, :], -0.5).then_inc(made, 1)

            @block.tensor
            def _(pe):
                pe.wait_ge(made, 2)
                pe.wait_ge(loaded, 16 * (B + 1))
                for b in range(B):
                    for i in range(QT):
                        last = nc.tensor.transpose(c.ps_s[:, b, i * P:(i + 1) * P], c.X[:, b * QT + i, :], c.ident[:, :])
                    last.then_inc(turned, 1)
                for b in range(B):
                    last = nc.tensor.transpose(c.ps_t[:, 0, b * KC:(b + 1) * KC], CR[:, b, :], c.ident[0:KC, 0:KC])
                last.then_inc(turned, 1)

            @block.vector
            def _(dve):
                for b in range(B):
                    dve.wait_ge(turned, b + 1)
                    nc.vector.tensor_copy(c.XT[:, b * S:(b + 1) * S], c.ps_s[:, b, :])
                dve.wait_ge(turned, B + 1)
                nc.vector.tensor_copy(c.CTT[:, :], c.ps_t[:, 0, 0:B * KC])


SPLIT_OPS = 5


def split_parts(nc, dve, chain, full, part):
    chain.inc(nc.vector.tensor_copy(part(0), full))
    chain.wait(dve)
    for i in (1, 2):
        chain.inc(nc.vector.tensor_tensor(full, full, part(i - 1), ALU.subtract))
        chain.wait(dve)
        chain.inc(nc.vector.tensor_copy(part(i), full))
        chain.wait(dve)


def narrow_projections(c, tag, own, wq, wk, wv, bq=None, bk=None, bv=None, qscale=1.0, scratch=None):
    nc = c.nc
    W = c.sb(f"{tag}_W", [P, 3, P], F32, own)
    BQK = c.sb(f"{tag}_BQK", [P, 2], F32, own)
    BV = c.sb(f"{tag}_BV", [P, P], F32, own)
    FULL = c.sb(f"{tag}_FULL", [P, 2, S], F32, own)
    PARTS = c.sb(f"{tag}_PARTS", [P, 2, NPART, S], BF16, own)
    kinds = [0] if wk is None else [0, 1]
    items = [(b, w) for b in range(B) for w in kinds]
    s_w, s_bias, s_proj, s_full, s_split, s_v, s_vn = (
        c.sem(f"{tag}_p{n}") for n in ("w", "bias", "proj", "full", "split", "v", "vn"))
    s_store = [c.sem(f"{tag}_store{i}") for i in range(2)]
    weights = [w for w in (wq, wk, wv) if w is not None]
    biases = [w for w in (bq, bk, bv) if w is not None]

    with nc.Block() as block:
        @block.sync
        def _(sp):
            for i, w in enumerate((wq, wk, wv)):
                if w is not None:
                    sp.dma_start(W[:, i, :], w).then_inc(s_w, 16)
            for i, v in enumerate((bq, bk)):
                if v is not None:
                    sp.dma_start(BQK[:, i:i + 1], col(v)).then_inc(s_w, 16)
            if bv is not None:
                sp.dma_start(BV[:, :], row(bv)).then_inc(s_w, 16)
            for i, (b, w) in enumerate(items):
                sp.wait_ge(s_split, SPLIT_OPS * (i + 1))
                sp.dma_start(scratch[b, w], PARTS[:, i % 2]).then_inc(s_store[i % 2], 16)
            for i in range(2):
                sp.wait_ge(s_store[i], 16 * (len(items) // 2))

        @block.tensor
        def _(pe):
            pe.wait_ge(s_w, 16 * (len(weights) + len(biases)))
            for i, (b, w) in enumerate(items):
                if i >= 2:
                    pe.wait_ge(s_full, i - 1)
                nc.tensor.matmul(c.ps_s[:, i % 2, :], W[:, w, :], c.XT[:, b * S:(b + 1) * S],
                                 start=True, stop=True).then_inc(s_proj, 1)
                if w == 0 and wv is not None:
                    if b >= 2:
                        pe.wait_ge(s_vn, b - 1)
                    for m in range(QT):
                        n = b * QT + m
                        last = nc.tensor.matmul(c.ps_t[:, b % 2, m * P:(m + 1) * P], c.XT[:, n * P:(n + 1) * P],
                                                W[:, 2, :], start=True, stop=True)
                    last.then_inc(s_v, 1)

        @block.scalar
        def _(act):
            if bq is not None:
                act.wait_ge(s_bias, 1)
            for i, (b, w) in enumerate(items):
                act.wait_ge(s_proj, i + 1)
                if i >= 2:
                    act.wait_ge(s_split, SPLIT_OPS * (i - 1))
                scale = qscale if w == 0 else 1.0
                if (bq, bk)[w] is None:
                    ins = nc.scalar.activation(FULL[:, i % 2, :], c.ps_s[:, i % 2, :], ACT.Copy, scale=scale)
                else:
                    ins = nc.scalar.activation(FULL[:, i % 2, :], c.ps_s[:, i % 2, :], ACT.Identity,
                                               bias=BQK[:, w:w + 1], scale=scale)
                ins.then_inc(s_full, 1)

        @block.vector
        def _(dve):
            chain = Chain(s_split)
            dve.wait_ge(s_w, 16 * (len(weights) + len(biases)))
            if bq is not None:
                nc.vector.tensor_scalar(BQK[:, 0:1], BQK[:, 0:1], qscale, None, ALU.mult).then_inc(s_bias, 1)
            for i, (b, w) in enumerate(items):
                dve.wait_ge(s_full, i + 1)
                if i >= 2:
                    dve.wait_ge(s_store[i % 2], 16 * (i // 2))
                part = lambda j: PARTS[:, i % 2, j, :]
                split_parts(nc, dve, chain, FULL[:, i % 2, :], part)
                if w == 0 and wv is not None:
                    dve.wait_ge(s_v, b + 1)
                    dst = c.VN[:, b * QT:(b + 1) * QT, :]
                    src = c.ps_t[:, b % 2, :].rearrange("p (m d) -> p m d", m=QT)
                    if bv is None:
                        nc.vector.tensor_copy(dst, src).then_inc(s_vn, 1)
                    else:
                        nc.vector.tensor_tensor(dst, src, BV[:, :].rearrange("p (a d) -> p a d", a=1).broadcast_to([P, QT, P]),
                                                ALU.add).then_inc(s_vn, 1)


def load_stacks(nc, sp, scratch, b, QX, KX, sem):
    slot = slice((b % 2) * H, (b % 2 + 1) * H)
    for i in range(NPART):
        for j in range(NPART):
            r = HD8 * (NPART * i + j)
            for w, part, stack in ((0, i, QX), (1, j, KX)):
                if stack is not None:
                    sp.dma_start(stack[r:r + HD8, slot, :],
                                 scratch[b, w, :, part, :].rearrange("(h d) t -> d h t", d=HD8)).then_inc(sem, 16)


def gather_values(c, tag, own, pool, t, first, s_pv, s_vg, cross_values=None):
    nc = c.nc
    if not first:
        pool.wait_ge(s_pv, t)
    if cross_values is None:
        for kt in range(QT):
            src = c.VN[:, bass.ds((t // GROUPS) * QT + kt, 1), bass.ds((t % GROUPS) * GH * HD8, GH * HD8)]
            last = nc.gpsimd.tensor_copy(c.VG[:, kt, :, 0:HD8], src.rearrange("p a (h d) -> p (a h) d", d=HD8))
    else:
        last = nc.gpsimd.tensor_copy(c.VG[0:SROWS, 0, 0:1, 0:HD8], cross_values[:, bass.ds(t // GROUPS, 1), :])
    last.then_inc(s_vg, 1)


def group_end_act(c, act, t, s_pv, s_ct, s_ftr, CT4, first=False):
    act.wait_ge(s_pv, t + 1)
    if not first:
        act.wait_ge(s_ftr, t)
    c.nc.scalar.activation(CT4[:, :], c.ps_v[:, :], ACT.Copy).then_inc(s_ct, 1)


def group_end_pe(c, pe, t, s_ct, s_ctx, s_ftr, CT4, first=False):
    pe.wait_ge(s_ct, t + 1)
    if not first:
        pe.wait_ge(s_ctx, t)
    for i in range(QT):
        last = c.nc.tensor.transpose(c.ps_f[:, i * P:(i + 1) * P], CT4[:, i * P:(i + 1) * P], c.ident[:, :])
    last.then_inc(s_ftr, 1)


def group_end_dve(c, dve, t, s_ftr, s_rden, s_ctx, RDEN):
    nc = c.nc
    dve.wait_ge(s_ftr, t + 1)
    sums = c.ps_f[:, :].rearrange("p (q h w) -> p q h w", q=QT, h=GH)
    nc.vector.reciprocal(RDEN[:, :, :], sums[:, :, :, HD8]).then_inc(s_rden, 1)
    dve.wait_ge(s_rden, t + 1)
    out = c.CTX[:, bass.ds((t // GROUPS) * QT, QT), bass.ds((t % GROUPS) * GH * HD8, GH * HD8)]
    nc.vector.tensor_tensor(out.rearrange("p q (h d) -> p q h d", d=HD8), sums[:, :, :, 0:HD8],
                            RDEN[:, :, :].rearrange("p q (h a) -> p q h a", a=1).broadcast_to([P, QT, GH, HD8]),
                            ALU.mult).then_inc(s_ctx, 1)


def narrow_attention(c, tag, own, QX, KX, scratch, s_qx, causal=None):
    nc = c.nc
    PR = c.sb(f"{tag}_PR", [P, 2, QT, S], F32, own)
    PT = c.sb(f"{tag}_PT", [P, GH, QT, S], F32, own)
    CT4 = c.sb(f"{tag}_CT4", [P, S], F32, own)
    NM = c.sb(f"{tag}_NM", [P, 2, QT], F32, own)
    M1 = c.sb(f"{tag}_M1", [P, QT], F32, own)
    M2 = c.sb(f"{tag}_M2", [P, QT], F32, own)
    RDEN = c.sb(f"{tag}_RDEN", [P, QT, GH], F32, own)
    (scores, maxed, exped, turned, out_dve, out_act, products, s_vg, s_ct, s_ftr, s_rden, s_ctx, s_rel) = (
        c.sem(f"{tag}_{n}") for n in ("scores", "maxed", "exped", "turned", "out_dve", "out_act", "products",
                                      "vg", "ct", "ftr", "rden", "ctx", "rel"))
    keys = (lambda qt: (qt + 1) * P) if causal else (lambda qt: S)

    def score_pair(pe, t, j, pair, first):
        n = t * GH + j
        if pair == 0 and j == 0:
            pe.wait_ge(s_qx, (t // GROUPS + 1) * 18 * 16)
        if not first:
            if causal:
                pe.wait_ge(maxed, 2 * (n - 1) + pair + 1)
            else:
                pe.wait_ge(exped, QT * (n - 1) + 2 * pair + 2)
        head = (t % (2 * GROUPS)) * GH + j
        for qt in (2 * pair, 2 * pair + 1):
            last = nc.tensor.matmul(c.ps_s[:, qt, 0:keys(qt)], QX[:, bass.ds(head, 1), qt * P:(qt + 1) * P],
                                    KX[:, bass.ds(head, 1), 0:keys(qt)], start=True, stop=True)
        last.then_inc(scores, 1)

    def turn(pe, t, j, qt, first):
        n = t * GH + j
        pe.wait_ge(exped, QT * n + qt + 1)
        if not (first and qt < 2):
            pe.wait_ge((out_dve, out_act)[qt % 2], 2 * n + qt // 2)
        for kt in range(keys(qt) // P):
            last = nc.tensor.transpose(c.ps_t[:, qt % 2, kt * P:(kt + 1) * P], PR[:, j % 2, qt, kt * P:(kt + 1) * P],
                                       c.ident[:, :])
        last.then_inc(turned, 1)

    def take(engine, t, j, qt):
        n = t * GH + j
        engine.wait_ge(turned, QT * n + qt + 1)
        if j == 0:
            engine.wait_ge(products, t)
        k = keys(qt) // P
        dst = PT[:, j, 0:k, qt * P:(qt + 1) * P]
        src = c.ps_t[:, qt % 2, 0:k * P].rearrange("p (k q) -> p k q", q=P)
        if qt % 2:
            nc.scalar.activation(dst, src, ACT.Copy).then_inc(out_act, 1)
        else:
            nc.vector.tensor_copy(dst, src).then_inc(out_dve, 1)

    def maxima(dve, t, j, pair):
        n = t * GH + j
        if causal:
            dve.sem_clear(s_rel)
        dve.wait_ge(scores, 2 * n + pair + 1)
        if not causal:
            nc.vector.tensor_reduce(NM[:, j % 2, 2 * pair:2 * pair + 2], c.ps_s[:, 2 * pair:2 * pair + 2, :],
                                    AX.X, ALU.max, negate=True).then_inc(maxed, 1)
            return
        TAB, MASK, _ = causal
        own_ops = Chain(s_rel)
        tiles = (2 * pair, 2 * pair + 1)
        for qt in tiles:
            d = slice(qt * P, (qt + 1) * P)
            own_ops.inc(nc.vector.tensor_tensor(PR[:, j % 2, qt, d], c.ps_s[:, qt, d], TAB[:, 3 * P:4 * P], ALU.mult))
        own_ops.wait(dve)
        for qt in tiles:
            d = slice(qt * P, (qt + 1) * P)
            own_ops.inc(nc.vector.tensor_tensor_reduce(
                out=PR[:, j % 2, qt, d], in0=PR[:, j % 2, qt, d], in1=MASK[:, :], scale=1.0, scalar=LOWEST,
                op0=ALU.add, op1=ALU.max, accum_out=(M1 if qt else M2)[:, qt:qt + 1]))
        own_ops.wait(dve)
        for qt in tiles:
            if qt:
                d = slice(0, qt * P)
                own_ops.inc(nc.vector.tensor_tensor_reduce(
                    out=PR[:, j % 2, qt, d], in0=c.ps_s[:, qt, d], in1=TAB[:, (3 - qt) * P:3 * P], scale=1.0,
                    scalar=M1[:, qt:qt + 1], op0=ALU.mult, op1=ALU.max, accum_out=M2[:, qt:qt + 1]))
        own_ops.wait(dve)
        nc.vector.tensor_scalar(NM[:, j % 2, 2 * pair:2 * pair + 2], M2[:, 2 * pair:2 * pair + 2], -1.0, None,
                                ALU.mult).then_inc(maxed, 1)

    def probabilities(act, t, j, qt):
        n = t * GH + j
        act.wait_ge(maxed, 2 * n + qt // 2 + 1)
        k = keys(qt)
        src = PR[:, j % 2, qt, 0:k] if causal else c.ps_s[:, qt, :]
        nc.scalar.activation(PR[:, j % 2, qt, 0:k], src, ACT.Exp, bias=NM[:, j % 2, qt:qt + 1]).then_inc(exped, 1)

    def after(t, j):
        return (t, j + 1) if j + 1 < GH else (t + 1, 0)

    with nc.Block() as block:
        @block.sync
        def _(sp):
            for b in range(2, B):
                sp.wait_ge(s_qx, b * 18 * 16)
                sp.wait_ge(scores, 2 * H * (b - 1))
                load_stacks(nc, sp, scratch, b, QX, KX, s_qx)

        @block.gpsimd
        def _(pool):
            def step(t, first, last):
                gather_values(c, tag, own, pool, t, first, products, s_vg)
            peeled(pool, STEPS, step)

        @block.tensor
        def _(pe):
            score_pair(pe, 0, 0, 0, True)
            score_pair(pe, 0, 0, 1, True)

            def step(t, first, last):
                for j in range(GH):
                    ahead = after(t, j)
                    more = not (last and j == GH - 1)
                    for pair in range(2):
                        turn(pe, t, j, 2 * pair, first and j == 0)
                        turn(pe, t, j, 2 * pair + 1, first and j == 0)
                        if more:
                            score_pair(pe, *ahead, pair, False)
                    if j == 0 and not first:
                        group_end_pe(c, pe, t - 1, s_ct, s_ctx, s_ftr, CT4)
                pe.wait_ge(out_dve, 2 * GH * (t + 1))
                pe.wait_ge(out_act, 2 * GH * (t + 1))
                pe.wait_ge(s_vg, t + 1)
                if not first:
                    pe.wait_ge(s_ct, t)
                for kt in range(QT):
                    q0 = kt * P if causal else 0
                    for j in range(GH):
                        mm = nc.tensor.matmul(c.ps_v[j * CW:(j + 1) * CW, q0:S], c.VG[:, kt, j, :],
                                              PT[:, j, kt, q0:S], start=(kt == 0), stop=(kt == QT - 1))
                mm.then_inc(products, 1)
            peeled(pe, STEPS, step)
            group_end_pe(c, pe, STEPS - 1, s_ct, s_ctx, s_ftr, CT4)

        @block.vector
        def _(dve):
            maxima(dve, 0, 0, 0)
            maxima(dve, 0, 0, 1)

            def step(t, first, last):
                for j in range(GH):
                    ahead = after(t, j)
                    more = not (last and j == GH - 1)
                    for pair in range(2):
                        take(dve, t, j, 2 * pair)
                        if more:
                            maxima(dve, *ahead, pair)
                    if j == 0 and not first:
                        group_end_dve(c, dve, t - 1, s_ftr, s_rden, s_ctx, RDEN)
            peeled(dve, STEPS, step)
            group_end_dve(c, dve, STEPS - 1, s_ftr, s_rden, s_ctx, RDEN)

        @block.scalar
        def _(act):
            for qt in range(QT):
                probabilities(act, 0, 0, qt)

            def step(t, first, last):
                for j in range(GH):
                    ahead = after(t, j)
                    more = not (last and j == GH - 1)
                    for pair in range(2):
                        take(act, t, j, 2 * pair + 1)
                        if j == 0 and pair == 0 and not first:
                            group_end_act(c, act, t - 1, products, s_ct, s_ftr, CT4)
                        if more:
                            probabilities(act, *ahead, 2 * pair)
                            probabilities(act, *ahead, 2 * pair + 1)
            peeled(act, STEPS, step)
            group_end_act(c, act, STEPS - 1, products, s_ct, s_ftr, CT4)


def norm_chunk(nc, dve, R, dst, ST, MV, RS, chain, done, s_stats, s_rstd, n):
    for i in range(QT):
        chain.inc(nc.vector.bn_stats(ST[:, i, :], R[:, i, :]))
    chain.wait(dve)
    for i in range(QT):
        last = nc.vector.bn_aggr(MV[:, i, :], ST[:, i, :])
    last.then_inc(s_stats, 1)
    dve.wait_ge(s_rstd, 2 * (n + 1))
    for i in range(QT):
        done.inc(nc.vector.tensor_scalar(dst[:, i, :], R[:, i, :], MV[:, i, 0:1], RS[:, i:i + 1],
                                         ALU.subtract, ALU.mult))


def norm_chunk_pool(c, pool, MV, RS, s_stats, s_rstd, n):
    nc = c.nc
    pool.wait_ge(s_stats, n + 1)
    nc.gpsimd.tensor_scalar(RS[:, :], MV[:, :, 1], EPS, None, ALU.add).then_inc(s_rstd, 1)
    pool.wait_ge(s_rstd, 2 * n + 1)
    nc.gpsimd.tensor_tensor(RS[:, :], RS[:, :], c.neghalf[:, :], ALU.pow).then_inc(s_rstd, 1)


def finish(c, tag, source, wo=None, bias=None, mode="post", pre=None, out=None, OT=None):
    nc = c.nc
    with ExitStack() as own:
        W = c.sb(f"{tag}_fW", [P, P], F32, own)
        BO = c.sb(f"{tag}_fBO", [P, P], F32, own)
        WB = c.sb(f"{tag}_fWB", [P, 2], F32, own)
        CT = c.sb(f"{tag}_fCT", [P, 2, QT, P], F32, own)
        R = c.sb(f"{tag}_fR", [P, QT, P], F32, own)
        R2 = c.sb(f"{tag}_fR2", [P, 2, QT, P], F32, own)
        ST = c.sb(f"{tag}_fST", [P, QT, 6], F32, own)
        MV = c.sb(f"{tag}_fMV", [P, QT, 2], F32, own)
        RS = c.sb(f"{tag}_fRS", [P, QT], F32, own)
        s_w, s_t1, s_ct, s_o, s_sum, s_chain, s_stats, s_rstd, s_n, s_t2, s_xt, s_out = (
            c.sem(f"{tag}_f{n}") for n in ("w", "t1", "ct", "o", "sum", "chain", "stats", "rstd", "n", "t2", "xt", "out"))
        n_w = 16 * ((wo is not None) + (bias is not None) + 2 * (pre is not None))
        norms = 1 if (mode == "inner" or pre is None) else 2
        with nc.Block() as block:
            @block.sync
            def _(sp):
                if wo is not None:
                    sp.dma_start(W[:, :], wo).then_inc(s_w, 16)
                if bias is not None:
                    sp.dma_start(BO[:, :], row(bias)).then_inc(s_w, 16)
                if pre is not None:
                    sp.dma_start(WB[:, 0:1], col(pre[0])).then_inc(s_w, 16)
                    sp.dma_start(WB[:, 1:2], col(pre[1])).then_inc(s_w, 16)
                if out is not None:
                    for b in range(B):
                        sp.wait_ge(s_n, QT * (b + 1))
                        sp.dma_start(out[b].rearrange("(n p) d -> p n d", p=P),
                                     c.X[:, b * QT:(b + 1) * QT, :]).then_inc(s_out, 16)
                    sp.wait_ge(s_out, 16 * B)

            @block.gpsimd
            def _(pool):
                for n in range(norms * B):
                    norm_chunk_pool(c, pool, MV, RS, s_stats, s_rstd, n)

            @block.tensor
            def _(pe):
                if n_w:
                    pe.wait_ge(s_w, n_w)

                def before(b):
                    if source == "x":
                        return
                    src = c.CTX[:, b * QT:(b + 1) * QT, :] if source == "ctx" else OT[:, b, :].rearrange("p (i t) -> p i t", i=QT)
                    if source == "ctx":
                        if b >= 2:
                            pe.wait_ge(s_ct, b - 1)
                        for i in range(QT):
                            last = nc.tensor.transpose(c.ps_s[:, b % 2, i * P:(i + 1) * P], src[:, i, :], c.ident[:, :])
                        last.then_inc(s_t1, 1)
                        pe.wait_ge(s_ct, b + 1)
                    if b >= 2:
                        pe.wait_ge(s_sum, b - 1)
                    for i in range(QT):
                        dst = c.ps_s[:, 2 + b % 2, i * P:(i + 1) * P]
                        if source == "ctx":
                            last = nc.tensor.matmul(dst, CT[:, b % 2, i, :], W[:, :], start=True, stop=True)
                        else:
                            last = nc.tensor.transpose(dst, src[:, i, :], c.ident[:, :])
                    last.then_inc(s_o, 1)

                def behind(b):
                    if out is not None:
                        return
                    pe.wait_ge(s_n, QT * (b + 1))
                    if b >= 2:
                        pe.wait_ge(s_xt, b - 1)
                    for i in range(QT):
                        src = c.X[:, b * QT + i, :] if (mode == "post" and pre is None) else R2[:, b % 2, i, :]
                        last = nc.tensor.transpose(c.ps_t[:, b % 2, i * P:(i + 1) * P], src, c.ident[:, :])
                    last.then_inc(s_t2, 1)

                before(0)
                for b in range(B):
                    if b + 1 < B:
                        before(b + 1)
                    behind(b)

            @block.scalar
            def _(act):
                def before(b):
                    if source == "ctx":
                        act.wait_ge(s_t1, b + 1)
                        if b >= 2:
                            act.wait_ge(s_o, b - 1)
                        nc.scalar.activation(CT[:, b % 2, :, :], c.ps_s[:, b % 2, :].rearrange("p (i t) -> p i t", i=QT),
                                             ACT.Copy).then_inc(s_ct, 1)

                def behind(b):
                    if out is not None:
                        return
                    act.wait_ge(s_t2, b + 1)
                    dst, src = c.XT[:, b * S:(b + 1) * S], c.ps_t[:, b % 2, :]
                    if pre is None:
                        nc.scalar.activation(dst, src, ACT.Copy).then_inc(s_xt, 1)
                    else:
                        nc.scalar.activation(dst, src, ACT.Identity, bias=WB[:, 1:2], scale=WB[:, 0:1]).then_inc(s_xt, 1)
                if n_w:
                    act.wait_ge(s_w, n_w)
                before(0)
                for b in range(B):
                    if b + 1 < B:
                        before(b + 1)
                    behind(b)

            @block.vector
            def _(dve):
                chain, done = Chain(s_chain), Chain(s_n)
                if n_w:
                    dve.wait_ge(s_w, n_w)
                n = 0
                for b in range(B):
                    x = c.X[:, b * QT:(b + 1) * QT, :]
                    r = x
                    if source != "x":
                        dve.wait_ge(s_o, b + 1)
                        o = c.ps_s[:, 2 + b % 2, :].rearrange("p (i t) -> p i t", i=QT)
                        r = R[:, :, :]
                        nc.vector.tensor_tensor(r, x, o, ALU.add).then_inc(s_sum, 1)
                        dve.wait_ge(s_sum, b + 1)
                        if bias is not None:
                            chain.inc(nc.vector.tensor_tensor(
                                r, r, BO[:, :].rearrange("p (a d) -> p a d", a=1).broadcast_to([P, QT, P]), ALU.add))
                            chain.wait(dve)
                    if mode == "inner":
                        chain.inc(nc.vector.tensor_tensor(x, x, r, ALU.add))
                        dst = R2[:, b % 2]
                    else:
                        dst = x
                    if mode == "inner" and b >= 2:
                        dve.wait_ge(s_t2, b - 1)
                    norm_chunk(nc, dve, r, dst, ST, MV, RS, chain, done if norms == 1 else chain, s_stats, s_rstd, n)
                    n += 1
                    if norms == 2:
                        chain.wait(dve)
                        if b >= 2:
                            dve.wait_ge(s_t2, b - 1)
                        norm_chunk(nc, dve, x, R2[:, b % 2], ST, MV, RS, chain, done, s_stats, s_rstd, n)
                        n += 1
                    done.wait(dve)


def distance_tables(c, rel, TAB, MASK, s_mask, own):
    nc = c.nc
    near = QT * P - P - CLIP
    DI = c.sb("rel_DI", [P, QT * P - near], mybir.dt.int32, own)
    D = c.sb("rel_D", [P, QT * P - near], F32, own)
    T = c.sb("rel_T", [P, QT * P - near], F32, own)
    E = c.sb("rel_E", [P, CLIP + 1], F32, own)
    s_e, s_iota, s_chain = c.sem("rel_e"), c.sem("rel_iota"), c.sem("rel_chain")
    with nc.Block() as block:
        @block.sync
        def _(sp):
            sp.dma_start(E[:, :], row(rel)).then_inc(s_e, 16)

        @block.gpsimd
        def _(pool):
            nc.gpsimd.iota(DI[:, :], pattern=[[-1, QT * P - near]], base=(QT - 1) * P - near, channel_multiplier=1)\
                .then_inc(s_iota, 1)
            nc.gpsimd.memset(MASK[:, :], 0.0).then_inc(s_iota, 1)
            pool.wait_ge(s_iota, 2)
            nc.gpsimd.affine_select(out=MASK[:, :], in_=MASK[:, :], compare_op=ALU.is_ge, fill=MASKED,
                                    base=0, pattern=[[-1, P]], channel_multiplier=1).then_inc(s_mask, 1)

        @block.vector
        def _(dve):
            chain = Chain(s_chain)
            dve.wait_ge(s_e, 16)
            dve.wait_ge(s_iota, 1)
            chain.inc(nc.vector.tensor_scalar(E[:, :], E[:, :], ISQ8, None, ALU.mult))
            chain.inc(nc.vector.tensor_copy(D[:, :], DI[:, :]))
            chain.wait(dve)
            chain.inc(nc.vector.tensor_copy(TAB[:, 0:near], E[:, CLIP:CLIP + 1].broadcast_to([P, near])))
            chain.inc(nc.vector.tensor_scalar(TAB[:, near:], D[:, :], float(CLIP), E[:, CLIP:CLIP + 1], ALU.is_ge, ALU.mult))
            chain.wait(dve)
            for r in range(CLIP):
                chain.inc(nc.vector.tensor_scalar(T[:, :], D[:, :], float(r), E[:, r:r + 1], ALU.is_equal, ALU.mult))
                chain.wait(dve)
                chain.inc(nc.vector.tensor_tensor(TAB[:, near:], TAB[:, near:], T[:, :], ALU.add))
                chain.wait(dve)


def first_loads(c, tag, scratch, QX, KX, s_qx):
    nc = c.nc
    s_zero = c.sem(f"{tag}_zero")
    with nc.Block() as block:
        @block.gpsimd
        def _(pool):
            nc.gpsimd.memset(QX[64:SROWS, :, :], 0.0).then_inc(s_zero, 1)
            if KX is not None:
                nc.gpsimd.memset(KX[64:SROWS, :, :], 0.0).then_inc(s_zero, 1)

        @block.sync
        def _(sp):
            sp.wait_ge(s_zero, 1 if KX is None else 2)
            for b in range(2):
                if b:
                    sp.wait_ge(s_qx, (9 if KX is None else 18) * 16)
                load_stacks(nc, sp, scratch, b, QX, KX, s_qx)


def narrow_self_attention(c, tag, wq, wk, wv, scratch, bq=None, bk=None, bv=None, qscale=1.0, rel=None):
    with ExitStack() as own:
        QX = c.sb(f"{tag}_QX", [SROWS, 2 * H, S], BF16, own)
        KX = c.sb(f"{tag}_KX", [SROWS, 2 * H, S], BF16, own)
        c.VN = c.sb(f"{tag}_VN", [P, NT, P], F32, own)
        s_qx = c.sem(f"{tag}_qx")
        causal = None
        if rel is not None:
            TAB = c.sb(f"{tag}_TAB", [P, QT * P], F32, own)
            MASK = c.sb(f"{tag}_MASK", [P, P], F32, own)
            causal = (TAB, MASK, c.sem(f"{tag}_mask"))
            with ExitStack() as brief:
                distance_tables(c, rel, *causal, brief)
        with ExitStack() as brief:
            narrow_projections(c, tag, brief, wq, wk, wv, bq, bk, bv, qscale, scratch)
        first_loads(c, tag, scratch, QX, KX, s_qx)
        narrow_attention(c, tag, own, QX, KX, scratch, s_qx, causal)


def cross_operands(c, tag, wk, bk, wv, bv, KX, VB):
    nc = c.nc
    GR = SROWS // HD8
    with ExitStack() as own:
        WK = c.sb(f"{tag}_WK", [P, HD8], F32, own)
        WKR = c.sb(f"{tag}_WKR", [P, SROWS], F32, own)
        BK = c.sb(f"{tag}_BK", [SROWS, 1], F32, own)
        WV = c.sb(f"{tag}_oWV", [P, HD8], F32, own)
        BV = c.sb(f"{tag}_oBV", [KC, HD8], F32, own)
        G = c.sb(f"{tag}_G", [SROWS, GR], F32, own)
        MK = c.sb(f"{tag}_MK", [SROWS, NPART], F32, own)
        FULL = c.sb(f"{tag}_KF", [SROWS, B * KC], F32, own)
        PARTS = c.sb(f"{tag}_KP", [SROWS, NPART, B * KC], BF16, own)
        s_w, s_g, s_ops, s_k, s_v, s_split = (c.sem(f"{tag}_o{n}") for n in ("w", "g", "ops", "k", "v", "split"))
        with nc.Block() as block:
            @block.sync
            def _(sp):
                sp.dma_start(WK[:, :], wk).then_inc(s_w, 16)
                sp.dma_start(WV[:, :], wv).then_inc(s_w, 16)
                sp.dma_start(BV[:, :], row(bv, KC)).then_inc(s_w, 16)
                for g in range(NPART * NPART):
                    sp.dma_start(BK[g * HD8:(g + 1) * HD8, :], col(bk)).then_inc(s_w, 16)

            @block.gpsimd
            def _(pool):
                nc.gpsimd.memset(VB[:, :, :], 0.0)
                nc.gpsimd.memset(G[:, :], 1.0).then_inc(s_g, 1)
                pool.wait_ge(s_g, 1)
                nc.gpsimd.affine_select(out=G[:, :], in_=G[:, :], compare_op=ALU.is_ge, fill=0.0, base=0,
                                        pattern=[[-HD8, GR]], channel_multiplier=1).then_inc(s_g, 1)
                pool.wait_ge(s_g, 2)
                nc.gpsimd.affine_select(out=G[:, :], in_=G[:, :], compare_op=ALU.is_ge, fill=0.0, base=HD8 - 1,
                                        pattern=[[HD8, GR]], channel_multiplier=-1).then_inc(s_g, 1)

            @block.tensor
            def _(pe):
                pe.wait_ge(s_w, 16 * 12)
                pe.wait_ge(s_ops, 2)
                nc.tensor.matmul(c.ps_s[0:SROWS, 0, 0:B * KC], WKR[:, :], c.CTT[:, :], start=True, stop=True).then_inc(s_k, 1)
                for b in range(B):
                    last = nc.tensor.matmul(c.ps_t[0:KC, 0, b * HD8:(b + 1) * HD8], c.CTT[:, b * KC:(b + 1) * KC], WV[:, :],
                                            start=True, stop=True)
                last.then_inc(s_v, 1)

            @block.vector
            def _(dve):
                ops, split = Chain(s_ops), Chain(s_split)
                dve.wait_ge(s_w, 16 * 12)
                ops.inc(nc.vector.memset(WKR[:, NPART * NPART * HD8:], 0.0))
                ops.inc(nc.vector.tensor_copy(
                    WKR[:, 0:NPART * NPART * HD8].rearrange("p (g d) -> p g d", d=HD8),
                    WK[:, :].rearrange("p (a d) -> p a d", a=1).broadcast_to([P, NPART * NPART, HD8])))
                dve.wait_ge(s_g, 3)
                g = G[:, 0:NPART * NPART].rearrange("p (i j) -> p j i", j=NPART)
                ops.inc(nc.vector.reduce_sum(MK[:, :], g, AX.X))
                dve.wait_ge(s_k, 1)
                rows = NPART * NPART * HD8
                ops.inc(nc.vector.tensor_copy(FULL[:, :], c.ps_s[0:SROWS, 0, 0:B * KC]))
                ops.wait(dve)
                ops.inc(nc.vector.tensor_scalar(FULL[0:rows, :], FULL[0:rows, :], BK[0:rows, :], None, ALU.add))
                ops.wait(dve)
                split_parts(nc, dve, split, FULL[:, :], lambda i: PARTS[:, i, :])
                kx = KX[:, :, :].rearrange("p b k -> p (b k)")
                ops.inc(nc.vector.tensor_scalar(kx, PARTS[:, 0, :], MK[:, 0:1], None, ALU.mult))
                for i in (1, 2):
                    ops.wait(dve)
                    ops.inc(nc.vector.scalar_tensor_tensor(kx, PARTS[:, i, :], MK[:, i:i + 1], kx, ALU.mult, ALU.add))
                dve.wait_ge(s_v, 1)
                nc.vector.tensor_tensor(VB[0:KC, :, :], c.ps_t[0:KC, 0, 0:B * HD8].rearrange("p (b d) -> p b d", b=B),
                                        BV[:, :].rearrange("p (a d) -> p a d", a=1).broadcast_to([KC, B, HD8]), ALU.add)


def narrow_cross(c, tag, own, QX, KX, VB, scratch, s_qx):
    nc = c.nc
    SC = c.sb(f"{tag}_SC", [P, 2, QT, KC], F32, own)
    PR = c.sb(f"{tag}_PR", [P, 2, QT, KC], F32, own)
    PT = c.sb(f"{tag}_PT", [SROWS, GH, S], F32, own)
    CT4 = c.sb(f"{tag}_CT4", [P, S], F32, own)
    M = c.sb(f"{tag}_M", [P, 2, QT], F32, own)
    RDEN = c.sb(f"{tag}_RDEN", [P, QT, GH], F32, own)
    (scores, maxed, lessened, exped, turned, taken, products, s_vg, s_ct, s_ftr, s_rden, s_ctx, s_zero) = (
        c.sem(f"{tag}_{n}") for n in ("scores", "maxed", "lessened", "exped", "turned", "taken", "products",
                                      "vg", "ct", "ftr", "rden", "ctx", "ptzero"))
    NK = GH

    def ahead(t, j, k):
        return (t, j + k) if j + k < GH else (t + 1, j + k - GH)

    def score(pe, t, j, first):
        n = t * GH + j
        if j == 0:
            pe.wait_ge(s_qx, (t // GROUPS + 1) * 9 * 16)
        if not first:
            pe.wait_ge(lessened, n - NK + 1)
        head = (t % (2 * GROUPS)) * GH + j
        for qt in range(QT):
            last = nc.tensor.matmul(c.ps_s[:, j, qt * KC:(qt + 1) * KC], QX[:, bass.ds(head, 1), qt * P:(qt + 1) * P],
                                    KX[:, bass.ds(t // GROUPS, 1), :], start=True, stop=True)
        last.then_inc(scores, 1)

    with nc.Block() as block:
        @block.sync
        def _(sp):
            for b in range(2, B):
                sp.wait_ge(s_qx, b * 9 * 16)
                sp.wait_ge(scores, H * (b - 1))
                load_stacks(nc, sp, scratch, b, QX, None, s_qx)

        @block.gpsimd
        def _(pool):
            nc.gpsimd.memset(PT[64:SROWS, :, :], 0.0).then_inc(s_zero, 1)
            pool.wait_ge(s_zero, 1)

            def step(t, first, last):
                gather_values(c, tag, own, pool, t, first, products, s_vg, VB)
            peeled(pool, STEPS, step)

        @block.tensor
        def _(pe):
            score(pe, 0, 0, True)
            score(pe, 0, 1, True)

            def step(t, first, last):
                for j in range(GH):
                    n = t * GH + j
                    pe.wait_ge(exped, n + 1)
                    if not (first and j < 2):
                        pe.wait_ge(taken, n - 1)
                    for qt in range(QT):
                        mm = nc.tensor.transpose(c.ps_t[0:KC, j % 2, qt * P:(qt + 1) * P], PR[:, j % 2, qt, :], c.ident[:, :])
                    mm.then_inc(turned, 1)
                    if not (last and j >= 2):
                        score(pe, *ahead(t, j, 2), first and j < 2)
                    if j == 1 and not first:
                        group_end_pe(c, pe, t - 1, s_ct, s_ctx, s_ftr, CT4)
                pe.wait_ge(taken, GH * (t + 1))
                pe.wait_ge(s_vg, t + 1)
                if not first:
                    pe.wait_ge(s_ct, t)
                for j in range(GH):
                    mm = nc.tensor.matmul(c.ps_v[j * CW:(j + 1) * CW, :], c.VG[0:SROWS, 0, 0, :], PT[:, j, :],
                                          start=True, stop=True)
                mm.then_inc(products, 1)
            peeled(pe, STEPS, step)
            group_end_pe(c, pe, STEPS - 1, s_ct, s_ctx, s_ftr, CT4)

        @block.vector
        def _(dve):
            def lessen(t, j):
                n = t * GH + j
                dve.wait_ge(scores, n + 1)
                src = c.ps_s[:, j, 0:QT * KC].rearrange("p (q k) -> p q k", q=QT)
                nc.vector.reduce_max(M[:, j % 2, :], src, AX.X).then_inc(maxed, 1)
                dve.wait_ge(maxed, n + 1)
                nc.vector.tensor_tensor(SC[:, j % 2], src, M[:, j % 2, :].rearrange("p (q a) -> p q a", a=1).broadcast_to([P, QT, KC]),
                                        ALU.subtract).then_inc(lessened, 1)
            lessen(0, 0)
            lessen(0, 1)

            def step(t, first, last):
                for j in range(GH):
                    if not (last and j >= 2):
                        nt, nj = ahead(t, j, 2)
                        dve.wait_ge(exped, t * GH + j + 1)
                        lessen(nt, nj)
                    if j == 1 and not first:
                        group_end_dve(c, dve, t - 1, s_ftr, s_rden, s_ctx, RDEN)
            peeled(dve, STEPS, step)
            group_end_dve(c, dve, STEPS - 1, s_ftr, s_rden, s_ctx, RDEN)

        @block.scalar
        def _(act):
            def prob(t, j, first):
                n = t * GH + j
                act.wait_ge(lessened, n + 1)
                if not first:
                    act.wait_ge(turned, n - 1)
                nc.scalar.activation(PR[:, j % 2], SC[:, j % 2], ACT.Exp).then_inc(exped, 1)
            prob(0, 0, True)
            prob(0, 1, True)
            act.wait_ge(s_zero, 1)

            def step(t, first, last):
                for j in range(GH):
                    n = t * GH + j
                    act.wait_ge(turned, n + 1)
                    if j == 0:
                        act.wait_ge(products, t)
                    nc.scalar.activation(PT[0:KC, j, :], c.ps_t[0:KC, j % 2, :], ACT.Copy).then_inc(taken, 1)
                    if not (last and j >= 2):
                        prob(*ahead(t, j, 2), False)
                    if j == 0 and not first:
                        group_end_act(c, act, t - 1, products, s_ct, s_ftr, CT4)
            peeled(act, STEPS, step)
            group_end_act(c, act, STEPS - 1, products, s_ct, s_ftr, CT4)


def narrow_cross_attention(c, tag, wq, bq, wk, bk, wv, bv, scratch):
    with ExitStack() as own:
        QX = c.sb(f"{tag}_QX", [SROWS, 2 * H, S], BF16, own)
        KX = c.sb(f"{tag}_KX", [SROWS, B, KC], BF16, own)
        VB = c.sb(f"{tag}_VB", [SROWS, B, HD8], F32, own)
        s_qx = c.sem(f"{tag}_qx")
        with ExitStack() as brief:
            narrow_projections(c, tag, brief, wq, None, None, bq=bq, scratch=scratch)
        cross_operands(c, tag, wk, bk, wv, bv, KX, VB)
        first_loads(c, tag, scratch, QX, None, s_qx)
        narrow_cross(c, tag, own, QX, KX, VB, scratch, s_qx)


def wide_self_attention(c, tag, wq, wk, wv, wo, OT):
    nc = c.nc
    SPAN = 2 * S - P
    TM = QT * H
    with ExitStack() as own:
        WQ, WK, WV = (c.sb(f"{tag}_W{n}", [P, H * HD64], F32, own) for n in "qkv")
        WO = c.sb(f"{tag}_Wo", [P, PAIRS, P], F32, own)
        BH = c.sb(f"{tag}_BH", [P, H, SPAN], F32, own)
        XB = c.sb(f"{tag}_XB", [P, S], F32, own)
        VB = c.sb(f"{tag}_VB", [P, QT, H * HD64], F32, own)
        Q = c.sb(f"{tag}_Q", [P, 2, S], F32, own)
        KZ = c.sb(f"{tag}_KZ", [P, 2, 2, S], F32, own)
        PR = c.sb(f"{tag}_PR", [P, 2, QT, S], F32, own)
        PT = c.sb(f"{tag}_PT", [P, 2, QT, S], F32, own)
        CT = c.sb(f"{tag}_CT", [P, S], F32, own)
        M = c.sb(f"{tag}_M", [P, 2, QT], F32, own)
        NM = c.sb(f"{tag}_NM", [P, 2, QT], F32, own)
        DEN = c.sb(f"{tag}_DEN", [P, 2, QT], F32, own)
        GO = c.sb(f"{tag}_GO", [P, 1], F32, own)
        RDEN = c.sb(f"{tag}_RDEN", [P, 2, QT], F32, own)
        (s_w, s_made, s_iota, s_xb, s_vproj, v_act, v_dve, proj, q_out, k_out, scores, biased, negated, exped, inverted,
         normed, turned, taken, products, heads_out, added, s_ot) = (
            c.sem(f"{tag}_{n}") for n in
            ("w", "made", "iota", "xb", "vproj", "v_act", "v_dve", "proj", "q_out", "k_out", "scores", "biased", "negated",
             "exped", "inverted", "normed", "turned", "taken", "products", "heads_out", "added", "ot"))
        ps_q, ps_k, ps_o = c.ps_s[:, 2, :], c.ps_f[:, :], c.ps_s[:, 3, :]

        with nc.Block() as block:
            @block.sync
            def _(sp):
                for dst, src in ((WQ, wq), (WK, wk), (WV, wv)):
                    sp.dma_start(dst[:, :], src).then_inc(s_w, 16)
                sp.dma_start(WO[:, :, :], wo.rearrange("(g p) n -> p g n", p=P)).then_inc(s_w, 16)

            @block.gpsimd
            def _(pool):
                DI = BH[:, 0, :].bitcast(mybir.dt.int32)
                nc.gpsimd.memset(KZ[:, :, :, :], 0.0)
                nc.gpsimd.iota(DI, pattern=[[-1, SPAN]], base=S - P, channel_multiplier=1).then_inc(s_iota, 1)

            @block.vector
            def _(dve):
                chain = Chain(s_made)
                T = BH[:, H - 1, :]
                dve.wait_ge(s_iota, 1)
                chain.inc(nc.vector.tensor_copy(BH[:, 1, :], BH[:, 0, :].bitcast(mybir.dt.int32)))
                chain.wait(dve)
                chain.inc(nc.vector.tensor_scalar(BH[:, 2, :], BH[:, 1, :], -1.0, None, ALU.mult))
                chain.wait(dve)
                chain.inc(nc.vector.tensor_tensor(T, BH[:, 1, :], BH[:, 2, :], ALU.min))
                for h in range(H):
                    chain.wait(dve)
                    slope = 2.0 ** (-8.0 / (H - h))
                    chain.inc(nc.vector.tensor_scalar(BH[:, h, :], T, slope, None, ALU.mult))

        with nc.Block() as block:
            @block.tensor
            def _(pe):
                pe.wait_ge(s_w, 16 * 4)

                def project(b, p):
                    if p >= 1:
                        wait(pe, q_out, b * PAIRS + p)
                        wait(pe, k_out, b * H + 2 * p)
                    w = slice(p * P, (p + 1) * P)
                    nc.tensor.matmul(ps_q, WQ[:, w], XB[:, :], start=True, stop=True).then_inc(proj, 1)
                    nc.tensor.matmul(ps_k, WK[:, w], XB[:, :], start=True, stop=True).then_inc(proj, 1)

                def score(b, i, qt):
                    m, p = QT * i + qt, i // 2
                    if i % 2 == 0 and qt == 0:
                        wait(pe, q_out, b * PAIRS + p + 1)
                        wait(pe, k_out, b * H + 2 * p + 2)
                    wait(pe, biased, b * TM + max(m - 1, 0))
                    nc.tensor.matmul(c.ps_s[:, qt % 2, :], Q[:, p % 2, qt * P:(qt + 1) * P], KZ[:, p % 2, i % 2, :],
                                     start=True, stop=True).then_inc(scores, 1)

                def turn(b, i, qt):
                    m = QT * i + qt
                    wait(pe, normed, b * TM + m + 1)
                    wait(pe, taken, b * TM + max(m - 1, 0))
                    for kt in range(QT):
                        mm = nc.tensor.transpose(c.ps_t[:, qt % 2, kt * P:(kt + 1) * P],
                                                 PR[:, i % 2, qt, kt * P:(kt + 1) * P], c.ident[:, :])
                    mm.then_inc(turned, 1)

                def weigh(b, p):
                    wait(pe, taken, b * TM + 2 * QT * (p + 1))
                    wait(pe, heads_out, b * PAIRS + p)
                    for kt in range(QT):
                        for e in range(2):
                            h = 2 * p + e
                            mm = nc.tensor.matmul(c.ps_v[e * HD64:(e + 1) * HD64, :], VB[:, kt, h * HD64:(h + 1) * HD64],
                                                  PT[:, e, kt, :], start=(kt == 0), stop=(kt == QT - 1))
                    mm.then_inc(products, 1)

                def add(b, p):
                    wait(pe, heads_out, b * PAIRS + p + 1)
                    if p == 0:
                        wait(pe, s_ot, b)
                    nc.tensor.matmul(ps_o, WO[:, p, :], CT[:, :], start=(p == 0), stop=(p == PAIRS - 1)).then_inc(added, 1)

                def batch(b):
                    wait(pe, s_xb, b + 1)
                    project(b, 0)
                    for g in range(2 * QT):
                        if g >= 2:
                            wait(pe, (v_act, v_dve)[g % 2], b * QT + g // 2)
                        else:
                            wait(pe, taken, b * TM)
                        nc.tensor.matmul(c.ps_t[:, g % 2, :], XB[:, (g // 2) * P:(g // 2 + 1) * P],
                                         WV[:, (g % 2) * 512:(g % 2 + 1) * 512], start=True, stop=True).then_inc(s_vproj, 1)
                    for qt in range(QT):
                        score(b, 0, qt)
                    wait(pe, v_act, b * QT + QT)
                    wait(pe, v_dve, b * QT + QT)
                    for i in range(H):
                        p = i // 2
                        for qt in range(QT):
                            turn(b, i, qt)
                            if i + 1 < H:
                                score(b, i + 1, qt)
                            if qt == 1 and i % 2 == 0 and p:
                                add(b, p - 1)
                            if qt == 2 and i % 2 == 0 and p + 1 < PAIRS:
                                project(b, p + 1)
                        if i % 2:
                            weigh(b, p)
                    add(b, PAIRS - 1)
                first_then_loop(pe, B, batch)

            @block.vector
            def _(dve):
                def bias(b, h, qt):
                    m = QT * h + qt
                    if h < 2:
                        wait(dve, turned, b * TM)
                    else:
                        wait(dve, turned, b * TM + m - 2 * QT + 1)
                    wait(dve, scores, b * TM + m + 1)
                    nc.vector.memset(GO[:, :], 0.0)
                    nc.vector.tensor_tensor_reduce(
                        out=PR[:, h % 2, qt, :], in0=c.ps_s[:, qt % 2, :], in1=BH[:, h, S - P - qt * P:2 * S - P - qt * P],
                        scale=1.0, scalar=LOWEST, op0=ALU.add, op1=ALU.max, accum_out=M[:, h % 2, qt:qt + 1]).then_inc(biased, 1)
                    wait(dve, biased, b * TM + m + 1)
                    nc.vector.tensor_scalar(NM[:, h % 2, qt:qt + 1], M[:, h % 2, qt:qt + 1], -1.0, None,
                                            ALU.mult).then_inc(negated, 1)

                def norm(b, h, qt):
                    m = QT * h + qt
                    wait(dve, exped, b * TM + m + 1)
                    nc.vector.reciprocal(RDEN[:, h % 2, qt:qt + 1], DEN[:, h % 2, qt:qt + 1]).then_inc(inverted, 1)
                    wait(dve, inverted, b * TM + m + 1)
                    nc.vector.tensor_scalar(PR[:, h % 2, qt, :], PR[:, h % 2, qt, :], RDEN[:, h % 2, qt:qt + 1], None,
                                            ALU.mult).then_inc(normed, 1)

                def head(b, h):
                    for qt in range(QT):
                        bias(b, h, qt)
                        if qt:
                            norm(b, h, qt - 1)
                    norm(b, h, QT - 1)

                def keys_out(b, p):
                    wait(dve, proj, b * H + 2 * p + 2)
                    wait(dve, scores, b * TM + max(2 * QT * (p - 1), 0))
                    for e in range(2):
                        r = slice(e * HD64, (e + 1) * HD64)
                        nc.vector.tensor_copy(KZ[r, p % 2, e, :], ps_k[r, :]).then_inc(k_out, 1)

                def take_heads(b, p):
                    wait(dve, products, b * PAIRS + p + 1)
                    wait(dve, added, b * PAIRS + p)
                    nc.vector.tensor_copy(CT[:, :], c.ps_v[:, :]).then_inc(heads_out, 1)

                def batch(b):
                    wait(dve, s_vproj, b * 2 * QT)
                    wait(dve, proj, b * H)
                    nc.vector.tensor_copy(XB[:, :], c.XT[:, bass.ds(b * S, S)]).then_inc(s_xb, 1)
                    keys_out(b, 0)
                    wait(dve, products, b * PAIRS)
                    for g in range(1, 2 * QT, 2):
                        wait(dve, s_vproj, b * 2 * QT + g + 1)
                        nc.vector.tensor_copy(VB[:, g // 2, 512:1024], c.ps_t[:, 1, :]).then_inc(v_dve, 1)
                    head(b, 0)
                    for i in range(H):
                        p = i // 2
                        if i % 2 == 0 and p:
                            take_heads(b, p - 1)
                        if i + 1 < H:
                            head(b, i + 1)
                        if i % 2 == 0 and p + 1 < PAIRS:
                            keys_out(b, p + 1)
                    take_heads(b, PAIRS - 1)
                first_then_loop(dve, B, batch)

            @block.scalar
            def _(act):
                def exp(b, h, qt):
                    m = QT * h + qt
                    wait(act, negated, b * TM + m + 1)
                    nc.scalar.activation(PR[:, h % 2, qt, :], PR[:, h % 2, qt, :], ACT.Exp, bias=NM[:, h % 2, qt:qt + 1],
                                         accum_out=DEN[:, h % 2, qt:qt + 1]).then_inc(exped, 1)

                def take(b, i, qt):
                    m = QT * i + qt
                    wait(act, turned, b * TM + m + 1)
                    wait(act, products, b * PAIRS + i // 2)
                    nc.scalar.activation(PT[:, i % 2, :, qt * P:(qt + 1) * P],
                                         c.ps_t[:, qt % 2, :].rearrange("p (k q) -> p k q", q=P), ACT.Copy).then_inc(taken, 1)

                def queries_out(b, p):
                    wait(act, proj, b * H + 2 * p + 1)
                    wait(act, scores, b * TM + max(2 * QT * (p - 1), 0))
                    nc.scalar.activation(Q[:, p % 2, :], ps_q, ACT.Copy, scale=ISQ64).then_inc(q_out, 1)

                def batch(b):
                    queries_out(b, 0)
                    wait(act, products, b * PAIRS)
                    for g in range(0, 2 * QT, 2):
                        wait(act, s_vproj, b * 2 * QT + g + 1)
                        nc.scalar.activation(VB[:, g // 2, 0:512], c.ps_t[:, 0, :], ACT.Copy).then_inc(v_act, 1)
                    for qt in range(QT):
                        exp(b, 0, qt)
                    for i in range(H):
                        for qt in range(QT):
                            take(b, i, qt)
                            if i + 1 < H:
                                exp(b, i + 1, qt)
                        if i % 2 == 0 and i // 2 + 1 < PAIRS:
                            queries_out(b, i // 2 + 1)
                    wait(act, added, b * PAIRS + PAIRS)
                    nc.scalar.activation(OT[:, bass.ds(b, 1), :], ps_o, ACT.Copy).then_inc(s_ot, 1)
                first_then_loop(act, B, batch)


def wide_cross_attention(c, tag, wq, bq, wk, bk, wv, bv, wo, bo, OT):
    nc = c.nc
    with ExitStack() as own:
        WQ, WK, WV = (c.sb(f"{tag}_W{n}", [P, H * HD64], F32, own) for n in "qkv")
        WO = c.sb(f"{tag}_Wo", [P, PAIRS, P], F32, own)
        BQ = c.sb(f"{tag}_BQ", [P, PAIRS], F32, own)
        BK = c.sb(f"{tag}_BK", [P, PAIRS], F32, own)
        BV = c.sb(f"{tag}_BV", [KC, H * HD64], F32, own)
        BO = c.sb(f"{tag}_BO", [P, 1], F32, own)
        KB = c.sb(f"{tag}_KB", [P, PAIRS, B, 2, KC], F32, own)
        VA = c.sb(f"{tag}_VA", [SROWS, B, H * HD64], F32, own)
        VB = c.sb(f"{tag}_VB", [SROWS, H * HD64], F32, own)
        Q = c.sb(f"{tag}_Q", [P, 2, S], F32, own)
        SC = c.sb(f"{tag}_SC", [P, 2, 2 * QT, KC], F32, own)
        PR = c.sb(f"{tag}_PR", [P, 2, 2 * QT, KC], F32, own)
        PT = c.sb(f"{tag}_PT", [SROWS, 2, S], F32, own)
        CT = c.sb(f"{tag}_CT", [P, S], F32, own)
        M = c.sb(f"{tag}_M", [P, 2 * QT], F32, own)
        DEN = c.sb(f"{tag}_DEN", [P, 2 * QT], F32, own)
        RDEN = c.sb(f"{tag}_RDEN", [P, 2 * QT], F32, own)
        (s_w, s_zero, s_scaled, s_kproj, s_kout, s_vproj, s_vout, s_vb, proj, q_out, scores, maxed, lessened, exped, summed,
         inverted, normed, turned, t_act, t_dve, products, heads_out, added, s_ot) = (
            c.sem(f"{tag}_{n}") for n in
            ("w", "zero", "scaled", "kproj", "kout", "vproj", "vout", "vb", "proj", "q_out", "scores", "maxed", "lessened",
             "exped", "summed", "inverted", "normed", "turned", "t_act", "t_dve", "products", "heads_out", "added", "ot"))
        N_W = 16 * 8

        with nc.Block() as block:
            @block.sync
            def _(sp):
                for dst, src in ((WQ, wq), (WK, wk), (WV, wv)):
                    sp.dma_start(dst[:, :], src.rearrange("m h d -> m (h d)")).then_inc(s_w, 16)
                sp.dma_start(WO[:, :, :], wo.rearrange("(g e) d n -> (e d) g n", e=2)).then_inc(s_w, 16)
                sp.dma_start(BQ[:, :], bq.rearrange("(g e) d -> (e d) g", e=2),
                             allow_slow_non_contiguous=True).then_inc(s_w, 16)
                sp.dma_start(BK[:, :], bk.rearrange("(g e) d -> (e d) g", e=2),
                             allow_slow_non_contiguous=True).then_inc(s_w, 16)
                sp.dma_start(BV[:, :], row(bv.rearrange("h d -> (h d)"), KC)).then_inc(s_w, 16)
                sp.dma_start(BO[:, :], col(bo)).then_inc(s_w, 16)

            @block.gpsimd
            def _(pool):
                nc.gpsimd.memset(KB[:, :, :, :, :], 0.0).then_inc(s_zero, 1)
                pool.wait_ge(s_zero, 1)
                nc.gpsimd.memset(VA[64:SROWS, :, :], 0.0).then_inc(s_zero, 1)
                pool.wait_ge(s_zero, 2)
                nc.gpsimd.memset(PT[64:SROWS, :, :], 0.0)

            @block.tensor
            def _(pe):
                pe.wait_ge(s_w, N_W)
                for p in range(PAIRS):
                    if p >= 2:
                        pe.wait_ge(s_kout, 2 * (p - 1))
                    nc.tensor.matmul(c.ps_s[:, p % 2, 0:B * KC], WK[:, p * P:(p + 1) * P], c.CTT[:, :],
                                     start=True, stop=True).then_inc(s_kproj, 1)
                    b, half = p // 2, p % 2
                    if p >= 2:
                        pe.wait_ge(s_vout, p - 1)
                    nc.tensor.matmul(c.ps_t[0:KC, half, :], c.CTT[:, b * KC:(b + 1) * KC], WV[:, half * 512:(half + 1) * 512],
                                     start=True, stop=True).then_inc(s_vproj, 1)

            @block.vector
            def _(dve):
                dve.wait_ge(s_w, N_W)
                nc.vector.tensor_scalar(BQ[:, :], BQ[:, :], ISQ64, None, ALU.mult).then_inc(s_scaled, 1)
                dve.wait_ge(s_zero, 2)
                for p in range(PAIRS):
                    dve.wait_ge(s_kproj, p + 1)
                    for e in range(2):
                        r = slice(e * HD64, (e + 1) * HD64)
                        nc.vector.tensor_scalar(KB[r, p, :, e, :], c.ps_s[r, p % 2, 0:B * KC].rearrange("p (b k) -> p b k", b=B),
                                                BK[r, p:p + 1], None, ALU.add).then_inc(s_kout, 1)
                    b, half = p // 2, p % 2
                    dve.wait_ge(s_vproj, p + 1)
                    v = slice(half * 512, (half + 1) * 512)
                    nc.vector.tensor_tensor(VA[0:KC, b, v], c.ps_t[0:KC, half, :], BV[:, v], ALU.add).then_inc(s_vout, 1)

        with nc.Block() as block:
            @block.tensor
            def _(pe):
                def project(b, p):
                    wait(pe, q_out, b * PAIRS + p)
                    nc.tensor.matmul(c.ps_s[:, 2, :], WQ[:, p * P:(p + 1) * P], c.XT[:, bass.ds(b * S, S)],
                                     start=True, stop=True).then_inc(proj, 1)

                def score(b, p):
                    wait(pe, q_out, b * PAIRS + p + 1)
                    wait(pe, lessened, b * PAIRS + p)
                    for qt in range(QT):
                        mm = nc.tensor.matmul(c.ps_s[:, qt // 2, (qt % 2) * 2 * KC:(qt % 2 + 1) * 2 * KC],
                                              Q[:, p % 2, qt * P:(qt + 1) * P],
                                              KB[:, p, bass.ds(b, 1), :, :].rearrange("p a e k -> p (a e k)"),
                                              start=True, stop=True)
                    mm.then_inc(scores, 1)

                def turn(b, p):
                    wait(pe, normed, b * PAIRS + p + 1)
                    wait(pe, t_act, b * PAIRS + p)
                    wait(pe, t_dve, b * PAIRS + p)
                    for e in range(2):
                        for qt in range(QT):
                            mm = nc.tensor.transpose(c.ps_t[0:KC, e, qt * P:(qt + 1) * P], PR[:, p % 2, 2 * qt + e, :],
                                                     c.ident[:, :])
                        mm.then_inc(turned, 1)

                def weigh(b, p):
                    wait(pe, t_act, b * PAIRS + p + 1)
                    wait(pe, t_dve, b * PAIRS + p + 1)
                    wait(pe, heads_out, b * PAIRS + p)
                    for e in range(2):
                        h = 2 * p + e
                        mm = nc.tensor.matmul(c.ps_v[e * HD64:(e + 1) * HD64, :], VB[:, h * HD64:(h + 1) * HD64], PT[:, e, :],
                                              start=True, stop=True)
                    mm.then_inc(products, 1)

                def add(b, p):
                    wait(pe, heads_out, b * PAIRS + p + 1)
                    if p == 0:
                        wait(pe, s_ot, b)
                    nc.tensor.matmul(c.ps_f[:, :], WO[:, p, :], CT[:, :], start=(p == 0), stop=(p == PAIRS - 1)).then_inc(added, 1)

                def batch(b):
                    project(b, 0)
                    project(b, 1)
                    score(b, 0)
                    wait(pe, s_vb, b + 1)
                    for p in range(PAIRS):
                        if p + 1 < PAIRS:
                            score(b, p + 1)
                        turn(b, p)
                        if p + 2 < PAIRS:
                            project(b, p + 2)
                        if p:
                            add(b, p - 1)
                        weigh(b, p)
                    add(b, PAIRS - 1)
                first_then_loop(pe, B, batch)

            @block.vector
            def _(dve):
                def lessen(b, p):
                    n = b * PAIRS + p
                    src = c.ps_s[:, 0:2, 0:4 * KC].rearrange("p a (m k) -> p a m k", k=KC)
                    dve.wait_ge(scores, n + 1)
                    nc.vector.reduce_max(M[:, :].rearrange("p (a m) -> p a m", a=2), src, AX.X).then_inc(maxed, 1)
                    dve.wait_ge(maxed, n + 1)
                    if p < 2:
                        wait(dve, exped, b * PAIRS)
                    else:
                        dve.wait_ge(exped, n - 1)
                    nc.vector.tensor_tensor(SC[:, p % 2].rearrange("p (a m) k -> p a m k", a=2), src,
                                            M[:, :].rearrange("p (a m b) -> p a m b", a=2, b=1).broadcast_to([P, 2, 4, KC]),
                                            ALU.subtract).then_inc(lessened, 1)

                def norm(b, p):
                    n = b * PAIRS + p
                    dve.wait_ge(exped, n + 1)
                    nc.vector.reduce_sum(DEN[:, :], PR[:, p % 2], AX.X).then_inc(summed, 1)
                    dve.wait_ge(summed, n + 1)
                    nc.vector.reciprocal(RDEN[:, :], DEN[:, :]).then_inc(inverted, 1)
                    dve.wait_ge(inverted, n + 1)
                    nc.vector.tensor_tensor(PR[:, p % 2], PR[:, p % 2],
                                            RDEN[:, :].rearrange("p (m a) -> p m a", a=1).broadcast_to([P, 2 * QT, KC]),
                                            ALU.mult).then_inc(normed, 1)

                def take(b, p):
                    n = b * PAIRS + p
                    dve.wait_ge(turned, 2 * n + 2)
                    dve.wait_ge(products, n)
                    nc.vector.tensor_copy(PT[0:KC, 1, :], c.ps_t[0:KC, 1, :]).then_inc(t_dve, 1)

                def take_heads(b, p):
                    n = b * PAIRS + p
                    dve.wait_ge(products, n + 1)
                    dve.wait_ge(added, n)
                    nc.vector.tensor_copy(CT[:, :], c.ps_v[:, :]).then_inc(heads_out, 1)

                def batch(b):
                    wait(dve, products, b * PAIRS)
                    nc.vector.tensor_copy(VB[:, :], VA[:, bass.ds(b, 1), :].rearrange("p a n -> p (a n)")).then_inc(s_vb, 1)
                    lessen(b, 0)
                    norm(b, 0)
                    for p in range(PAIRS):
                        if p + 1 < PAIRS:
                            lessen(b, p + 1)
                        take(b, p)
                        if p + 1 < PAIRS:
                            norm(b, p + 1)
                        take_heads(b, p)
                first_then_loop(dve, B, batch)

            @block.scalar
            def _(act):
                def exp(b, p):
                    n = b * PAIRS + p
                    act.wait_ge(lessened, n + 1)
                    if p < 2:
                        wait(act, turned, 2 * b * PAIRS)
                    else:
                        act.wait_ge(turned, 2 * (n - 1))
                    nc.scalar.activation(PR[:, p % 2], SC[:, p % 2], ACT.Exp).then_inc(exped, 1)

                def queries_out(b, p):
                    n = b * PAIRS + p
                    act.wait_ge(proj, n + 1)
                    if p < 2:
                        wait(act, scores, b * PAIRS)
                    else:
                        act.wait_ge(scores, n - 1)
                    nc.scalar.activation(Q[:, p % 2, :], c.ps_s[:, 2, :], ACT.Identity, bias=BQ[:, p:p + 1],
                                         scale=ISQ64).then_inc(q_out, 1)

                def batch(b):
                    queries_out(b, 0)
                    queries_out(b, 1)
                    exp(b, 0)
                    for p in range(PAIRS):
                        if p + 1 < PAIRS:
                            exp(b, p + 1)
                        act.wait_ge(turned, 2 * (b * PAIRS + p) + 1)
                        wait(act, products, b * PAIRS + p)
                        nc.scalar.activation(PT[0:KC, 0, :], c.ps_t[0:KC, 0, :], ACT.Copy).then_inc(t_act, 1)
                        if p + 2 < PAIRS:
                            queries_out(b, p + 2)
                    wait(act, added, b * PAIRS + PAIRS)
                    nc.scalar.activation(OT[:, bass.ds(b, 1), :], c.ps_f[:, :], ACT.Identity, bias=BO[:, 0:1]).then_inc(s_ot, 1)
                first_then_loop(act, B, batch)


def gates(c, tag, wg, GATE):
    nc = c.nc
    with ExitStack() as own:
        WG = c.sb(f"{tag}_WG", [P, NE], F32, own)
        L = c.sb(f"{tag}_L", [P, NT, NE], F32, own)
        E = c.sb(f"{tag}_E", [P, NT, NE], F32, own)
        C1 = c.sb(f"{tag}_C1", [P, NT, NE, NE], F32, own)
        C2 = c.sb(f"{tag}_C2", [P, NT, NE, NE], F32, own)
        LOW = c.sb(f"{tag}_LOW", [P, NE, NE], F32, own)
        RK = c.sb(f"{tag}_RK", [P, NT, NE], F32, own)
        M = c.sb(f"{tag}_GM", [P, NT], F32, own)
        s_w, s_low, s_logits, s_chain, s_exp = (c.sem(f"{tag}_g{n}") for n in ("w", "low", "logits", "chain", "exp"))
        with nc.Block() as block:
            @block.sync
            def _(sp):
                sp.dma_start(WG[:, :], wg).then_inc(s_w, 16)

            @block.gpsimd
            def _(pool):
                nc.gpsimd.memset(LOW[:, :, :], 1.0).then_inc(s_low, 1)
                pool.wait_ge(s_low, 1)
                nc.gpsimd.affine_select(out=LOW[:, :, :], in_=LOW[:, :, :], compare_op=ALU.is_gt, fill=0.0, base=0,
                                        pattern=[[1, NE], [-1, NE]], channel_multiplier=0).then_inc(s_low, 1)

            @block.tensor
            def _(pe):
                pe.wait_ge(s_w, 16)
                for n in range(NT):
                    last = nc.tensor.matmul(c.ps_s[:, 0, n * NE:(n + 1) * NE], c.XT[:, n * P:(n + 1) * P], WG[:, :],
                                            start=True, stop=True)
                last.then_inc(s_logits, 1)

            @block.scalar
            def _(act):
                act.wait_ge(s_chain, 3)
                nc.scalar.activation(E[:, :, :], E[:, :, :], ACT.Exp).then_inc(s_exp, 1)

            @block.vector
            def _(dve):
                chain = Chain(s_chain)
                if GATE.shape[2] > NE:
                    nc.vector.memset(GATE[:, :, NE:], 1.0)
                dve.wait_ge(s_logits, 1)
                chain.inc(nc.vector.tensor_copy(L[:, :, :], c.ps_s[:, 0, 0:NT * NE].rearrange("p (n e) -> p n e", e=NE)))
                chain.wait(dve)
                chain.inc(nc.vector.reduce_max(M[:, :], L[:, :, :], AX.X))
                chain.wait(dve)
                by_tile = M[:, :].rearrange("p (n a) -> p n a", a=1).broadcast_to([P, NT, NE])
                chain.inc(nc.vector.tensor_tensor(E[:, :, :], L[:, :, :], by_tile, ALU.subtract))
                of_e = L[:, :, :].rearrange("p n (e a) -> p n e a", a=1).broadcast_to([P, NT, NE, NE])
                of_j = L[:, :, :].rearrange("p n (a j) -> p n a j", a=1).broadcast_to([P, NT, NE, NE])
                chain.inc(nc.vector.tensor_tensor(C1[:, :, :, :], of_j, of_e, ALU.is_gt))
                chain.inc(nc.vector.tensor_tensor(C2[:, :, :, :], of_j, of_e, ALU.is_equal))
                chain.wait(dve)
                dve.wait_ge(s_low, 2)
                c2 = C2[:, :, :, :].rearrange("p n e j -> p n (e j)")
                chain.inc(nc.vector.tensor_tensor(
                    c2, c2, LOW[:, :, :].rearrange("p (a e) j -> p a (e j)", a=1).broadcast_to([P, NT, NE * NE]), ALU.mult))
                chain.wait(dve)
                chain.inc(nc.vector.tensor_tensor(C1[:, :, :, :], C1[:, :, :, :], C2[:, :, :, :], ALU.add))
                chain.wait(dve)
                chain.inc(nc.vector.reduce_sum(RK[:, :, :], C1[:, :, :, :], AX.X))
                chain.wait(dve)
                dve.wait_ge(s_exp, 1)
                gate = GATE[:, :, 0:NE]
                chain.inc(nc.vector.scalar_tensor_tensor(gate, RK[:, :, :], 2.0, E[:, :, :], ALU.is_lt, ALU.mult))
                chain.wait(dve)
                chain.inc(nc.vector.reduce_sum(M[:, :], gate, AX.X))
                chain.wait(dve)
                chain.inc(nc.vector.reciprocal(M[:, :], M[:, :]))
                chain.wait(dve)
                nc.vector.tensor_tensor(gate, gate, by_tile, ALU.mult)


def experts(c, tag, GATE, w1, w2, w3=None, b1=None, b2=None, shared=None):
    nc = c.nc
    hid = w1.shape[2]
    CH = hid // P
    gated = w3 is not None
    total = NE + (shared is not None)
    with ExitStack() as own:
        W1 = [c.sb(f"{tag}_W1{i}", [P, hid], F32, own) for i in range(2)]
        W3 = [c.sb(f"{tag}_W3{i}", [P, hid], F32, own) for i in range(2)] if gated else None
        W2 = [c.sb(f"{tag}_W2{i}", [P, CH, P], F32, own) for i in range(2)]
        HT = c.sb(f"{tag}_HT", [P, 2, CH, S], F32, own)
        GT = c.sb(f"{tag}_GT", [P, 2, CH, S], F32, own) if gated else None
        B1 = c.sb(f"{tag}_B1", [P, NE, CH], F32, own) if not gated else None
        BE = c.sb(f"{tag}_BE", [P, 2, CH], F32, own) if not gated else None
        B2 = c.sb(f"{tag}_B2", [P, NE, P], F32, own) if not gated else None
        s_w = [c.sem(f"{tag}_w{i}") for i in range(2)]
        s_b, s_be, s_first, s_act, s_hidden, s_second, s_added = (
            c.sem(f"{tag}_{n}") for n in ("bias", "be", "first", "act", "hidden", "second", "added"))
        N_W = 16 * (3 if gated else 2)
        ADDS = QT if gated else 2 * QT
        sources = (w1, w2) + ((w3,) if gated else ())

        def load(sp, e, i, shared_too=False):
            if shared_too:
                srcs = ((W1[i][:, :], shared[0]), (W3[i][:, :], shared[1]),
                        (W2[i][:, :, :], shared[2].rearrange("(c p) n -> p c n", p=P)))
            else:
                srcs = ((W1[i][:, :], w1[e]), (W2[i][:, :, :], w2[e].rearrange("(c p) n -> p c n", p=P)))
                if gated:
                    srcs += ((W3[i][:, :], w3[e]),)
            for dst, src in srcs:
                sp.dma_start(dst, src).then_inc(s_w[i], 16)

        def run(engine, one):
            def pair(t, first, last):
                for i in range(2):
                    one(t, i, first and i == 0, last and i == 1 and total % 2 == 0)
            if total % 2:
                pair(0, True, False)
                with engine.Fori(1, total // 2) as t:
                    pair(t, False, False)
                one(total // 2, 0, False, True)
            else:
                peeled(engine, total // 2, pair)

        with nc.Block() as block:
            @block.sync
            def _(sp):
                if not gated:
                    sp.dma_start(B1[:, :, :], b1.rearrange("e (c p) -> p e c", p=P), allow_slow_non_contiguous=True).then_inc(s_b, 16)
                    sp.dma_start(B2[:, :, :].rearrange("p e n -> p (e n)"), row(b2.rearrange("e n -> (e n)"))).then_inc(s_b, 16)
                load(sp, 0, 0)
                load(sp, 1, 1)
                for e in range(2, NE):
                    sp.wait_ge(s_second, (e - 1) * B)
                    sp.wait_ge(s_w[e % 2], e // 2 * N_W)
                    load(sp, e, e % 2)
                if shared is not None:
                    sp.wait_ge(s_second, (NE - 1) * B)
                    sp.wait_ge(s_w[0], NE // 2 * N_W)
                    load(sp, None, 0, True)

            @block.tensor
            def _(pe):
                def first_products(t, i, b, first):
                    k = (2 * t + i) * B + b
                    if b == 0:
                        pe.wait_ge(s_w[i], (t + 1) * N_W)
                    for ch in range(2 * CH if gated else CH):
                        if not first:
                            if gated and ch >= CH:
                                pe.wait_ge(s_hidden, (k - 1) * CH + ch - CH + 1)
                            else:
                                pe.wait_ge(s_act, (k - 1) * CH + ch + 1)
                        W = W3[i] if gated and ch >= CH else W1[i]
                        nc.tensor.matmul(c.ps_s[:, ch, :], W[:, (ch % CH) * P:(ch % CH + 1) * P], c.XT[:, b * S:(b + 1) * S],
                                         start=True, stop=True).then_inc(s_first, 1)

                def second_products(t, i, b, first):
                    k = (2 * t + i) * B + b
                    pe.wait_ge(s_hidden if gated else s_act, (k + 1) * CH)
                    if not (first and b < 2):
                        pe.wait_ge(s_added, (k - 1) * ADDS)
                    for q in range(QT):
                        for ch in range(CH):
                            mm = nc.tensor.matmul(c.ps_t[:, b % 2, q * P:(q + 1) * P], HT[:, b % 2, ch, q * P:(q + 1) * P],
                                                  W2[i][:, ch, :], start=(ch == 0), stop=(ch == CH - 1))
                    mm.then_inc(s_second, 1)

                def one(t, i, first, last):
                    for b in range(B):
                        if b + 1 < B:
                            first_products(t, i, b + 1, False)
                        elif not last:
                            first_products(t + i, 1 - i, 0, False)
                        second_products(t, i, b, first)
                first_products(0, 0, 0, True)
                run(pe, one)

            @block.scalar
            def _(act):
                if not gated:
                    act.wait_ge(s_b, 32)

                def one(t, i, first, last):
                    if not gated:
                        nc.scalar.activation(BE[:, i, :], B1[:, bass.ds(2 * t + i, 1), :].rearrange("p a c -> p (a c)"),
                                             ACT.Copy).then_inc(s_be, 1)
                        act.wait_ge(s_be, 2 * t + i + 1)
                    for b in range(B):
                        k = (2 * t + i) * B + b
                        for ch in range(CH):
                            act.wait_ge(s_first, k * (2 * CH if gated else CH) + ch + 1)
                            if not (first and b < 2):
                                if gated:
                                    act.wait_ge(s_hidden, (k - 2) * CH + ch + 1)
                                else:
                                    act.wait_ge(s_second, k - 1)
                            if gated:
                                nc.scalar.activation(GT[:, b % 2, ch, :], c.ps_s[:, ch, :], ACT.Silu).then_inc(s_act, 1)
                            else:
                                nc.scalar.activation(HT[:, b % 2, ch, :], c.ps_s[:, ch, :], ACT.Gelu_apprx_tanh,
                                                     bias=BE[:, i, ch:ch + 1]).then_inc(s_act, 1)
                run(act, one)

            @block.vector
            def _(dve):
                if not gated:
                    dve.wait_ge(s_b, 32)

                def hidden(t, i, b, first):
                    k = (2 * t + i) * B + b
                    for ch in range(CH):
                        dve.wait_ge(s_first, k * 2 * CH + CH + ch + 1)
                        dve.wait_ge(s_act, k * CH + ch + 1)
                        if not (first and b < 2):
                            dve.wait_ge(s_second, k - 1)
                        nc.vector.tensor_tensor(HT[:, b % 2, ch, :], GT[:, b % 2, ch, :], c.ps_s[:, CH + ch, :],
                                                ALU.mult).then_inc(s_hidden, 1)

                def add(t, i, b, first):
                    k = (2 * t + i) * B + b
                    e = 2 * t + i
                    if not gated:
                        if not (first and b == 0):
                            dve.wait_ge(s_added, k * ADDS)
                        for q in range(QT):
                            x = c.X[:, b * QT + q, :]
                            gate = GATE[:, b * QT + q, bass.ds(e, 1)]
                            nc.vector.scalar_tensor_tensor(x, B2[:, bass.ds(e, 1), :].rearrange("p a n -> p (a n)"), gate, x,
                                                           ALU.mult, ALU.add).then_inc(s_added, 1)
                        dve.wait_ge(s_added, k * ADDS + QT)
                    elif not (first and b == 0):
                        dve.wait_ge(s_added, k * ADDS)
                    dve.wait_ge(s_second, k + 1)
                    for q in range(QT):
                        x = c.X[:, b * QT + q, :]
                        gate = GATE[:, b * QT + q, bass.ds(e, 1)]
                        nc.vector.scalar_tensor_tensor(x, c.ps_t[:, b % 2, q * P:(q + 1) * P], gate, x,
                                                       ALU.mult, ALU.add).then_inc(s_added, 1)

                def one(t, i, first, last):
                    for b in range(B):
                        if gated:
                            if b + 1 < B:
                                hidden(t, i, b + 1, first)
                            elif not last:
                                hidden(t + i, 1 - i, 0, False)
                        add(t, i, b, first)
                if gated:
                    hidden(0, 0, 0, True)
                run(dve, one)


def decoder(nc, a, out):
    scratch = nc.dram_tensor("split_parts", (B, 2, P, NPART, S), BF16, kind="Internal").ap()
    with ExitStack() as ctx:
        c = Core(nc, ctx)
        setup(c, a["x"], a["ctx_1024"])

        narrow_self_attention(c, "a", a["L0_attn_Wq"], a["L0_attn_Wk"], a["L0_attn_Wv"], scratch, rel=a["L0_attn_rel_emb"])
        finish(c, "a", "ctx", wo=a["L0_attn_Wo"], bias=a["L0_attn_bo"])
        narrow_cross_attention(c, "b", a["L0_xattn_Wq"], a["L0_xattn_bq"], a["L0_xattn_Wk"], a["L0_xattn_bk"],
                               a["L0_xattn_Wv"], a["L0_xattn_bv"], scratch)
        finish(c, "b", "ctx", wo=a["L0_xattn_Wo"], bias=a["L0_xattn_bo"], pre=(a["L0_ffn_ln1_w"], a["L0_ffn_ln1_b"]))
        q, k, v = (slice(i * P, (i + 1) * P) for i in range(3))
        w, b = a["L0_ffn_w_qkv"], a["L0_ffn_b_qkv"]
        narrow_self_attention(c, "c", w[:, q], w[:, k], w[:, v], scratch, b[q], b[k], b[v], qscale=ISQ8)
        finish(c, "c", "ctx", wo=a["L0_ffn_w_o"], bias=a["L0_ffn_b_o"], mode="inner",
               pre=(a["L0_ffn_ln2_w"], a["L0_ffn_ln2_b"]))
        with ExitStack() as own:
            GATE = c.sb("GATE0", [P, NT, NE], F32, own)
            gates(c, "f", a["L0_ffn_w_gate"], GATE)
            experts(c, "f", GATE, a["L0_ffn_w1"], a["L0_ffn_w2"], b1=a["L0_ffn_b1"], b2=a["L0_ffn_b2"])
        finish(c, "f", "x", pre=(a["L1_attn_ln_gamma"], a["L1_attn_ln_beta"]))
        c.recycle_semaphores()
        with ExitStack() as own:
            OT = c.sb("OT_d", [P, B, S], F32, own)
            wide_self_attention(c, "d", a["L1_attn_Wq"], a["L1_attn_Wk"], a["L1_attn_Wv"], a["L1_attn_Wo"], OT)
            finish(c, "d", "dm", OT=OT)
        with ExitStack() as own:
            OT = c.sb("OT_e", [P, B, S], F32, own)
            wide_cross_attention(c, "e", *(a[f"L1_xattn_{n}"] for n in ("Wq", "bq", "Wk", "bk", "Wv", "bv", "Wo", "bo")), OT)
            finish(c, "e", "dm", OT=OT)
        with ExitStack() as own:
            GATE = c.sb("GATE1", [P, NT, NE + 1], F32, own)
            gates(c, "g", a["L1_ffn_w_router"], GATE)
            experts(c, "g", GATE, a["L1_ffn_w1"], a["L1_ffn_w2"], w3=a["L1_ffn_w3"],
                    shared=(a["L1_ffn_sw1"], a["L1_ffn_sw3"], a["L1_ffn_sw2"]))
        finish(c, "g", "x", out=out)


_NAMES = ["x", "ctx_1024"] \
    + [f"L0_attn_{n}" for n in ("Wq", "Wk", "Wv", "Wo", "bo", "rel_emb")] \
    + [f"L0_xattn_{n}" for n in ("Wq", "bq", "Wk", "bk", "Wv", "bv", "Wo", "bo")] \
    + [f"L0_ffn_{n}" for n in ("ln1_w", "ln1_b", "ln2_w", "ln2_b", "w_qkv", "b_qkv", "w_o", "b_o", "w_gate",
                               "w1", "b1", "w2", "b2")] \
    + [f"L1_attn_{n}" for n in ("ln_gamma", "ln_beta", "Wq", "Wk", "Wv", "Wo")] \
    + [f"L1_xattn_{n}" for n in ("Wq", "bq", "Wk", "bk", "Wv", "bv", "Wo", "bo")] \
    + [f"L1_ffn_{n}" for n in ("w_router", "w1", "w3", "w2", "sw1", "sw3", "sw2")]


def kernel(**inputs):
    import numpy as np
    import concourse.bacc as bacc
    from concourse.bass_utils import run_bass_kernel_spmd

    nc = bacc.Bacc("TRN2", target_bir_lowering=False, num_devices=1)
    arrays, aps = {}, {}
    for name in _NAMES:
        array = np.ascontiguousarray(inputs[name])
        arrays[f"in_{name}"] = array
        aps[name] = nc.dram_tensor(f"in_{name}", array.shape, mybir.dt.from_np(array.dtype), kind="ExternalInput").ap()
    out = nc.dram_tensor("out", (B, S, P), F32, kind="ExternalOutput").ap()
    decoder(nc, aps, out)
    result = run_bass_kernel_spmd(nc, [arrays], core_ids=[0])
    return result.results[0]["out"]
```

```python
import concourse.bass as bass
from concourse import mybir
from contextlib import ExitStack

F32 = mybir.dt.float32
BF16 = mybir.dt.bfloat16
ALU = mybir.AluOpType
ACT = mybir.ActivationFunctionType
AX = mybir.AxisListType

P = 128
B = 4
S = 512
QT = S // P
NT = B * QT
TOK = B * S
KC = 77
H = 16
HD8 = P // H
HD64 = 64
PAIRS = H // 2
GH = 4
GROUPS = H // GH
STEPS = B * GROUPS
CW = P // GH
NPART = 3
SROWS = 96
NE = 8
HID0 = 512
HID1 = 256
CLIP = 16
EPS = 1e-5
MASKED = -1e30
LOWEST = -3e38
ISQ8 = float(HD8) ** -0.5
ISQ64 = float(HD64) ** -0.5


class Chain:

    def __init__(self, sem, base=0):
        self.sem, self.base, self.n = sem, base, 0

    def inc(self, instruction):
        instruction.then_inc(self.sem, 1)
        self.n += 1

    def value(self):
        return self.base + self.n

    def wait(self, engine):
        engine.wait_ge(self.sem, self.base + self.n)


def peeled(engine, count, body):
    body(0, True, False)
    with engine.Fori(1, count - 1) as t:
        body(t, False, False)
    body(count - 1, False, True)


def first_then_loop(engine, count, body):
    body(0)
    with engine.Fori(1, count) as t:
        body(t)


def wait(engine, sem, value):
    if not isinstance(value, int) or value > 0:
        engine.wait_ge(sem, value)


class Core:

    def __init__(self, nc, ctx):
        self.nc, self.ctx, self.sems = nc, ctx, []
        self.X = self.sb("X", [P, NT, P], F32)
        self.XT = self.sb("XT", [P, TOK], F32)
        self.CTX = self.sb("CTX", [P, NT, P], F32)
        self.CTT = self.sb("CTT", [P, B * KC], F32)
        self.ident = self.sb("ident", [P, P], F32)
        self.VG = self.sb("VG", [P, QT, GH, CW], F32)
        self.neghalf = self.sb("neghalf", [P, 4], F32)
        self.ps_s = ctx.enter_context(nc.psum_tensor("ps_s", [P, 4, 512], F32))
        self.ps_t = ctx.enter_context(nc.psum_tensor("ps_t", [P, 2, 512], F32))
        self.ps_v = ctx.enter_context(nc.psum_tensor("ps_v", [P, 512], F32))
        self.ps_f = ctx.enter_context(nc.psum_tensor("ps_f", [P, 512], F32))

    def sb(self, name, shape, dt, ctx=None):
        return (ctx or self.ctx).enter_context(self.nc.sbuf_tensor(name, shape, dt))

    def sem(self, name):
        self.sems.append(self.nc.alloc_semaphore(name=name))
        return self.sems[-1]

    def recycle_semaphores(self):
        self.nc.clear_and_free_semaphores(self.sems)
        self.nc.all_engine_barrier()
        self.sems = []


def row(ap, parts=P):
    n = ap.shape[0]
    return ap.rearrange("(a n) -> a n", a=1).broadcast_to([parts, n])


def col(ap):
    return ap.rearrange("(p a) -> p a", a=1)


def setup(c, x, ctx_in):
    nc = c.nc
    with ExitStack() as own:
        CR = c.sb("CR", [KC, B, P], F32, own)
        loaded, made, turned, copied = (c.sem(f"setup_{n}") for n in ("loaded", "made", "turned", "copied"))
        with nc.Block() as block:
            @block.sync
            def _(sp):
                for b in range(B):
                    sp.dma_start(c.X[:, b * QT:(b + 1) * QT, :],
                                 x[b].rearrange("(n p) d -> p n d", p=P)).then_inc(loaded, 16)
                sp.dma_start(CR[:, :, :], ctx_in.rearrange("b k d -> k b d")).then_inc(loaded, 16)

            @block.gpsimd
            def _(pool):
                nc.gpsimd.memset(c.ident[:, :], 0.0).then_inc(made, 1)
                pool.wait_ge(made, 1)
                nc.gpsimd.affine_select(out=c.ident[:, :], in_=c.ident[:, :], compare_op=ALU.not_equal, fill=1.0,
                                        base=0, pattern=[[-1, P]], channel_multiplier=1).then_inc(made, 1)
                nc.gpsimd.memset(c.VG[:, :, :, :], 1.0)
                nc.gpsimd.memset(c.neghalf[:, :], -0.5).then_inc(made, 1)

            @block.tensor
            def _(pe):
                pe.wait_ge(made, 2)
                pe.wait_ge(loaded, 16 * (B + 1))
                for b in range(B):
                    for i in range(QT):
                        last = nc.tensor.transpose(c.ps_s[:, b, i * P:(i + 1) * P], c.X[:, b * QT + i, :], c.ident[:, :])
                    last.then_inc(turned, 1)
                for b in range(B):
                    last = nc.tensor.transpose(c.ps_t[:, 0, b * KC:(b + 1) * KC], CR[:, b, :], c.ident[0:KC, 0:KC])
                last.then_inc(turned, 1)

            @block.vector
            def _(dve):
                for b in range(B):
                    dve.wait_ge(turned, b + 1)
                    nc.vector.tensor_copy(c.XT[:, b * S:(b + 1) * S], c.ps_s[:, b, :])
                dve.wait_ge(turned, B + 1)
                nc.vector.tensor_copy(c.CTT[:, :], c.ps_t[:, 0, 0:B * KC])


SPLIT_OPS = 5


def split_parts(nc, dve, chain, full, part):
    chain.inc(nc.vector.tensor_copy(part(0), full))
    chain.wait(dve)
    for i in (1, 2):
        chain.inc(nc.vector.tensor_tensor(full, full, part(i - 1), ALU.subtract))
        chain.wait(dve)
        chain.inc(nc.vector.tensor_copy(part(i), full))
        chain.wait(dve)


def stacks(c, ctx):
    c.QX = c.sb("QX", [P, 2 * H, S], BF16, ctx)
    c.KX = c.sb("KX", [P, 2 * H, S], BF16, ctx)


def constant_rows(c, engine, ops):
    ops.memset(c.KX[64:SROWS, :, :], 0.0)
    ops.memset(c.KX[SROWS:P, :, :], 1.0)
    ops.memset(c.QX[64:P, :, :], 0.0)


def narrow_projections(c, tag, own, scratch, QX, KX, s_qx, wq, wk, wv, bq=None, bk=None, bv=None, qscale=1.0):
    nc = c.nc
    W = c.sb(f"{tag}_W", [P, 3, P], F32, own)
    BQK = c.sb(f"{tag}_BQK", [P, 2], F32, own)
    BV = c.sb(f"{tag}_BV", [P, P], F32, own)
    FULL = c.sb(f"{tag}_FULL", [P, 2, S], F32, own)
    PARTS = c.sb(f"{tag}_PARTS", [P, 2, NPART, S], BF16, own)
    kinds = [0] if wk is None else [0, 1]
    items = [(b, w) for b in range(B) for w in kinds]
    s_w, s_bias, s_proj, s_full, s_split, s_v, s_vn = (
        c.sem(f"{tag}_p{n}") for n in ("w", "bias", "proj", "full", "split", "v", "vn"))
    s_store = [c.sem(f"{tag}_store{i}") for i in range(2)]
    weights = [w for w in (wq, wk, wv) if w is not None]
    biases = [w for w in (bq, bk, bv) if w is not None]

    with nc.Block() as block:
        @block.sync
        def _(sp):
            for i, w in enumerate((wq, wk, wv)):
                if w is not None:
                    sp.dma_start(W[:, i, :], w).then_inc(s_w, 16)
            for i, v in enumerate((bq, bk)):
                if v is not None:
                    sp.dma_start(BQK[:, i:i + 1], col(v)).then_inc(s_w, 16)
            if bv is not None:
                sp.dma_start(BV[:, :], row(bv)).then_inc(s_w, 16)
            for i, (b, w) in enumerate(items):
                sp.wait_ge(s_split, SPLIT_OPS * (i + 1))
                sp.dma_start(scratch[b, w], PARTS[:, i % 2]).then_inc(s_store[i % 2], 16)
                if w == kinds[-1] and b in (1, 2):
                    for k in range(len(kinds) * (b - 1), len(kinds) * b):
                        sp.wait_ge(s_store[k % 2], 16 * (k // 2 + 1))
                    if b == 2:
                        sp.wait_ge(s_qx, STACK_LOADS * len(kinds) * 16)
                    load_stacks(nc, sp, scratch, b - 1, QX, KX, s_qx)
            for i in range(2):
                sp.wait_ge(s_store[i], 16 * (len(items) // 2))

        @block.tensor
        def _(pe):
            pe.wait_ge(s_w, 16 * (len(weights) + len(biases)))
            for i, (b, w) in enumerate(items):
                if i >= 2:
                    pe.wait_ge(s_full, i - 1)
                nc.tensor.matmul(c.ps_s[:, i % 2, :], W[:, w, :], c.XT[:, b * S:(b + 1) * S],
                                 start=True, stop=True).then_inc(s_proj, 1)
                if w == 0 and wv is not None:
                    if b >= 2:
                        pe.wait_ge(s_vn, b - 1)
                    for m in range(QT):
                        n = b * QT + m
                        last = nc.tensor.matmul(c.ps_t[:, b % 2, m * P:(m + 1) * P], c.XT[:, n * P:(n + 1) * P],
                                                W[:, 2, :], start=True, stop=True)
                    last.then_inc(s_v, 1)

        @block.scalar
        def _(act):
            if bq is not None:
                act.wait_ge(s_bias, 1)
            for i, (b, w) in enumerate(items):
                act.wait_ge(s_proj, i + 1)
                if i >= 2:
                    act.wait_ge(s_split, SPLIT_OPS * (i - 1))
                scale = qscale if w == 0 else 1.0
                if (bq, bk)[w] is None:
                    ins = nc.scalar.activation(FULL[:, i % 2, :], c.ps_s[:, i % 2, :], ACT.Copy, scale=scale)
                else:
                    ins = nc.scalar.activation(FULL[:, i % 2, :], c.ps_s[:, i % 2, :], ACT.Identity,
                                               bias=BQK[:, w:w + 1], scale=scale)
                ins.then_inc(s_full, 1)

        @block.vector
        def _(dve):
            chain = Chain(s_split)
            dve.wait_ge(s_w, 16 * (len(weights) + len(biases)))
            if bq is not None:
                nc.vector.tensor_scalar(BQK[:, 0:1], BQK[:, 0:1], qscale, None, ALU.mult).then_inc(s_bias, 1)
            for i, (b, w) in enumerate(items):
                dve.wait_ge(s_full, i + 1)
                if i >= 2:
                    dve.wait_ge(s_store[i % 2], 16 * (i // 2))
                part = lambda j: PARTS[:, i % 2, j, :]
                split_parts(nc, dve, chain, FULL[:, i % 2, :], part)
                if w == 0 and wv is not None:
                    dve.wait_ge(s_v, b + 1)
                    dst = c.VN[:, b * QT:(b + 1) * QT, :]
                    src = c.ps_t[:, b % 2, :].rearrange("p (m d) -> p m d", m=QT)
                    if bv is None:
                        nc.vector.tensor_copy(dst, src).then_inc(s_vn, 1)
                    else:
                        nc.vector.tensor_tensor(dst, src, BV[:, :].rearrange("p (a d) -> p a d", a=1).broadcast_to([P, QT, P]),
                                                ALU.add).then_inc(s_vn, 1)


STACK_LOADS = NPART * NPART


def load_stacks(nc, sp, scratch, b, QX, KX, sem):
    slot = slice((b % 2) * H, (b % 2 + 1) * H)
    for i in range(NPART):
        for j in range(NPART):
            r = HD8 * (NPART * i + j)
            for w, part, stack in ((0, i, QX), (1, j, KX)):
                if stack is not None:
                    sp.dma_start(stack[r:r + HD8, slot, :],
                                 scratch[b, w, :, part, :].rearrange("(h d) t -> d h t", d=HD8)).then_inc(sem, 16)


def gather_values(c, pool, t, first, s_pv, s_vg, cross_values=None, per_group=1):
    nc = c.nc
    if not first:
        pool.wait_ge(s_pv, per_group * t)
    if cross_values is None:
        for kt in range(QT):
            src = c.VN[:, bass.ds((t // GROUPS) * QT + kt, 1), bass.ds((t % GROUPS) * GH * HD8, GH * HD8)]
            last = nc.gpsimd.tensor_copy(c.VG[:, kt, :, 0:HD8], src.rearrange("p a (h d) -> p (a h) d", d=HD8))
    else:
        last = nc.gpsimd.tensor_copy(c.VG[0:SROWS, 0, 0:1, 0:HD8], cross_values[:, bass.ds(t // GROUPS, 1), :])
    last.then_inc(s_vg, 1)


def group_end_act(c, act, t, s_pv, s_ct, s_ftr, CT4, first=False, per_group=1):
    act.wait_ge(s_pv, per_group * (t + 1))
    if not first:
        act.wait_ge(s_ftr, t)
    c.nc.scalar.activation(CT4[:, :], c.ps_v[:, :], ACT.Copy).then_inc(s_ct, 1)


def group_end_pe(c, pe, t, s_ct, s_ctx, s_ftr, CT4, first=False):
    pe.wait_ge(s_ct, t + 1)
    if not first:
        pe.wait_ge(s_ctx, t)
    for i in range(QT):
        last = c.nc.tensor.transpose(c.ps_f[:, i * P:(i + 1) * P], CT4[:, i * P:(i + 1) * P], c.ident[:, :])
    last.then_inc(s_ftr, 1)


def group_end_dve(c, dve, t, s_ftr, s_rden, s_ctx, RDEN):
    nc = c.nc
    dve.wait_ge(s_ftr, t + 1)
    sums = c.ps_f[:, :].rearrange("p (q h w) -> p q h w", q=QT, h=GH)
    nc.vector.reciprocal(RDEN[:, :, :], sums[:, :, :, HD8]).then_inc(s_rden, 1)
    dve.wait_ge(s_rden, t + 1)
    out = c.CTX[:, bass.ds((t // GROUPS) * QT, QT), bass.ds((t % GROUPS) * GH * HD8, GH * HD8)]
    nc.vector.tensor_tensor(out.rearrange("p q (h d) -> p q h d", d=HD8), sums[:, :, :, 0:HD8],
                            RDEN[:, :, :].rearrange("p q (h a) -> p q h a", a=1).broadcast_to([P, QT, GH, HD8]),
                            ALU.mult).then_inc(s_ctx, 1)


def narrow_full_attention(c, tag, own, QX, KX, scratch, s_qx):
    nc = c.nc
    NM = c.sb(f"{tag}_NM", [P, QT, GH], F32, own)
    MP = c.sb(f"{tag}_MP", [P, QT, NPART, GH], BF16, own)
    MX = c.sb(f"{tag}_MX", [GH * NPART, S], BF16, own)
    IB = c.sb(f"{tag}_IB", [P, P], BF16, own)
    PT = c.sb(f"{tag}_PT", [P, 2, GH, 2, S], F32, own)
    CT4 = c.sb(f"{tag}_CT4", [P, S], F32, own)
    RDEN = c.sb(f"{tag}_RDEN", [P, QT, GH], F32, own)
    (scores, maxed, parted, mturned, s_mx, s_mload, s_ib, st, exped, products, s_vg, s_ct, s_ftr, s_rden, s_ctx) = (
        c.sem(f"{tag}_{n}") for n in ("scores", "maxed", "parted", "mturned", "mx", "mload", "ib", "st", "exped",
                                      "products", "vg", "ct", "ftr", "rden", "ctx"))
    NF = c.sb(f"{tag}_NF", [P, QT, GH], F32, own)
    PART_OPS = SPLIT_OPS + 1
    AHEAD = 2
    TILES = GH * QT

    def slot(u):
        return (u % (2 * GROUPS)) * GH

    def score(pe, u, i, first):
        n = u * TILES + i
        if i == 0:
            pe.wait_ge(s_qx, (u // GROUPS + 1) * 2 * STACK_LOADS * 16)
        if not (first and i < 2):
            pe.wait_ge(maxed, n - 1)
        qt = i % QT
        head = slot(u) + i // QT
        nc.tensor.matmul(c.ps_t[:, i % 2, :], QX[0:SROWS, bass.ds(head, 1), qt * P:(qt + 1) * P],
                         KX[0:SROWS, bass.ds(head, 1), :], start=True, stop=True).then_inc(scores, 1)

    def turn_maxima(pe, u, early=False):
        pe.wait_ge(parted, PART_OPS * (u + 1))
        if not early:
            pe.wait_ge(s_ctx, u - 2)
        for qt in range(QT):
            mm = nc.tensor.matmul(c.ps_f[0:GH * NPART, qt * P:(qt + 1) * P], MP[:, qt, :, :].rearrange("p i h -> p (i h)"),
                                  IB[:, :], start=True, stop=True)
        mm.then_inc(mturned, 1)

    def score_by_key(pe, t, half, j, first):
        m = (2 * t + half) * GH + j
        if half == 0 and j == 0:
            pe.wait_ge(s_mload, NPART * 16 * (t + 1))
        if not (first and half == 0 and j < 2):
            pe.wait_ge(exped, m - 1)
        head = slot(t) + j
        for k in range(2):
            kt = 2 * half + k
            mm = nc.tensor.matmul(c.ps_s[:, 2 * (j % 2) + k, :], KX[:, bass.ds(head, 1), kt * P:(kt + 1) * P],
                                  QX[:, bass.ds(head, 1), :], start=True, stop=True)
        mm.then_inc(st, 1)

    def value_products(pe, t, kt, first):
        half, k = divmod(kt, 2)
        if kt == 0:
            pe.wait_ge(s_vg, t + 1)
            if not first:
                pe.wait_ge(s_ct, t)
        if k == 0:
            pe.wait_ge(exped, (2 * t + half + 1) * GH)
        for j in range(GH):
            mm = nc.tensor.matmul(c.ps_v[j * CW:(j + 1) * CW, :], c.VG[:, kt, j, :], PT[:, half, j, k, :],
                                  start=(kt == 0), stop=(kt == QT - 1))
        if k == 1:
            mm.then_inc(products, 1)

    with nc.Block() as block:
        @block.sync
        def _(sp):
            def load_maxima(u):
                sp.wait_ge(s_mx, u + 1)
                for i in range(NPART):
                    sp.dma_start(QX[SROWS + i:SROWS + i + 1, bass.ds(slot(u), GH), :],
                                 MX[i * GH:(i + 1) * GH, :]).then_inc(s_mload, 16)

            def load_batch(b):
                sp.wait_ge(s_qx, b * 2 * STACK_LOADS * 16)
                sp.wait_ge(products, 2 * GROUPS * (b - 1))
                load_stacks(nc, sp, scratch, b, QX, KX, s_qx)

            done = 0
            for b in range(2, B):
                with sp.Fori(done, GROUPS * (b - 1) + 2) as u:
                    load_maxima(u)
                done = GROUPS * (b - 1) + 2
                load_batch(b)
            with sp.Fori(done, STEPS) as u:
                load_maxima(u)

        @block.gpsimd
        def _(pool):
            def step(t, first, last):
                gather_values(c, pool, t, first, products, s_vg, per_group=2)
            peeled(pool, STEPS, step)

        @block.tensor
        def _(pe):
            pe.wait_ge(s_ib, 1)
            for u in range(AHEAD):
                for i in range(TILES):
                    score(pe, u, i, u == 0)
            turn_maxima(pe, 0, True)

            def step(t, first, last, ahead=True):
                for half in range(2):
                    for j in range(GH):
                        if ahead:
                            score(pe, t + AHEAD, 8 * half + 2 * j, False)
                        score_by_key(pe, t, half, j, first)
                        if ahead:
                            score(pe, t + AHEAD, 8 * half + 2 * j + 1, False)
                        if j in (1, 3):
                            if half:
                                value_products(pe, t, j // 2, first)
                            elif not first:
                                value_products(pe, t - 1, 2 + j // 2, False)
                        if half == 0 and j == 2 and not last:
                            if first:
                                pe.wait_ge(s_mx, 1)
                            turn_maxima(pe, t + 1, first)
                        if half == 1 and j == 1 and not first:
                            if not last:
                                pe.wait_ge(s_mx, t + 2)
                            group_end_pe(c, pe, t - 1, s_ct, s_ctx, s_ftr, CT4)
            step(0, True, False)
            with pe.Fori(1, STEPS - AHEAD) as t:
                step(t, False, False)
            step(STEPS - 2, False, False, ahead=False)
            step(STEPS - 1, False, True, ahead=False)
            for kt in (2, 3):
                value_products(pe, STEPS - 1, kt, False)
            group_end_pe(c, pe, STEPS - 1, s_ct, s_ctx, s_ftr, CT4)

        @block.vector
        def _(dve):
            def maxima(u, i):
                dve.wait_ge(scores, u * TILES + i + 1)
                j, qt = i // QT, i % QT
                nc.vector.tensor_reduce(NM[:, qt, j:j + 1], c.ps_t[:, i % 2, :], AX.X, ALU.max,
                                        negate=True).then_inc(maxed, 1)

            def part_op(u, i):
                n = PART_OPS * u + i
                if i == 0:
                    dve.wait_ge(maxed, TILES * (u + 1))
                wait(dve, parted, n)
                part = lambda k: MP[:, :, k, :]
                if i == 0:
                    ins = nc.vector.tensor_copy(NF[:, :, :], NM[:, :, :])
                elif i % 2:
                    ins = nc.vector.tensor_copy(part(i // 2), NF[:, :, :])
                else:
                    ins = nc.vector.tensor_tensor(NF[:, :, :], NF[:, :, :], part(i // 2 - 1), ALU.subtract)
                ins.then_inc(parted, 1)

            nc.vector.tensor_copy(IB[:, :], c.ident[:, :]).then_inc(s_ib, 1)
            for u in range(AHEAD):
                for i in range(TILES):
                    maxima(u, i)
                for i in range(PART_OPS if u == 0 else 1):
                    part_op(u, i)

            def step(t, first, last, ahead=True):
                if not last:
                    dve.wait_ge(mturned, t + 1)
                    dve.wait_ge(parted, PART_OPS * (t + 1) + 1)
                for i in range(TILES):
                    if ahead:
                        maxima(t + AHEAD, i)
                    if i + 1 < PART_OPS and not last:
                        part_op(t + 1, i + 1)
                    if i == 12 and not first:
                        group_end_dve(c, dve, t - 1, s_ftr, s_rden, s_ctx, RDEN)
                if ahead:
                    part_op(t + AHEAD, 0)
            step(0, True, False)
            with dve.Fori(1, STEPS - AHEAD) as t:
                step(t, False, False)
            step(STEPS - 2, False, False, ahead=False)
            step(STEPS - 1, False, True, ahead=False)
            group_end_dve(c, dve, STEPS - 1, s_ftr, s_rden, s_ctx, RDEN)

        @block.scalar
        def _(act):
            def take_maxima(u, first):
                act.wait_ge(mturned, u + 1)
                if not first:
                    act.wait_ge(s_mload, NPART * 16 * u)
                nc.scalar.activation(MX[:, :], c.ps_f[0:GH * NPART, :], ACT.Copy).then_inc(s_mx, 1)

            take_maxima(0, True)

            def step(t, first, last):
                for half in range(2):
                    n = 2 * t + half
                    if not first:
                        act.wait_ge(products, n - 1)
                    for j in range(GH):
                        act.wait_ge(st, n * GH + j + 1)
                        nc.scalar.activation(PT[:, half, j, :, :], c.ps_s[:, 2 * (j % 2):2 * (j % 2) + 2, :],
                                             ACT.Exp).then_inc(exped, 1)
                        if half == 0 and j == 2 and not last:
                            take_maxima(t + 1, False)
                    if half == 0 and not first:
                        group_end_act(c, act, t - 1, products, s_ct, s_ftr, CT4, per_group=2)
            peeled(act, STEPS, step)
            group_end_act(c, act, STEPS - 1, products, s_ct, s_ftr, CT4, per_group=2)


def narrow_causal_attention(c, tag, own, QX, KX, scratch, s_qx, causal):
    nc = c.nc
    PR = c.sb(f"{tag}_PR", [P, 2, QT, S], F32, own)
    PT = c.sb(f"{tag}_PT", [P, 2, GH, QT, S], F32, own)
    CT4 = c.sb(f"{tag}_CT4", [P, S], F32, own)
    NM = c.sb(f"{tag}_NM", [P, 2, QT], F32, own)
    M1 = c.sb(f"{tag}_M1", [P, QT], F32, own)
    M2 = c.sb(f"{tag}_M2", [P, QT], F32, own)
    RDEN = c.sb(f"{tag}_RDEN", [P, QT, GH], F32, own)
    (scores, maxed, exped, turned, out_dve, out_act, products, s_vg, s_ct, s_ftr, s_rden, s_ctx, s_rel) = (
        c.sem(f"{tag}_{n}") for n in ("scores", "maxed", "exped", "turned", "out_dve", "out_act", "products",
                                      "vg", "ct", "ftr", "rden", "ctx", "rel"))
    keys = lambda qt: (qt + 1) * P

    def score_pair(pe, t, j, pair, first):
        n = t * GH + j
        if pair == 0 and j == 0:
            pe.wait_ge(s_qx, (t // GROUPS + 1) * 2 * STACK_LOADS * 16)
        if not first:
            pe.wait_ge(maxed, 2 * (n - 1) + pair + 1)
        head = (t % (2 * GROUPS)) * GH + j
        for qt in (2 * pair, 2 * pair + 1):
            last = nc.tensor.matmul(c.ps_s[:, qt, 0:keys(qt)], QX[:, bass.ds(head, 1), qt * P:(qt + 1) * P],
                                    KX[:, bass.ds(head, 1), 0:keys(qt)], start=True, stop=True)
        last.then_inc(scores, 1)

    def turn(pe, t, j, qt, first):
        n = t * GH + j
        pe.wait_ge(exped, QT * n + qt + 1)
        if not (first and qt < 2):
            before, m = (qt - 2, n) if qt >= 2 else (qt + 2, n - 1)
            if before == 0:
                pe.wait_ge(out_dve, m + 1)
            else:
                pe.wait_ge(out_act, (QT - 1) * m + before)
        for kt in range(keys(qt) // P):
            last = nc.tensor.transpose(c.ps_t[:, qt % 2, kt * P:(kt + 1) * P], PR[:, j % 2, qt, kt * P:(kt + 1) * P],
                                       c.ident[:, :])
        last.then_inc(turned, 1)

    def take(engine, t, side, j, qt, first):
        n = t * GH + j
        engine.wait_ge(turned, QT * n + qt + 1)
        if j == 0 and not first:
            engine.wait_ge(products, t - 1)
        k = keys(qt) // P
        dst = PT[:, side, j, 0:k, qt * P:(qt + 1) * P]
        src = c.ps_t[:, qt % 2, 0:k * P].rearrange("p (k q) -> p k q", q=P)
        if qt:
            nc.scalar.activation(dst, src, ACT.Copy).then_inc(out_act, 1)
        else:
            nc.vector.tensor_copy(dst, src).then_inc(out_dve, 1)

    def value_products(pe, t, side, kt):
        if kt == 0:
            pe.wait_ge(out_dve, GH * (t + 1))
            pe.wait_ge(out_act, (QT - 1) * GH * (t + 1))
            pe.wait_ge(s_vg, t + 1)
            if not (isinstance(t, int) and t == 0):
                pe.wait_ge(s_ct, t)
        for j in range(GH):
            mm = nc.tensor.matmul(c.ps_v[j * CW:(j + 1) * CW, kt * P:S], c.VG[:, kt, j, :],
                                  PT[:, side, j, kt, kt * P:S], start=(kt == 0), stop=(kt == QT - 1))
        if kt == QT - 1:
            mm.then_inc(products, 1)

    def steps(engine, step):
        step(0, 0, 0)
        step(1, 1, 1)
        with engine.Fori(2, STEPS - 2, 2) as t:
            step(t, 0, None)
            step(t + 1, 1, None)
        step(STEPS - 2, 0, None)
        step(STEPS - 1, 1, -1)

    def maxima(dve, t, j, pair):
        n = t * GH + j
        dve.sem_clear(s_rel)
        dve.wait_ge(scores, 2 * n + pair + 1)
        TAB, MASK = causal
        own_ops = Chain(s_rel)
        tiles = (2 * pair, 2 * pair + 1)
        step = QT + 1
        both = lambda t: t.rearrange("p q (n k) -> p (q n) k", k=P)[:, step * tiles[0]:step * tiles[1] + 1:step, :]
        own_ops.inc(nc.vector.tensor_tensor(
            both(PR[:, j % 2]), both(c.ps_s[:, :, :]),
            TAB[:, 3 * P:4 * P].rearrange("p (a k) -> p a k", a=1).broadcast_to([P, 2, P]), ALU.mult))
        own_ops.wait(dve)
        for qt in tiles:
            d = slice(qt * P, (qt + 1) * P)
            own_ops.inc(nc.vector.tensor_tensor_reduce(
                out=PR[:, j % 2, qt, d], in0=PR[:, j % 2, qt, d], in1=MASK[:, :], scale=1.0, scalar=LOWEST,
                op0=ALU.add, op1=ALU.max, accum_out=(M1 if qt else M2)[:, qt:qt + 1]))
        own_ops.wait(dve)
        for qt in tiles:
            if qt:
                d = slice(0, qt * P)
                own_ops.inc(nc.vector.tensor_tensor_reduce(
                    out=PR[:, j % 2, qt, d], in0=c.ps_s[:, qt, d], in1=TAB[:, (3 - qt) * P:3 * P], scale=1.0,
                    scalar=M1[:, qt:qt + 1], op0=ALU.mult, op1=ALU.max, accum_out=M2[:, qt:qt + 1]))
        own_ops.wait(dve)
        nc.vector.tensor_scalar(NM[:, j % 2, 2 * pair:2 * pair + 2], M2[:, 2 * pair:2 * pair + 2], -1.0, None,
                                ALU.mult).then_inc(maxed, 1)

    def probabilities(act, t, j, qt):
        n = t * GH + j
        act.wait_ge(maxed, 2 * n + qt // 2 + 1)
        k = keys(qt)
        nc.scalar.activation(PR[:, j % 2, qt, 0:k], PR[:, j % 2, qt, 0:k], ACT.Exp, bias=NM[:, j % 2, qt:qt + 1]).then_inc(exped, 1)

    def after(t, j):
        return (t, j + 1) if j + 1 < GH else (t + 1, 0)

    with nc.Block() as block:
        @block.sync
        def _(sp):
            for b in range(2, B):
                sp.wait_ge(s_qx, b * 2 * STACK_LOADS * 16)
                sp.wait_ge(scores, 2 * H * (b - 1))
                load_stacks(nc, sp, scratch, b, QX, KX, s_qx)

        @block.gpsimd
        def _(pool):
            def step(t, first, last):
                gather_values(c, pool, t, first, products, s_vg)
            peeled(pool, STEPS, step)

        @block.tensor
        def _(pe):
            score_pair(pe, 0, 0, 0, True)
            score_pair(pe, 0, 0, 1, True)

            def step(t, side, place):
                for j in range(GH):
                    for pair in range(2):
                        if not (place == -1 and j == GH - 1):
                            score_pair(pe, *after(t, j), pair, False)
                        turn(pe, t, j, 2 * pair, place == 0 and j == 0)
                        turn(pe, t, j, 2 * pair + 1, place == 0 and j == 0)
                    if j == 0 and place not in (0, 1):
                        group_end_pe(c, pe, t - 2, s_ct, s_ctx, s_ftr, CT4)
                    if j < 3 and place != 0:
                        for kt in ((0,), (1,), (2, 3))[j]:
                            value_products(pe, t - 1, 1 - side, kt)
            steps(pe, step)
            group_end_pe(c, pe, STEPS - 2, s_ct, s_ctx, s_ftr, CT4)
            for kt in range(QT):
                value_products(pe, STEPS - 1, 1, kt)
            group_end_pe(c, pe, STEPS - 1, s_ct, s_ctx, s_ftr, CT4)

        @block.vector
        def _(dve):
            maxima(dve, 0, 0, 0)
            maxima(dve, 0, 0, 1)

            def step(t, side, place):
                for j in range(GH):
                    for pair in range(2):
                        if pair == 0:
                            take(dve, t, side, j, 0, place in (0, 1))
                        if not (place == -1 and j == GH - 1):
                            maxima(dve, *after(t, j), pair)
                    if j == 1 and place not in (0, 1):
                        group_end_dve(c, dve, t - 2, s_ftr, s_rden, s_ctx, RDEN)
            steps(dve, step)
            for t in (STEPS - 2, STEPS - 1):
                group_end_dve(c, dve, t, s_ftr, s_rden, s_ctx, RDEN)

        @block.scalar
        def _(act):
            for qt in range(QT):
                probabilities(act, 0, 0, qt)

            def step(t, side, place):
                for j in range(GH):
                    for pair in range(2):
                        for qt in (2 * pair, 2 * pair + 1):
                            if qt:
                                take(act, t, side, j, qt, place in (0, 1))
                        if not (place == -1 and j == GH - 1):
                            ahead = after(t, j)
                            probabilities(act, *ahead, 2 * pair)
                            probabilities(act, *ahead, 2 * pair + 1)
                    if j == 3 and place != 0:
                        group_end_act(c, act, t - 1, products, s_ct, s_ftr, CT4, first=(place == 1))
            steps(act, step)
            group_end_act(c, act, STEPS - 1, products, s_ct, s_ftr, CT4)


def norm_chunk(nc, dve, R, dst, ST, MV, RS, chain, done, s_stats, s_rstd, n):
    for i in range(QT):
        chain.inc(nc.vector.bn_stats(ST[:, i, :], R[:, i, :]))
    chain.wait(dve)
    for i in range(QT):
        last = nc.vector.bn_aggr(MV[:, i, :], ST[:, i, :])
    last.then_inc(s_stats, 1)
    dve.wait_ge(s_rstd, 2 * (n + 1))
    for i in range(QT):
        done.inc(nc.vector.tensor_scalar(dst[:, i, :], R[:, i, :], MV[:, i, 0:1], RS[:, i:i + 1],
                                         ALU.subtract, ALU.mult))


def norm_chunk_pool(c, pool, MV, RS, s_stats, s_rstd, n):
    nc = c.nc
    pool.wait_ge(s_stats, n + 1)
    nc.gpsimd.tensor_scalar(RS[:, :], MV[:, :, 1], EPS, None, ALU.add).then_inc(s_rstd, 1)
    pool.wait_ge(s_rstd, 2 * n + 1)
    nc.gpsimd.tensor_tensor(RS[:, :], RS[:, :], c.neghalf[:, :], ALU.pow).then_inc(s_rstd, 1)


def finish(c, tag, source, wo=None, bias=None, mode="post", pre=None, out=None, OT=None):
    nc = c.nc
    with ExitStack() as own:
        W = c.sb(f"{tag}_fW", [P, P], F32, own)
        BO = c.sb(f"{tag}_fBO", [P, P], F32, own)
        WB = c.sb(f"{tag}_fWB", [P, 2], F32, own)
        CT = c.sb(f"{tag}_fCT", [P, 2, QT, P], F32, own)
        R = c.sb(f"{tag}_fR", [P, QT, P], F32, own)
        R2 = c.sb(f"{tag}_fR2", [P, 2, QT, P], F32, own)
        ST = c.sb(f"{tag}_fST", [P, QT, 6], F32, own)
        MV = c.sb(f"{tag}_fMV", [P, QT, 2], F32, own)
        RS = c.sb(f"{tag}_fRS", [P, QT], F32, own)
        s_w, s_t1, s_ct, s_o, s_sum, s_chain, s_stats, s_rstd, s_n, s_t2, s_xt, s_out = (
            c.sem(f"{tag}_f{n}") for n in ("w", "t1", "ct", "o", "sum", "chain", "stats", "rstd", "n", "t2", "xt", "out"))
        n_w = 16 * ((wo is not None) + (bias is not None) + 2 * (pre is not None))
        norms = 1 if (mode == "inner" or pre is None) else 2
        with nc.Block() as block:
            @block.sync
            def _(sp):
                if wo is not None:
                    sp.dma_start(W[:, :], wo).then_inc(s_w, 16)
                if bias is not None:
                    sp.dma_start(BO[:, :], row(bias)).then_inc(s_w, 16)
                if pre is not None:
                    sp.dma_start(WB[:, 0:1], col(pre[0])).then_inc(s_w, 16)
                    sp.dma_start(WB[:, 1:2], col(pre[1])).then_inc(s_w, 16)
                if out is not None:
                    for b in range(B):
                        sp.wait_ge(s_n, QT * (b + 1))
                        sp.dma_start(out[b].rearrange("(n p) d -> p n d", p=P),
                                     c.X[:, b * QT:(b + 1) * QT, :]).then_inc(s_out, 16)
                    sp.wait_ge(s_out, 16 * B)

            @block.gpsimd
            def _(pool):
                for n in range(norms * B):
                    norm_chunk_pool(c, pool, MV, RS, s_stats, s_rstd, n)

            @block.tensor
            def _(pe):
                if n_w:
                    pe.wait_ge(s_w, n_w)

                def before(b):
                    if source == "x":
                        return
                    src = c.CTX[:, b * QT:(b + 1) * QT, :] if source == "ctx" else OT[:, b, :].rearrange("p (i t) -> p i t", i=QT)
                    if source == "ctx":
                        if b >= 2:
                            pe.wait_ge(s_ct, b - 1)
                        for i in range(QT):
                            last = nc.tensor.transpose(c.ps_s[:, b % 2, i * P:(i + 1) * P], src[:, i, :], c.ident[:, :])
                        last.then_inc(s_t1, 1)
                        pe.wait_ge(s_ct, b + 1)
                    if b >= 2:
                        pe.wait_ge(s_sum, b - 1)
                    for i in range(QT):
                        dst = c.ps_s[:, 2 + b % 2, i * P:(i + 1) * P]
                        if source == "ctx":
                            last = nc.tensor.matmul(dst, CT[:, b % 2, i, :], W[:, :], start=True, stop=True)
                        else:
                            last = nc.tensor.transpose(dst, src[:, i, :], c.ident[:, :])
                    last.then_inc(s_o, 1)

                def behind(b):
                    if out is not None:
                        return
                    pe.wait_ge(s_n, QT * (b + 1))
                    if b >= 2:
                        pe.wait_ge(s_xt, b - 1)
                    for i in range(QT):
                        src = c.X[:, b * QT + i, :] if (mode == "post" and pre is None) else R2[:, b % 2, i, :]
                        last = nc.tensor.transpose(c.ps_t[:, b % 2, i * P:(i + 1) * P], src, c.ident[:, :])
                    last.then_inc(s_t2, 1)

                before(0)
                for b in range(B):
                    if b + 1 < B:
                        before(b + 1)
                    behind(b)

            @block.scalar
            def _(act):
                def before(b):
                    if source == "ctx":
                        act.wait_ge(s_t1, b + 1)
                        if b >= 2:
                            act.wait_ge(s_o, b - 1)
                        nc.scalar.activation(CT[:, b % 2, :, :], c.ps_s[:, b % 2, :].rearrange("p (i t) -> p i t", i=QT),
                                             ACT.Copy).then_inc(s_ct, 1)

                def behind(b):
                    if out is not None:
                        return
                    act.wait_ge(s_t2, b + 1)
                    dst, src = c.XT[:, b * S:(b + 1) * S], c.ps_t[:, b % 2, :]
                    if pre is None:
                        nc.scalar.activation(dst, src, ACT.Copy).then_inc(s_xt, 1)
                    else:
                        nc.scalar.activation(dst, src, ACT.Identity, bias=WB[:, 1:2], scale=WB[:, 0:1]).then_inc(s_xt, 1)
                if n_w:
                    act.wait_ge(s_w, n_w)
                before(0)
                for b in range(B):
                    if b + 1 < B:
                        before(b + 1)
                    behind(b)

            @block.vector
            def _(dve):
                chain, done = Chain(s_chain), Chain(s_n)
                if n_w:
                    dve.wait_ge(s_w, n_w)
                n = 0
                for b in range(B):
                    x = c.X[:, b * QT:(b + 1) * QT, :]
                    r = x
                    if source != "x":
                        dve.wait_ge(s_o, b + 1)
                        o = c.ps_s[:, 2 + b % 2, :].rearrange("p (i t) -> p i t", i=QT)
                        r = R[:, :, :]
                        nc.vector.tensor_tensor(r, x, o, ALU.add).then_inc(s_sum, 1)
                        dve.wait_ge(s_sum, b + 1)
                        if bias is not None:
                            chain.inc(nc.vector.tensor_tensor(
                                r, r, BO[:, :].rearrange("p (a d) -> p a d", a=1).broadcast_to([P, QT, P]), ALU.add))
                            chain.wait(dve)
                    if mode == "inner":
                        chain.inc(nc.vector.tensor_tensor(x, x, r, ALU.add))
                        dst = R2[:, b % 2]
                    else:
                        dst = x
                    if mode == "inner" and b >= 2:
                        dve.wait_ge(s_t2, b - 1)
                    norm_chunk(nc, dve, r, dst, ST, MV, RS, chain, done if norms == 1 else chain, s_stats, s_rstd, n)
                    n += 1
                    if norms == 2:
                        chain.wait(dve)
                        if b >= 2:
                            dve.wait_ge(s_t2, b - 1)
                        norm_chunk(nc, dve, x, R2[:, b % 2], ST, MV, RS, chain, done, s_stats, s_rstd, n)
                        n += 1
                    done.wait(dve)


def distance_tables(c, rel, TAB, MASK, own):
    nc = c.nc
    near = QT * P - P - CLIP
    DI = c.sb("rel_DI", [P, QT * P - near], mybir.dt.int32, own)
    D = c.sb("rel_D", [P, QT * P - near], F32, own)
    T = c.sb("rel_T", [P, QT * P - near], F32, own)
    E = c.sb("rel_E", [P, CLIP + 1], F32, own)
    s_e, s_iota, s_chain, s_rows = (c.sem(f"rel_{n}") for n in ("e", "iota", "chain", "rows"))
    with nc.Block() as block:
        @block.sync
        def _(sp):
            sp.dma_start(E[:, :], row(rel)).then_inc(s_e, 16)

        @block.gpsimd
        def _(pool):
            nc.gpsimd.iota(DI[:, :], pattern=[[-1, QT * P - near]], base=(QT - 1) * P - near, channel_multiplier=1)\
                .then_inc(s_iota, 1)
            nc.gpsimd.memset(MASK[:, :], 0.0).then_inc(s_iota, 1)
            pool.wait_ge(s_iota, 2)
            nc.gpsimd.affine_select(out=MASK[:, :], in_=MASK[:, :], compare_op=ALU.is_ge, fill=MASKED,
                                    base=0, pattern=[[-1, P]], channel_multiplier=1)

        @block.vector
        def _(dve):
            chain = Chain(s_chain)
            dve.wait_ge(s_e, 16)
            dve.wait_ge(s_iota, 1)
            chain.inc(nc.vector.tensor_scalar(E[:, :], E[:, :], ISQ8, None, ALU.mult))
            chain.inc(nc.vector.tensor_copy(D[:, :], DI[:, :]))
            chain.wait(dve)
            chain.inc(nc.vector.tensor_copy(TAB[:, 0:near], E[:, CLIP:CLIP + 1].broadcast_to([P, near])))
            chain.inc(nc.vector.tensor_scalar(TAB[:, near:], D[:, :], float(CLIP), E[:, CLIP:CLIP + 1], ALU.is_ge, ALU.mult))
            chain.wait(dve)
            constant_rows(c, dve, nc.vector)
            for r in range(CLIP):
                chain.inc(nc.vector.tensor_scalar(T[:, :], D[:, :], float(r), E[:, r:r + 1], ALU.is_equal, ALU.mult))
                chain.wait(dve)
                chain.inc(nc.vector.tensor_tensor(TAB[:, near:], TAB[:, near:], T[:, :], ALU.add))
                chain.wait(dve)


def narrow_self_attention(c, tag, wq, wk, wv, scratch, bq=None, bk=None, bv=None, qscale=1.0, rel=None):
    with ExitStack() as own:
        QX, KX = c.QX, c.KX
        c.VN = c.sb(f"{tag}_VN", [P, NT, P], F32, own)
        s_qx = c.sem(f"{tag}_qx")
        causal = None
        if rel is not None:
            TAB = c.sb(f"{tag}_TAB", [P, QT * P], F32, own)
            MASK = c.sb(f"{tag}_MASK", [P, P], F32, own)
            causal = (TAB, MASK)
            with ExitStack() as brief:
                distance_tables(c, rel, *causal, brief)
        with ExitStack() as brief:
            narrow_projections(c, tag, brief, scratch, QX, KX, s_qx, wq, wk, wv, bq, bk, bv, qscale)
        if causal:
            narrow_causal_attention(c, tag, own, QX, KX, scratch, s_qx, causal)
        else:
            narrow_full_attention(c, tag, own, QX, KX, scratch, s_qx)


def cross_operands(c, tag, wk, bk, wv, bv, KX, VB):
    nc = c.nc
    GR = SROWS // HD8
    with ExitStack() as own:
        WK = c.sb(f"{tag}_WK", [P, HD8], F32, own)
        WKR = c.sb(f"{tag}_WKR", [P, SROWS], F32, own)
        BK = c.sb(f"{tag}_BK", [SROWS, 1], F32, own)
        WV = c.sb(f"{tag}_oWV", [P, HD8], F32, own)
        BV = c.sb(f"{tag}_oBV", [KC, HD8], F32, own)
        G = c.sb(f"{tag}_G", [SROWS, GR], F32, own)
        MK = c.sb(f"{tag}_MK", [SROWS, NPART], F32, own)
        FULL = c.sb(f"{tag}_KF", [SROWS, B * KC], F32, own)
        PARTS = c.sb(f"{tag}_KP", [SROWS, NPART, B * KC], BF16, own)
        s_w, s_g, s_ops, s_k, s_v, s_split = (c.sem(f"{tag}_o{n}") for n in ("w", "g", "ops", "k", "v", "split"))
        with nc.Block() as block:
            @block.sync
            def _(sp):
                sp.dma_start(WK[:, :], wk).then_inc(s_w, 16)
                sp.dma_start(WV[:, :], wv).then_inc(s_w, 16)
                sp.dma_start(BV[:, :], row(bv, KC)).then_inc(s_w, 16)
                for g in range(NPART * NPART):
                    sp.dma_start(BK[g * HD8:(g + 1) * HD8, :], col(bk)).then_inc(s_w, 16)

            @block.gpsimd
            def _(pool):
                nc.gpsimd.memset(VB[:, :, :], 0.0)
                nc.gpsimd.memset(G[:, :], 1.0).then_inc(s_g, 1)
                pool.wait_ge(s_g, 1)
                nc.gpsimd.affine_select(out=G[:, :], in_=G[:, :], compare_op=ALU.is_ge, fill=0.0, base=0,
                                        pattern=[[-HD8, GR]], channel_multiplier=1).then_inc(s_g, 1)
                pool.wait_ge(s_g, 2)
                nc.gpsimd.affine_select(out=G[:, :], in_=G[:, :], compare_op=ALU.is_ge, fill=0.0, base=HD8 - 1,
                                        pattern=[[HD8, GR]], channel_multiplier=-1).then_inc(s_g, 1)

            @block.tensor
            def _(pe):
                pe.wait_ge(s_w, 16 * 12)
                pe.wait_ge(s_ops, 2)
                nc.tensor.matmul(c.ps_s[0:SROWS, 0, 0:B * KC], WKR[:, :], c.CTT[:, :], start=True, stop=True).then_inc(s_k, 1)
                for b in range(B):
                    last = nc.tensor.matmul(c.ps_t[0:KC, 0, b * HD8:(b + 1) * HD8], c.CTT[:, b * KC:(b + 1) * KC], WV[:, :],
                                            start=True, stop=True)
                last.then_inc(s_v, 1)

            @block.vector
            def _(dve):
                ops, split = Chain(s_ops), Chain(s_split)
                dve.wait_ge(s_w, 16 * 12)
                ops.inc(nc.vector.memset(WKR[:, NPART * NPART * HD8:], 0.0))
                ops.inc(nc.vector.tensor_copy(
                    WKR[:, 0:NPART * NPART * HD8].rearrange("p (g d) -> p g d", d=HD8),
                    WK[:, :].rearrange("p (a d) -> p a d", a=1).broadcast_to([P, NPART * NPART, HD8])))
                dve.wait_ge(s_g, 3)
                g = G[:, 0:NPART * NPART].rearrange("p (i j) -> p j i", j=NPART)
                ops.inc(nc.vector.reduce_sum(MK[:, :], g, AX.X))
                dve.wait_ge(s_k, 1)
                rows = NPART * NPART * HD8
                ops.inc(nc.vector.tensor_copy(FULL[:, :], c.ps_s[0:SROWS, 0, 0:B * KC]))
                ops.wait(dve)
                ops.inc(nc.vector.tensor_scalar(FULL[0:rows, :], FULL[0:rows, :], BK[0:rows, :], None, ALU.add))
                ops.wait(dve)
                split_parts(nc, dve, split, FULL[:, :], lambda i: PARTS[:, i, :])
                kx = KX[:, :, :].rearrange("p b k -> p (b k)")
                ops.inc(nc.vector.tensor_scalar(kx, PARTS[:, 0, :], MK[:, 0:1], None, ALU.mult))
                for i in (1, 2):
                    ops.wait(dve)
                    ops.inc(nc.vector.scalar_tensor_tensor(kx, PARTS[:, i, :], MK[:, i:i + 1], kx, ALU.mult, ALU.add))
                dve.wait_ge(s_v, 1)
                nc.vector.tensor_tensor(VB[0:KC, :, :], c.ps_t[0:KC, 0, 0:B * HD8].rearrange("p (b d) -> p b d", b=B),
                                        BV[:, :].rearrange("p (a d) -> p a d", a=1).broadcast_to([KC, B, HD8]), ALU.add)


def narrow_cross(c, tag, own, QX, KX, VB, scratch, s_qx):
    nc = c.nc
    SC = c.sb(f"{tag}_SC", [P, 2, QT, KC], F32, own)
    PR = c.sb(f"{tag}_PR", [P, 2, QT, KC], F32, own)
    PT = c.sb(f"{tag}_PT", [SROWS, GH, S], F32, own)
    CT4 = c.sb(f"{tag}_CT4", [P, S], F32, own)
    M = c.sb(f"{tag}_M", [P, 2, QT], F32, own)
    RDEN = c.sb(f"{tag}_RDEN", [P, QT, GH], F32, own)
    (scores, maxed, lessened, exped, turned, taken, products, s_vg, s_ct, s_ftr, s_rden, s_ctx, s_zero) = (
        c.sem(f"{tag}_{n}") for n in ("scores", "maxed", "lessened", "exped", "turned", "taken", "products",
                                      "vg", "ct", "ftr", "rden", "ctx", "ptzero"))
    NK = GH

    def ahead(t, j, k):
        return (t, j + k) if j + k < GH else (t + 1, j + k - GH)

    def score(pe, t, j, first):
        n = t * GH + j
        if j == 0:
            pe.wait_ge(s_qx, (t // GROUPS + 1) * STACK_LOADS * 16)
        if not first:
            pe.wait_ge(lessened, n - NK + 1)
        head = (t % (2 * GROUPS)) * GH + j
        for qt in range(QT):
            last = nc.tensor.matmul(c.ps_s[:, j, qt * KC:(qt + 1) * KC], QX[0:SROWS, bass.ds(head, 1), qt * P:(qt + 1) * P],
                                    KX[:, bass.ds(t // GROUPS, 1), :], start=True, stop=True)
        last.then_inc(scores, 1)

    with nc.Block() as block:
        @block.sync
        def _(sp):
            for b in range(2, B):
                sp.wait_ge(s_qx, b * STACK_LOADS * 16)
                sp.wait_ge(scores, H * (b - 1))
                load_stacks(nc, sp, scratch, b, QX, None, s_qx)

        @block.gpsimd
        def _(pool):
            nc.gpsimd.memset(PT[64:SROWS, :, :], 0.0).then_inc(s_zero, 1)
            pool.wait_ge(s_zero, 1)

            def step(t, first, last):
                gather_values(c, pool, t, first, products, s_vg, VB)
            peeled(pool, STEPS, step)

        @block.tensor
        def _(pe):
            score(pe, 0, 0, True)
            score(pe, 0, 1, True)

            def step(t, first, last):
                for j in range(GH):
                    n = t * GH + j
                    pe.wait_ge(exped, n + 1)
                    if not (first and j < 2):
                        pe.wait_ge(taken, n - 1)
                    for qt in range(QT):
                        mm = nc.tensor.transpose(c.ps_t[0:KC, j % 2, qt * P:(qt + 1) * P], PR[:, j % 2, qt, :], c.ident[:, :])
                    mm.then_inc(turned, 1)
                    if not (last and j >= 2):
                        score(pe, *ahead(t, j, 2), first and j < 2)
                    if j == 1 and not first:
                        group_end_pe(c, pe, t - 1, s_ct, s_ctx, s_ftr, CT4)
                pe.wait_ge(taken, GH * (t + 1))
                pe.wait_ge(s_vg, t + 1)
                if not first:
                    pe.wait_ge(s_ct, t)
                for j in range(GH):
                    mm = nc.tensor.matmul(c.ps_v[j * CW:(j + 1) * CW, :], c.VG[0:SROWS, 0, 0, :], PT[:, j, :],
                                          start=True, stop=True)
                mm.then_inc(products, 1)
            peeled(pe, STEPS, step)
            group_end_pe(c, pe, STEPS - 1, s_ct, s_ctx, s_ftr, CT4)

        @block.vector
        def _(dve):
            def lessen(t, j):
                n = t * GH + j
                dve.wait_ge(scores, n + 1)
                src = c.ps_s[:, j, 0:QT * KC].rearrange("p (q k) -> p q k", q=QT)
                nc.vector.reduce_max(M[:, j % 2, :], src, AX.X).then_inc(maxed, 1)
                dve.wait_ge(maxed, n + 1)
                nc.vector.tensor_tensor(SC[:, j % 2], src, M[:, j % 2, :].rearrange("p (q a) -> p q a", a=1).broadcast_to([P, QT, KC]),
                                        ALU.subtract).then_inc(lessened, 1)
            lessen(0, 0)
            lessen(0, 1)

            def step(t, first, last):
                for j in range(GH):
                    if not (last and j >= 2):
                        nt, nj = ahead(t, j, 2)
                        dve.wait_ge(exped, t * GH + j + 1)
                        lessen(nt, nj)
                    if j == 1 and not first:
                        group_end_dve(c, dve, t - 1, s_ftr, s_rden, s_ctx, RDEN)
            peeled(dve, STEPS, step)
            group_end_dve(c, dve, STEPS - 1, s_ftr, s_rden, s_ctx, RDEN)

        @block.scalar
        def _(act):
            def prob(t, j, first):
                n = t * GH + j
                act.wait_ge(lessened, n + 1)
                if not first:
                    act.wait_ge(turned, n - 1)
                nc.scalar.activation(PR[:, j % 2], SC[:, j % 2], ACT.Exp).then_inc(exped, 1)
            prob(0, 0, True)
            prob(0, 1, True)
            act.wait_ge(s_zero, 1)

            def step(t, first, last):
                for j in range(GH):
                    n = t * GH + j
                    act.wait_ge(turned, n + 1)
                    if j == 0:
                        act.wait_ge(products, t)
                    nc.scalar.activation(PT[0:KC, j, :], c.ps_t[0:KC, j % 2, :], ACT.Copy).then_inc(taken, 1)
                    if not (last and j >= 2):
                        prob(*ahead(t, j, 2), False)
                    if j == 0 and not first:
                        group_end_act(c, act, t - 1, products, s_ct, s_ftr, CT4)
            peeled(act, STEPS, step)
            group_end_act(c, act, STEPS - 1, products, s_ct, s_ftr, CT4)


def narrow_cross_attention(c, tag, wq, bq, wk, bk, wv, bv, scratch):
    with ExitStack() as own:
        QX = c.QX
        KX = c.sb(f"{tag}_KX", [SROWS, B, KC], BF16, own)
        VB = c.sb(f"{tag}_VB", [SROWS, B, HD8], F32, own)
        s_qx = c.sem(f"{tag}_qx")
        with ExitStack() as brief:
            narrow_projections(c, tag, brief, scratch, QX, None, s_qx, wq, None, None, bq=bq)
        cross_operands(c, tag, wk, bk, wv, bv, KX, VB)
        narrow_cross(c, tag, own, QX, KX, VB, scratch, s_qx)


def wide_self_attention(c, tag, wq, wk, wv, wo, OT):
    nc = c.nc
    SPAN = 2 * S - P
    TM = QT * H
    with ExitStack() as own:
        WQ, WK, WV = (c.sb(f"{tag}_W{n}", [P, H * HD64], F32, own) for n in "qkv")
        WO = c.sb(f"{tag}_Wo", [P, PAIRS, P], F32, own)
        BH = c.sb(f"{tag}_BH", [P, H, SPAN], F32, own)
        XB = c.sb(f"{tag}_XB", [P, S], F32, own)
        VB = c.sb(f"{tag}_VB", [P, QT, H * HD64], F32, own)
        Q = c.sb(f"{tag}_Q", [P, 2, S], F32, own)
        KZ = c.sb(f"{tag}_KZ", [P, 2, 2, S], F32, own)
        PR = c.sb(f"{tag}_PR", [P, 2, QT, S], F32, own)
        PT = c.sb(f"{tag}_PT", [P, 2, 2, QT, S], F32, own)
        CT = c.sb(f"{tag}_CT", [P, S], F32, own)
        M = c.sb(f"{tag}_M", [P, 2, QT], F32, own)
        NM = c.sb(f"{tag}_NM", [P, 2, QT], F32, own)
        DEN = c.sb(f"{tag}_DEN", [P, 2, QT], F32, own)
        GO = c.sb(f"{tag}_GO", [P, 1], F32, own)
        RDEN = c.sb(f"{tag}_RDEN", [P, 2, QT], F32, own)
        (s_w, s_made, s_iota, s_xb, s_vproj, v_act, v_dve, proj, q_out, k_out, scores, biased, negated, exped, inverted,
         normed, turned, taken, products, heads_out, added, s_ot) = (
            c.sem(f"{tag}_{n}") for n in
            ("w", "made", "iota", "xb", "vproj", "v_act", "v_dve", "proj", "q_out", "k_out", "scores", "biased", "negated",
             "exped", "inverted", "normed", "turned", "taken", "products", "heads_out", "added", "ot"))
        ps_q, ps_k, ps_o = c.ps_s[:, 2, :], c.ps_f[:, :], c.ps_s[:, 3, :]

        with nc.Block() as block:
            @block.sync
            def _(sp):
                for dst, src in ((WQ, wq), (WK, wk), (WV, wv)):
                    sp.dma_start(dst[:, :], src).then_inc(s_w, 16)
                sp.dma_start(WO[:, :, :], wo.rearrange("(g p) n -> p g n", p=P)).then_inc(s_w, 16)

            @block.gpsimd
            def _(pool):
                DI = BH[:, 0, :].bitcast(mybir.dt.int32)
                nc.gpsimd.memset(KZ[:, :, :, :], 0.0)
                nc.gpsimd.iota(DI, pattern=[[-1, SPAN]], base=S - P, channel_multiplier=1).then_inc(s_iota, 1)

            @block.vector
            def _(dve):
                chain = Chain(s_made)
                T = BH[:, H - 1, :]
                dve.wait_ge(s_iota, 1)
                chain.inc(nc.vector.tensor_copy(BH[:, 1, :], BH[:, 0, :].bitcast(mybir.dt.int32)))
                chain.wait(dve)
                chain.inc(nc.vector.tensor_scalar(BH[:, 2, :], BH[:, 1, :], -1.0, None, ALU.mult))
                chain.wait(dve)
                chain.inc(nc.vector.tensor_tensor(T, BH[:, 1, :], BH[:, 2, :], ALU.min))
                for h in range(H):
                    chain.wait(dve)
                    slope = 2.0 ** (-8.0 / (H - h))
                    chain.inc(nc.vector.tensor_scalar(BH[:, h, :], T, slope, None, ALU.mult))

        with nc.Block() as block:
            @block.tensor
            def _(pe):
                pe.wait_ge(s_w, 16 * 4)

                def project(b, p):
                    if p >= 1:
                        wait(pe, q_out, b * PAIRS + p)
                        wait(pe, k_out, b * H + 2 * p)
                    w = slice(p * P, (p + 1) * P)
                    nc.tensor.matmul(ps_q, WQ[:, w], XB[:, :], start=True, stop=True).then_inc(proj, 1)
                    nc.tensor.matmul(ps_k, WK[:, w], XB[:, :], start=True, stop=True).then_inc(proj, 1)

                def score(b, i, qt):
                    m, p = QT * i + qt, i // 2
                    if i % 2 == 0 and qt == 0:
                        wait(pe, q_out, b * PAIRS + p + 1)
                        wait(pe, k_out, b * H + 2 * p + 2)
                    wait(pe, biased, b * TM + max(m - 1, 0))
                    nc.tensor.matmul(c.ps_s[:, qt % 2, :], Q[:, p % 2, qt * P:(qt + 1) * P], KZ[:, p % 2, i % 2, :],
                                     start=True, stop=True).then_inc(scores, 1)

                def turn(b, i, qt):
                    m = QT * i + qt
                    wait(pe, normed, b * TM + m + 1)
                    wait(pe, taken, b * TM + max(m - 1, 0))
                    for kt in range(QT):
                        mm = nc.tensor.transpose(c.ps_t[:, qt % 2, kt * P:(kt + 1) * P],
                                                 PR[:, i % 2, qt, kt * P:(kt + 1) * P], c.ident[:, :])
                    mm.then_inc(turned, 1)

                def weigh(b, p):
                    wait(pe, taken, b * TM + 2 * QT * (p + 1))
                    wait(pe, heads_out, b * PAIRS + p)
                    for kt in range(QT):
                        for e in range(2):
                            h = 2 * p + e
                            mm = nc.tensor.matmul(c.ps_v[e * HD64:(e + 1) * HD64, :], VB[:, kt, h * HD64:(h + 1) * HD64],
                                                  PT[:, p % 2, e, kt, :], start=(kt == 0), stop=(kt == QT - 1))
                    mm.then_inc(products, 1)

                def add(b, p):
                    wait(pe, heads_out, b * PAIRS + p + 1)
                    if p == 0:
                        wait(pe, s_ot, b)
                    nc.tensor.matmul(ps_o, WO[:, p, :], CT[:, :], start=(p == 0), stop=(p == PAIRS - 1)).then_inc(added, 1)

                def batch(b):
                    wait(pe, s_xb, b + 1)
                    project(b, 0)
                    for g in range(2 * QT):
                        if g >= 2:
                            wait(pe, (v_act, v_dve)[g % 2], b * QT + g // 2)
                        else:
                            wait(pe, taken, b * TM)
                        nc.tensor.matmul(c.ps_t[:, g % 2, :], XB[:, (g // 2) * P:(g // 2 + 1) * P],
                                         WV[:, (g % 2) * 512:(g % 2 + 1) * 512], start=True, stop=True).then_inc(s_vproj, 1)
                    for qt in range(QT):
                        score(b, 0, qt)
                    wait(pe, v_act, b * QT + QT)
                    wait(pe, v_dve, b * QT + QT)
                    for i in range(H):
                        p = i // 2
                        for qt in range(QT):
                            turn(b, i, qt)
                            if i + 1 < H:
                                score(b, i + 1, qt)
                            if qt == 0 and i % 2 == 0 and p:
                                weigh(b, p - 1)
                            if qt == 3 and i % 2 == 0 and p:
                                add(b, p - 1)
                            if qt == 1 and i % 2 == 0 and p + 1 < PAIRS:
                                project(b, p + 1)
                    weigh(b, PAIRS - 1)
                    add(b, PAIRS - 1)
                first_then_loop(pe, B, batch)

            @block.vector
            def _(dve):
                def bias(b, h, qt):
                    m = QT * h + qt
                    if h < 2:
                        wait(dve, turned, b * TM)
                    else:
                        wait(dve, turned, b * TM + m - 2 * QT + 1)
                    wait(dve, scores, b * TM + m + 1)
                    nc.vector.memset(GO[:, :], 0.0)
                    nc.vector.tensor_tensor_reduce(
                        out=PR[:, h % 2, qt, :], in0=c.ps_s[:, qt % 2, :], in1=BH[:, h, S - P - qt * P:2 * S - P - qt * P],
                        scale=1.0, scalar=LOWEST, op0=ALU.add, op1=ALU.max, accum_out=M[:, h % 2, qt:qt + 1]).then_inc(biased, 1)
                    wait(dve, biased, b * TM + m + 1)
                    nc.vector.tensor_scalar(NM[:, h % 2, qt:qt + 1], M[:, h % 2, qt:qt + 1], -1.0, None,
                                            ALU.mult).then_inc(negated, 1)

                def norm(b, h, qt):
                    m = QT * h + qt
                    wait(dve, exped, b * TM + m + 1)
                    nc.vector.reciprocal(RDEN[:, h % 2, qt:qt + 1], DEN[:, h % 2, qt:qt + 1]).then_inc(inverted, 1)
                    wait(dve, inverted, b * TM + m + 1)
                    nc.vector.tensor_scalar(PR[:, h % 2, qt, :], PR[:, h % 2, qt, :], RDEN[:, h % 2, qt:qt + 1], None,
                                            ALU.mult).then_inc(normed, 1)

                def head(b, h):
                    for qt in range(QT):
                        bias(b, h, qt)
                        if qt:
                            norm(b, h, qt - 1)
                        if qt == 1 and h % 2 and h > 1:
                            take_heads(b, h // 2 - 1)
                        if qt == 2 and h % 2 and h + 1 < H:
                            keys_out(b, (h + 1) // 2)
                    norm(b, h, QT - 1)

                def keys_out(b, p):
                    wait(dve, proj, b * H + 2 * p + 2)
                    wait(dve, scores, b * TM + max(2 * QT * (p - 1), 0))
                    for e in range(2):
                        r = slice(e * HD64, (e + 1) * HD64)
                        nc.vector.tensor_copy(KZ[r, p % 2, e, :], ps_k[r, :]).then_inc(k_out, 1)

                def take_heads(b, p):
                    wait(dve, products, b * PAIRS + p + 1)
                    wait(dve, added, b * PAIRS + p)
                    nc.vector.tensor_copy(CT[:, :], c.ps_v[:, :]).then_inc(heads_out, 1)

                def batch(b):
                    wait(dve, s_vproj, b * 2 * QT)
                    wait(dve, proj, b * H)
                    nc.vector.tensor_copy(XB[:, :], c.XT[:, bass.ds(b * S, S)]).then_inc(s_xb, 1)
                    keys_out(b, 0)
                    wait(dve, products, b * PAIRS)
                    for g in range(1, 2 * QT, 2):
                        wait(dve, s_vproj, b * 2 * QT + g + 1)
                        nc.vector.tensor_copy(VB[:, g // 2, 512:1024], c.ps_t[:, 1, :]).then_inc(v_dve, 1)
                    head(b, 0)
                    for i in range(H):
                        if i + 1 < H:
                            head(b, i + 1)
                    take_heads(b, PAIRS - 1)
                first_then_loop(dve, B, batch)

            @block.scalar
            def _(act):
                def exp(b, h, qt):
                    m = QT * h + qt
                    wait(act, negated, b * TM + m + 1)
                    nc.scalar.activation(PR[:, h % 2, qt, :], PR[:, h % 2, qt, :], ACT.Exp, bias=NM[:, h % 2, qt:qt + 1],
                                         accum_out=DEN[:, h % 2, qt:qt + 1]).then_inc(exped, 1)

                def take(b, i, qt):
                    m = QT * i + qt
                    wait(act, turned, b * TM + m + 1)
                    wait(act, products, b * PAIRS + i // 2 - 1)
                    nc.scalar.activation(PT[:, i // 2 % 2, i % 2, :, qt * P:(qt + 1) * P],
                                         c.ps_t[:, qt % 2, :].rearrange("p (k q) -> p k q", q=P), ACT.Copy).then_inc(taken, 1)

                def queries_out(b, p):
                    wait(act, proj, b * H + 2 * p + 1)
                    wait(act, scores, b * TM + max(2 * QT * (p - 1), 0))
                    nc.scalar.activation(Q[:, p % 2, :], ps_q, ACT.Copy, scale=ISQ64).then_inc(q_out, 1)

                def batch(b):
                    queries_out(b, 0)
                    wait(act, products, b * PAIRS)
                    for g in range(0, 2 * QT, 2):
                        wait(act, s_vproj, b * 2 * QT + g + 1)
                        nc.scalar.activation(VB[:, g // 2, 0:512], c.ps_t[:, 0, :], ACT.Copy).then_inc(v_act, 1)
                    for qt in range(QT):
                        exp(b, 0, qt)
                    for i in range(H):
                        for qt in range(QT):
                            take(b, i, qt)
                            if i + 1 < H:
                                exp(b, i + 1, qt)
                            if qt == 2 and i % 2 == 0 and i // 2 + 1 < PAIRS:
                                queries_out(b, i // 2 + 1)
                    wait(act, added, b * PAIRS + PAIRS)
                    nc.scalar.activation(OT[:, bass.ds(b, 1), :], ps_o, ACT.Copy).then_inc(s_ot, 1)
                first_then_loop(act, B, batch)


def wide_cross_attention(c, tag, wq, bq, wk, bk, wv, bv, wo, bo, OT):
    nc = c.nc
    with ExitStack() as own:
        WQ, WK, WV = (c.sb(f"{tag}_W{n}", [P, H * HD64], F32, own) for n in "qkv")
        WO = c.sb(f"{tag}_Wo", [P, PAIRS, P], F32, own)
        BQ = c.sb(f"{tag}_BQ", [P, PAIRS], F32, own)
        BK = c.sb(f"{tag}_BK", [P, PAIRS], F32, own)
        BV = c.sb(f"{tag}_BV", [KC, H * HD64], F32, own)
        BO = c.sb(f"{tag}_BO", [P, 1], F32, own)
        KB = c.sb(f"{tag}_KB", [P, PAIRS, B, 2, KC], F32, own)
        VA = c.sb(f"{tag}_VA", [SROWS, B, H * HD64], F32, own)
        VB = c.sb(f"{tag}_VB", [SROWS, H * HD64], F32, own)
        Q = c.sb(f"{tag}_Q", [P, 2, S], F32, own)
        SC = c.sb(f"{tag}_SC", [P, 2, 2 * QT, KC], F32, own)
        PR = c.sb(f"{tag}_PR", [P, 2, 2 * QT, KC], F32, own)
        PT = c.sb(f"{tag}_PT", [SROWS, 2, S], F32, own)
        CT = c.sb(f"{tag}_CT", [P, S], F32, own)
        M = c.sb(f"{tag}_M", [P, 2 * QT], F32, own)
        DEN = c.sb(f"{tag}_DEN", [P, 2 * QT], F32, own)
        RDEN = c.sb(f"{tag}_RDEN", [P, 2 * QT], F32, own)
        (s_w, s_zero, s_scaled, s_kproj, s_kout, s_vproj, s_vout, s_vb, proj, q_out, scores, maxed, lessened, exped, summed,
         inverted, normed, turned, t_act, t_dve, products, heads_out, added, s_ot) = (
            c.sem(f"{tag}_{n}") for n in
            ("w", "zero", "scaled", "kproj", "kout", "vproj", "vout", "vb", "proj", "q_out", "scores", "maxed", "lessened",
             "exped", "summed", "inverted", "normed", "turned", "t_act", "t_dve", "products", "heads_out", "added", "ot"))
        N_W = 16 * 8

        with nc.Block() as block:
            @block.sync
            def _(sp):
                for dst, src in ((WQ, wq), (WK, wk), (WV, wv)):
                    sp.dma_start(dst[:, :], src.rearrange("m h d -> m (h d)")).then_inc(s_w, 16)
                sp.dma_start(WO[:, :, :], wo.rearrange("(g e) d n -> (e d) g n", e=2)).then_inc(s_w, 16)
                sp.dma_start(BQ[:, :], bq.rearrange("(g e) d -> (e d) g", e=2),
                             allow_slow_non_contiguous=True).then_inc(s_w, 16)
                sp.dma_start(BK[:, :], bk.rearrange("(g e) d -> (e d) g", e=2),
                             allow_slow_non_contiguous=True).then_inc(s_w, 16)
                sp.dma_start(BV[:, :], row(bv.rearrange("h d -> (h d)"), KC)).then_inc(s_w, 16)
                sp.dma_start(BO[:, :], col(bo)).then_inc(s_w, 16)

            @block.gpsimd
            def _(pool):
                nc.gpsimd.memset(KB[:, :, :, :, :], 0.0).then_inc(s_zero, 1)
                pool.wait_ge(s_zero, 1)
                nc.gpsimd.memset(VA[64:SROWS, :, :], 0.0).then_inc(s_zero, 1)
                pool.wait_ge(s_zero, 2)
                nc.gpsimd.memset(PT[64:SROWS, :, :], 0.0)

            @block.tensor
            def _(pe):
                pe.wait_ge(s_w, N_W)
                for p in range(PAIRS):
                    if p >= 2:
                        pe.wait_ge(s_kout, 2 * (p - 1))
                    nc.tensor.matmul(c.ps_s[:, p % 2, 0:B * KC], WK[:, p * P:(p + 1) * P], c.CTT[:, :],
                                     start=True, stop=True).then_inc(s_kproj, 1)
                    b, half = p // 2, p % 2
                    if p >= 2:
                        pe.wait_ge(s_vout, p - 1)
                    nc.tensor.matmul(c.ps_t[0:KC, half, :], c.CTT[:, b * KC:(b + 1) * KC], WV[:, half * 512:(half + 1) * 512],
                                     start=True, stop=True).then_inc(s_vproj, 1)

            @block.vector
            def _(dve):
                dve.wait_ge(s_w, N_W)
                nc.vector.tensor_scalar(BQ[:, :], BQ[:, :], ISQ64, None, ALU.mult).then_inc(s_scaled, 1)
                dve.wait_ge(s_zero, 2)
                for p in range(PAIRS):
                    dve.wait_ge(s_kproj, p + 1)
                    for e in range(2):
                        r = slice(e * HD64, (e + 1) * HD64)
                        nc.vector.tensor_scalar(KB[r, p, :, e, :], c.ps_s[r, p % 2, 0:B * KC].rearrange("p (b k) -> p b k", b=B),
                                                BK[r, p:p + 1], None, ALU.add).then_inc(s_kout, 1)
                    b, half = p // 2, p % 2
                    dve.wait_ge(s_vproj, p + 1)
                    v = slice(half * 512, (half + 1) * 512)
                    nc.vector.tensor_tensor(VA[0:KC, b, v], c.ps_t[0:KC, half, :], BV[:, v], ALU.add).then_inc(s_vout, 1)

        with nc.Block() as block:
            @block.tensor
            def _(pe):
                def project(b, p):
                    wait(pe, q_out, b * PAIRS + p)
                    nc.tensor.matmul(c.ps_s[:, 2, :], WQ[:, p * P:(p + 1) * P], c.XT[:, bass.ds(b * S, S)],
                                     start=True, stop=True).then_inc(proj, 1)

                def score(b, p):
                    wait(pe, q_out, b * PAIRS + p + 1)
                    wait(pe, lessened, b * PAIRS + p)
                    for qt in range(QT):
                        mm = nc.tensor.matmul(c.ps_s[:, qt // 2, (qt % 2) * 2 * KC:(qt % 2 + 1) * 2 * KC],
                                              Q[:, p % 2, qt * P:(qt + 1) * P],
                                              KB[:, p, bass.ds(b, 1), :, :].rearrange("p a e k -> p (a e k)"),
                                              start=True, stop=True)
                    mm.then_inc(scores, 1)

                def turn(b, p):
                    wait(pe, normed, b * PAIRS + p + 1)
                    wait(pe, t_act, b * PAIRS + p)
                    wait(pe, t_dve, b * PAIRS + p)
                    for e in range(2):
                        for qt in range(QT):
                            mm = nc.tensor.transpose(c.ps_t[0:KC, e, qt * P:(qt + 1) * P], PR[:, p % 2, 2 * qt + e, :],
                                                     c.ident[:, :])
                        mm.then_inc(turned, 1)

                def weigh(b, p):
                    wait(pe, t_act, b * PAIRS + p + 1)
                    wait(pe, t_dve, b * PAIRS + p + 1)
                    wait(pe, heads_out, b * PAIRS + p)
                    for e in range(2):
                        h = 2 * p + e
                        mm = nc.tensor.matmul(c.ps_v[e * HD64:(e + 1) * HD64, :], VB[:, h * HD64:(h + 1) * HD64], PT[:, e, :],
                                              start=True, stop=True)
                    mm.then_inc(products, 1)

                def add(b, p):
                    wait(pe, heads_out, b * PAIRS + p + 1)
                    if p == 0:
                        wait(pe, s_ot, b)
                    nc.tensor.matmul(c.ps_f[:, :], WO[:, p, :], CT[:, :], start=(p == 0), stop=(p == PAIRS - 1)).then_inc(added, 1)

                def batch(b):
                    project(b, 0)
                    project(b, 1)
                    score(b, 0)
                    wait(pe, s_vb, b + 1)
                    for p in range(PAIRS):
                        if p + 1 < PAIRS:
                            score(b, p + 1)
                        turn(b, p)
                        if p + 2 < PAIRS:
                            project(b, p + 2)
                        if p:
                            add(b, p - 1)
                        weigh(b, p)
                    add(b, PAIRS - 1)
                first_then_loop(pe, B, batch)

            @block.vector
            def _(dve):
                def lessen(b, p):
                    n = b * PAIRS + p
                    src = c.ps_s[:, 0:2, 0:4 * KC].rearrange("p a (m k) -> p a m k", k=KC)
                    dve.wait_ge(scores, n + 1)
                    nc.vector.reduce_max(M[:, :].rearrange("p (a m) -> p a m", a=2), src, AX.X).then_inc(maxed, 1)
                    dve.wait_ge(maxed, n + 1)
                    if p < 2:
                        wait(dve, exped, b * PAIRS)
                    else:
                        dve.wait_ge(exped, n - 1)
                    nc.vector.tensor_tensor(SC[:, p % 2].rearrange("p (a m) k -> p a m k", a=2), src,
                                            M[:, :].rearrange("p (a m b) -> p a m b", a=2, b=1).broadcast_to([P, 2, 4, KC]),
                                            ALU.subtract).then_inc(lessened, 1)

                def norm(b, p):
                    n = b * PAIRS + p
                    dve.wait_ge(exped, n + 1)
                    nc.vector.reduce_sum(DEN[:, :], PR[:, p % 2], AX.X).then_inc(summed, 1)
                    dve.wait_ge(summed, n + 1)
                    nc.vector.reciprocal(RDEN[:, :], DEN[:, :]).then_inc(inverted, 1)
                    dve.wait_ge(inverted, n + 1)
                    nc.vector.tensor_tensor(PR[:, p % 2], PR[:, p % 2],
                                            RDEN[:, :].rearrange("p (m a) -> p m a", a=1).broadcast_to([P, 2 * QT, KC]),
                                            ALU.mult).then_inc(normed, 1)

                def take(b, p):
                    n = b * PAIRS + p
                    dve.wait_ge(turned, 2 * n + 2)
                    dve.wait_ge(products, n)
                    nc.vector.tensor_copy(PT[0:KC, 1, :], c.ps_t[0:KC, 1, :]).then_inc(t_dve, 1)

                def take_heads(b, p):
                    n = b * PAIRS + p
                    dve.wait_ge(products, n + 1)
                    dve.wait_ge(added, n)
                    nc.vector.tensor_copy(CT[:, :], c.ps_v[:, :]).then_inc(heads_out, 1)

                def batch(b):
                    wait(dve, products, b * PAIRS)
                    nc.vector.tensor_copy(VB[:, :], VA[:, bass.ds(b, 1), :].rearrange("p a n -> p (a n)")).then_inc(s_vb, 1)
                    lessen(b, 0)
                    norm(b, 0)
                    for p in range(PAIRS):
                        if p + 1 < PAIRS:
                            lessen(b, p + 1)
                        take(b, p)
                        if p + 1 < PAIRS:
                            norm(b, p + 1)
                        take_heads(b, p)
                first_then_loop(dve, B, batch)

            @block.scalar
            def _(act):
                def exp(b, p):
                    n = b * PAIRS + p
                    act.wait_ge(lessened, n + 1)
                    if p < 2:
                        wait(act, turned, 2 * b * PAIRS)
                    else:
                        act.wait_ge(turned, 2 * (n - 1))
                    nc.scalar.activation(PR[:, p % 2], SC[:, p % 2], ACT.Exp).then_inc(exped, 1)

                def queries_out(b, p):
                    n = b * PAIRS + p
                    act.wait_ge(proj, n + 1)
                    if p < 2:
                        wait(act, scores, b * PAIRS)
                    else:
                        act.wait_ge(scores, n - 1)
                    nc.scalar.activation(Q[:, p % 2, :], c.ps_s[:, 2, :], ACT.Identity, bias=BQ[:, p:p + 1],
                                         scale=ISQ64).then_inc(q_out, 1)

                def batch(b):
                    queries_out(b, 0)
                    queries_out(b, 1)
                    exp(b, 0)
                    for p in range(PAIRS):
                        if p + 1 < PAIRS:
                            exp(b, p + 1)
                        act.wait_ge(turned, 2 * (b * PAIRS + p) + 1)
                        wait(act, products, b * PAIRS + p)
                        nc.scalar.activation(PT[0:KC, 0, :], c.ps_t[0:KC, 0, :], ACT.Copy).then_inc(t_act, 1)
                        if p + 2 < PAIRS:
                            queries_out(b, p + 2)
                    wait(act, added, b * PAIRS + PAIRS)
                    nc.scalar.activation(OT[:, bass.ds(b, 1), :], c.ps_f[:, :], ACT.Identity, bias=BO[:, 0:1]).then_inc(s_ot, 1)
                first_then_loop(act, B, batch)


def gates(c, tag, wg, GATE):
    nc = c.nc
    with ExitStack() as own:
        WG = c.sb(f"{tag}_WG", [P, NE], F32, own)
        L = c.sb(f"{tag}_L", [P, NT, NE], F32, own)
        E = c.sb(f"{tag}_E", [P, NT, NE], F32, own)
        C1 = c.sb(f"{tag}_C1", [P, NT, NE, NE], F32, own)
        C2 = c.sb(f"{tag}_C2", [P, NT, NE, NE], F32, own)
        LOW = c.sb(f"{tag}_LOW", [P, NE, NE], F32, own)
        RK = c.sb(f"{tag}_RK", [P, NT, NE], F32, own)
        M = c.sb(f"{tag}_GM", [P, NT], F32, own)
        s_w, s_low, s_logits, s_chain, s_exp = (c.sem(f"{tag}_g{n}") for n in ("w", "low", "logits", "chain", "exp"))
        with nc.Block() as block:
            @block.sync
            def _(sp):
                sp.dma_start(WG[:, :], wg).then_inc(s_w, 16)

            @block.gpsimd
            def _(pool):
                nc.gpsimd.memset(LOW[:, :, :], 1.0).then_inc(s_low, 1)
                pool.wait_ge(s_low, 1)
                nc.gpsimd.affine_select(out=LOW[:, :, :], in_=LOW[:, :, :], compare_op=ALU.is_gt, fill=0.0, base=0,
                                        pattern=[[1, NE], [-1, NE]], channel_multiplier=0).then_inc(s_low, 1)

            @block.tensor
            def _(pe):
                pe.wait_ge(s_w, 16)
                for n in range(NT):
                    last = nc.tensor.matmul(c.ps_s[:, 0, n * NE:(n + 1) * NE], c.XT[:, n * P:(n + 1) * P], WG[:, :],
                                            start=True, stop=True)
                last.then_inc(s_logits, 1)

            @block.scalar
            def _(act):
                act.wait_ge(s_chain, 3)
                nc.scalar.activation(E[:, :, :], E[:, :, :], ACT.Exp).then_inc(s_exp, 1)

            @block.vector
            def _(dve):
                chain = Chain(s_chain)
                if GATE.shape[2] > NE:
                    nc.vector.memset(GATE[:, :, NE:], 1.0)
                dve.wait_ge(s_logits, 1)
                chain.inc(nc.vector.tensor_copy(L[:, :, :], c.ps_s[:, 0, 0:NT * NE].rearrange("p (n e) -> p n e", e=NE)))
                chain.wait(dve)
                chain.inc(nc.vector.reduce_max(M[:, :], L[:, :, :], AX.X))
                chain.wait(dve)
                by_tile = M[:, :].rearrange("p (n a) -> p n a", a=1).broadcast_to([P, NT, NE])
                chain.inc(nc.vector.tensor_tensor(E[:, :, :], L[:, :, :], by_tile, ALU.subtract))
                of_e = L[:, :, :].rearrange("p n (e a) -> p n e a", a=1).broadcast_to([P, NT, NE, NE])
                of_j = L[:, :, :].rearrange("p n (a j) -> p n a j", a=1).broadcast_to([P, NT, NE, NE])
                chain.inc(nc.vector.tensor_tensor(C1[:, :, :, :], of_j, of_e, ALU.is_gt))
                chain.inc(nc.vector.tensor_tensor(C2[:, :, :, :], of_j, of_e, ALU.is_equal))
                chain.wait(dve)
                dve.wait_ge(s_low, 2)
                c2 = C2[:, :, :, :].rearrange("p n e j -> p n (e j)")
                chain.inc(nc.vector.tensor_tensor(
                    c2, c2, LOW[:, :, :].rearrange("p (a e) j -> p a (e j)", a=1).broadcast_to([P, NT, NE * NE]), ALU.mult))
                chain.wait(dve)
                chain.inc(nc.vector.tensor_tensor(C1[:, :, :, :], C1[:, :, :, :], C2[:, :, :, :], ALU.add))
                chain.wait(dve)
                chain.inc(nc.vector.reduce_sum(RK[:, :, :], C1[:, :, :, :], AX.X))
                chain.wait(dve)
                dve.wait_ge(s_exp, 1)
                gate = GATE[:, :, 0:NE]
                chain.inc(nc.vector.scalar_tensor_tensor(gate, RK[:, :, :], 2.0, E[:, :, :], ALU.is_lt, ALU.mult))
                chain.wait(dve)
                chain.inc(nc.vector.reduce_sum(M[:, :], gate, AX.X))
                chain.wait(dve)
                chain.inc(nc.vector.reciprocal(M[:, :], M[:, :]))
                chain.wait(dve)
                nc.vector.tensor_tensor(gate, gate, by_tile, ALU.mult)


def experts(c, tag, GATE, w1, w2, w3=None, b1=None, b2=None, shared=None):
    nc = c.nc
    hid = w1.shape[2]
    CH = hid // P
    gated = w3 is not None
    total = NE + (shared is not None)
    with ExitStack() as own:
        W1 = [c.sb(f"{tag}_W1{i}", [P, hid], F32, own) for i in range(2)]
        W3 = [c.sb(f"{tag}_W3{i}", [P, hid], F32, own) for i in range(2)] if gated else None
        W2 = [c.sb(f"{tag}_W2{i}", [P, CH, P], F32, own) for i in range(2)]
        HT = c.sb(f"{tag}_HT", [P, 2, CH, S], F32, own)
        GT = c.sb(f"{tag}_GT", [P, 2, CH, S], F32, own) if gated else None
        B1 = c.sb(f"{tag}_B1", [P, NE, CH], F32, own) if not gated else None
        BE = c.sb(f"{tag}_BE", [P, 2, CH], F32, own) if not gated else None
        B2 = c.sb(f"{tag}_B2", [P, NE, P], F32, own) if not gated else None
        s_w = [c.sem(f"{tag}_w{i}") for i in range(2)]
        s_b, s_be, s_first, s_act, s_hidden, s_second, s_added = (
            c.sem(f"{tag}_{n}") for n in ("bias", "be", "first", "act", "hidden", "second", "added"))
        N_W = 16 * (3 if gated else 2)
        ADDS = QT if gated else 2 * QT
        sources = (w1, w2) + ((w3,) if gated else ())

        def load(sp, e, i, shared_too=False):
            if shared_too:
                srcs = ((W1[i][:, :], shared[0]), (W3[i][:, :], shared[1]),
                        (W2[i][:, :, :], shared[2].rearrange("(c p) n -> p c n", p=P)))
            else:
                srcs = ((W1[i][:, :], w1[e]), (W2[i][:, :, :], w2[e].rearrange("(c p) n -> p c n", p=P)))
                if gated:
                    srcs += ((W3[i][:, :], w3[e]),)
            for dst, src in srcs:
                sp.dma_start(dst, src).then_inc(s_w[i], 16)

        def run(engine, one):
            def pair(t, first, last):
                for i in range(2):
                    one(t, i, first and i == 0, last and i == 1 and total % 2 == 0)
            if total % 2:
                pair(0, True, False)
                with engine.Fori(1, total // 2) as t:
                    pair(t, False, False)
                one(total // 2, 0, False, True)
            else:
                peeled(engine, total // 2, pair)

        with nc.Block() as block:
            @block.sync
            def _(sp):
                if not gated:
                    sp.dma_start(B1[:, :, :], b1.rearrange("e (c p) -> p e c", p=P), allow_slow_non_contiguous=True).then_inc(s_b, 16)
                    sp.dma_start(B2[:, :, :].rearrange("p e n -> p (e n)"), row(b2.rearrange("e n -> (e n)"))).then_inc(s_b, 16)
                load(sp, 0, 0)
                load(sp, 1, 1)
                for e in range(2, NE):
                    sp.wait_ge(s_second, (e - 1) * B)
                    sp.wait_ge(s_w[e % 2], e // 2 * N_W)
                    load(sp, e, e % 2)
                if shared is not None:
                    sp.wait_ge(s_second, (NE - 1) * B)
                    sp.wait_ge(s_w[0], NE // 2 * N_W)
                    load(sp, None, 0, True)

            @block.tensor
            def _(pe):
                def first_products(t, i, b, first):
                    k = (2 * t + i) * B + b
                    if b == 0:
                        pe.wait_ge(s_w[i], (t + 1) * N_W)
                    for ch in range(2 * CH if gated else CH):
                        if not first:
                            if gated and ch >= CH:
                                pe.wait_ge(s_hidden, (k - 1) * CH + ch - CH + 1)
                            else:
                                pe.wait_ge(s_act, (k - 1) * CH + ch + 1)
                        W = W3[i] if gated and ch >= CH else W1[i]
                        nc.tensor.matmul(c.ps_s[:, ch, :], W[:, (ch % CH) * P:(ch % CH + 1) * P], c.XT[:, b * S:(b + 1) * S],
                                         start=True, stop=True).then_inc(s_first, 1)

                def second_products(t, i, b, first):
                    k = (2 * t + i) * B + b
                    pe.wait_ge(s_hidden if gated else s_act, (k + 1) * CH)
                    if not (first and b < 2):
                        pe.wait_ge(s_added, (k - 1) * ADDS)
                    for q in range(QT):
                        for ch in range(CH):
                            mm = nc.tensor.matmul(c.ps_t[:, b % 2, q * P:(q + 1) * P], HT[:, b % 2, ch, q * P:(q + 1) * P],
                                                  W2[i][:, ch, :], start=(ch == 0), stop=(ch == CH - 1))
                    mm.then_inc(s_second, 1)

                def one(t, i, first, last):
                    for b in range(B):
                        if b + 1 < B:
                            first_products(t, i, b + 1, False)
                        elif not last:
                            first_products(t + i, 1 - i, 0, False)
                        second_products(t, i, b, first)
                first_products(0, 0, 0, True)
                run(pe, one)

            @block.scalar
            def _(act):
                if not gated:
                    act.wait_ge(s_b, 32)

                def one(t, i, first, last):
                    if not gated:
                        nc.scalar.activation(BE[:, i, :], B1[:, bass.ds(2 * t + i, 1), :].rearrange("p a c -> p (a c)"),
                                             ACT.Copy).then_inc(s_be, 1)
                        act.wait_ge(s_be, 2 * t + i + 1)
                    for b in range(B):
                        k = (2 * t + i) * B + b
                        for ch in range(CH):
                            act.wait_ge(s_first, k * (2 * CH if gated else CH) + ch + 1)
                            if not (first and b < 2):
                                if gated:
                                    act.wait_ge(s_hidden, (k - 2) * CH + ch + 1)
                                else:
                                    act.wait_ge(s_second, k - 1)
                            if gated:
                                nc.scalar.activation(GT[:, b % 2, ch, :], c.ps_s[:, ch, :], ACT.Silu).then_inc(s_act, 1)
                            else:
                                nc.scalar.activation(HT[:, b % 2, ch, :], c.ps_s[:, ch, :], ACT.Gelu_apprx_tanh,
                                                     bias=BE[:, i, ch:ch + 1]).then_inc(s_act, 1)
                run(act, one)

            @block.vector
            def _(dve):
                if not gated:
                    dve.wait_ge(s_b, 32)

                def hidden(t, i, b, first):
                    k = (2 * t + i) * B + b
                    for ch in range(CH):
                        dve.wait_ge(s_first, k * 2 * CH + CH + ch + 1)
                        dve.wait_ge(s_act, k * CH + ch + 1)
                        if not (first and b < 2):
                            dve.wait_ge(s_second, k - 1)
                        nc.vector.tensor_tensor(HT[:, b % 2, ch, :], GT[:, b % 2, ch, :], c.ps_s[:, CH + ch, :],
                                                ALU.mult).then_inc(s_hidden, 1)

                def add(t, i, b, first):
                    k = (2 * t + i) * B + b
                    e = 2 * t + i
                    if not gated:
                        if not (first and b == 0):
                            dve.wait_ge(s_added, k * ADDS)
                        for q in range(QT):
                            x = c.X[:, b * QT + q, :]
                            gate = GATE[:, b * QT + q, bass.ds(e, 1)]
                            nc.vector.scalar_tensor_tensor(x, B2[:, bass.ds(e, 1), :].rearrange("p a n -> p (a n)"), gate, x,
                                                           ALU.mult, ALU.add).then_inc(s_added, 1)
                        dve.wait_ge(s_added, k * ADDS + QT)
                    elif not (first and b == 0):
                        dve.wait_ge(s_added, k * ADDS)
                    dve.wait_ge(s_second, k + 1)
                    for q in range(QT):
                        x = c.X[:, b * QT + q, :]
                        gate = GATE[:, b * QT + q, bass.ds(e, 1)]
                        nc.vector.scalar_tensor_tensor(x, c.ps_t[:, b % 2, q * P:(q + 1) * P], gate, x,
                                                       ALU.mult, ALU.add).then_inc(s_added, 1)

                def one(t, i, first, last):
                    for b in range(B):
                        if gated:
                            if b + 1 < B:
                                hidden(t, i, b + 1, first)
                            elif not last:
                                hidden(t + i, 1 - i, 0, False)
                        add(t, i, b, first)
                if gated:
                    hidden(0, 0, 0, True)
                run(dve, one)


def decoder(nc, a, out):
    scratch = nc.dram_tensor("split_parts", (B, 2, P, NPART, S), BF16, kind="Internal").ap()
    with ExitStack() as ctx:
        c = Core(nc, ctx)
        setup(c, a["x"], a["ctx_1024"])

        with ExitStack() as narrow:
            stacks(c, narrow)
            narrow_self_attention(c, "a", a["L0_attn_Wq"], a["L0_attn_Wk"], a["L0_attn_Wv"], scratch, rel=a["L0_attn_rel_emb"])
            finish(c, "a", "ctx", wo=a["L0_attn_Wo"], bias=a["L0_attn_bo"])
            narrow_cross_attention(c, "b", a["L0_xattn_Wq"], a["L0_xattn_bq"], a["L0_xattn_Wk"], a["L0_xattn_bk"],
                                   a["L0_xattn_Wv"], a["L0_xattn_bv"], scratch)
            finish(c, "b", "ctx", wo=a["L0_xattn_Wo"], bias=a["L0_xattn_bo"], pre=(a["L0_ffn_ln1_w"], a["L0_ffn_ln1_b"]))
            q, k, v = (slice(i * P, (i + 1) * P) for i in range(3))
            w, b = a["L0_ffn_w_qkv"], a["L0_ffn_b_qkv"]
            narrow_self_attention(c, "c", w[:, q], w[:, k], w[:, v], scratch, b[q], b[k], b[v], qscale=ISQ8)
            finish(c, "c", "ctx", wo=a["L0_ffn_w_o"], bias=a["L0_ffn_b_o"], mode="inner",
                   pre=(a["L0_ffn_ln2_w"], a["L0_ffn_ln2_b"]))
        with ExitStack() as own:
            GATE = c.sb("GATE0", [P, NT, NE], F32, own)
            gates(c, "f", a["L0_ffn_w_gate"], GATE)
            experts(c, "f", GATE, a["L0_ffn_w1"], a["L0_ffn_w2"], b1=a["L0_ffn_b1"], b2=a["L0_ffn_b2"])
        finish(c, "f", "x", pre=(a["L1_attn_ln_gamma"], a["L1_attn_ln_beta"]))
        c.recycle_semaphores()
        with ExitStack() as own:
            OT = c.sb("OT_d", [P, B, S], F32, own)
            wide_self_attention(c, "d", a["L1_attn_Wq"], a["L1_attn_Wk"], a["L1_attn_Wv"], a["L1_attn_Wo"], OT)
            finish(c, "d", "dm", OT=OT)
        with ExitStack() as own:
            OT = c.sb("OT_e", [P, B, S], F32, own)
            wide_cross_attention(c, "e", *(a[f"L1_xattn_{n}"] for n in ("Wq", "bq", "Wk", "bk", "Wv", "bv", "Wo", "bo")), OT)
            finish(c, "e", "dm", OT=OT)
        with ExitStack() as own:
            GATE = c.sb("GATE1", [P, NT, NE + 1], F32, own)
            gates(c, "g", a["L1_ffn_w_router"], GATE)
            experts(c, "g", GATE, a["L1_ffn_w1"], a["L1_ffn_w2"], w3=a["L1_ffn_w3"],
                    shared=(a["L1_ffn_sw1"], a["L1_ffn_sw3"], a["L1_ffn_sw2"]))
        finish(c, "g", "x", out=out)


_NAMES = ["x", "ctx_1024"] \
    + [f"L0_attn_{n}" for n in ("Wq", "Wk", "Wv", "Wo", "bo", "rel_emb")] \
    + [f"L0_xattn_{n}" for n in ("Wq", "bq", "Wk", "bk", "Wv", "bv", "Wo", "bo")] \
    + [f"L0_ffn_{n}" for n in ("ln1_w", "ln1_b", "ln2_w", "ln2_b", "w_qkv", "b_qkv", "w_o", "b_o", "w_gate",
                               "w1", "b1", "w2", "b2")] \
    + [f"L1_attn_{n}" for n in ("ln_gamma", "ln_beta", "Wq", "Wk", "Wv", "Wo")] \
    + [f"L1_xattn_{n}" for n in ("Wq", "bq", "Wk", "bk", "Wv", "bv", "Wo", "bo")] \
    + [f"L1_ffn_{n}" for n in ("w_router", "w1", "w3", "w2", "sw1", "sw3", "sw2")]


def kernel(**inputs):
    import numpy as np
    import concourse.bacc as bacc
    from concourse.bass_utils import run_bass_kernel_spmd

    nc = bacc.Bacc("TRN2", target_bir_lowering=False, num_devices=1)
    arrays, aps = {}, {}
    for name in _NAMES:
        array = np.ascontiguousarray(inputs[name])
        arrays[f"in_{name}"] = array
        aps[name] = nc.dram_tensor(f"in_{name}", array.shape, mybir.dt.from_np(array.dtype), kind="ExternalInput").ap()
    out = nc.dram_tensor("out", (B, S, P), F32, kind="ExternalOutput").ap()
    decoder(nc, aps, out)
    result = run_bass_kernel_spmd(nc, [arrays], core_ids=[0])
    return result.results[0]["out"]
```

```python
import concourse.bass as bass
from concourse import mybir
from contextlib import ExitStack
from typing import Callable, NamedTuple

F32 = mybir.dt.float32
BF16 = mybir.dt.bfloat16
ALU = mybir.AluOpType
ACT = mybir.ActivationFunctionType
AX = mybir.AxisListType

P = 128
B = 4
S = 512
QT = S // P
NT = B * QT
TOK = B * S
KC = 77
H = 16
HD8 = P // H
HD64 = 64
PAIRS = H // 2
GH = 4
GROUPS = H // GH
STEPS = B * GROUPS
CW = P // GH
NPART = 3
SROWS = 96
NE = 8
HID0 = 512
HID1 = 256
CLIP = 16
EPS = 1e-5
MASKED = -1e30
LOWEST = -3e38
ISQ8 = float(HD8) ** -0.5
ISQ64 = float(HD64) ** -0.5


class Chain:

    def __init__(self, sem, base=0):
        self.sem, self.base, self.n = sem, base, 0

    def inc(self, instruction):
        instruction.then_inc(self.sem, 1)
        self.n += 1

    def value(self):
        return self.base + self.n

    def wait(self, engine):
        engine.wait_ge(self.sem, self.base + self.n)


def peeled(engine, count, body):
    body(0, True, False)
    with engine.Fori(1, count - 1) as t:
        body(t, False, False)
    body(count - 1, False, True)


def first_then_loop(engine, count, body):
    body(0)
    with engine.Fori(1, count) as t:
        body(t)


def steps(engine, step):
    step(0, 0, 0)
    step(1, 1, 1)
    with engine.Fori(2, STEPS - 2, 2) as t:
        step(t, 0, None)
        step(t + 1, 1, None)
    step(STEPS - 2, 0, None)
    step(STEPS - 1, 1, -1)


def wait(engine, sem, value):
    if not isinstance(value, int) or value > 0:
        engine.wait_ge(sem, value)


class Core:

    def __init__(self, nc, ctx):
        self.nc, self.ctx, self.sems = nc, ctx, []
        self.X = self.sb("X", [P, NT, P], F32)
        self.XT = self.sb("XT", [P, TOK], F32)
        self.CTX = self.sb("CTX", [P, NT, P], F32)
        self.CTT = self.sb("CTT", [P, B * KC], F32)
        self.ident = self.sb("ident", [P, P], F32)
        self.VG = self.sb("VG", [P, QT, GH, CW], F32)
        self.neghalf = self.sb("neghalf", [P, 4], F32)
        self.ps_s = ctx.enter_context(nc.psum_tensor("ps_s", [P, 4, 512], F32))
        self.ps_t = ctx.enter_context(nc.psum_tensor("ps_t", [P, 2, 512], F32))
        self.ps_v = ctx.enter_context(nc.psum_tensor("ps_v", [P, 512], F32))
        self.ps_f = ctx.enter_context(nc.psum_tensor("ps_f", [P, 512], F32))

    def sb(self, name, shape, dt, ctx=None):
        return (ctx or self.ctx).enter_context(self.nc.sbuf_tensor(name, shape, dt))

    def sem(self, name):
        self.sems.append(self.nc.alloc_semaphore(name=name))
        return self.sems[-1]

    def recycle_semaphores(self):
        self.nc.clear_and_free_semaphores(self.sems)
        self.nc.all_engine_barrier()
        self.sems = []


def row(ap, parts=P):
    n = ap.shape[0]
    return ap.rearrange("(a n) -> a n", a=1).broadcast_to([parts, n])


def col(ap):
    return ap.rearrange("(p a) -> p a", a=1)


def setup(c, x, ctx_in):
    nc = c.nc
    with ExitStack() as own:
        CR = c.sb("CR", [KC, B, P], F32, own)
        loaded, made, turned, copied = (c.sem(f"setup_{n}") for n in ("loaded", "made", "turned", "copied"))
        with nc.Block() as block:
            @block.sync
            def _(sp):
                for b in range(B):
                    sp.dma_start(c.X[:, b * QT:(b + 1) * QT, :],
                                 x[b].rearrange("(n p) d -> p n d", p=P)).then_inc(loaded, 16)
                sp.dma_start(CR[:, :, :], ctx_in.rearrange("b k d -> k b d")).then_inc(loaded, 16)

            @block.gpsimd
            def _(pool):
                nc.gpsimd.memset(c.ident[:, :], 0.0).then_inc(made, 1)
                pool.wait_ge(made, 1)
                nc.gpsimd.affine_select(out=c.ident[:, :], in_=c.ident[:, :], compare_op=ALU.not_equal, fill=1.0,
                                        base=0, pattern=[[-1, P]], channel_multiplier=1).then_inc(made, 1)
                nc.gpsimd.memset(c.VG[:, :, :, :], 1.0)
                nc.gpsimd.memset(c.neghalf[:, :], -0.5).then_inc(made, 1)

            @block.tensor
            def _(pe):
                pe.wait_ge(made, 2)
                pe.wait_ge(loaded, 16 * (B + 1))
                for b in range(B):
                    for i in range(QT):
                        last = nc.tensor.transpose(c.ps_s[:, b, i * P:(i + 1) * P], c.X[:, b * QT + i, :], c.ident[:, :])
                    last.then_inc(turned, 1)
                for b in range(B):
                    last = nc.tensor.transpose(c.ps_t[:, 0, b * KC:(b + 1) * KC], CR[:, b, :], c.ident[0:KC, 0:KC])
                last.then_inc(turned, 1)

            @block.vector
            def _(dve):
                for b in range(B):
                    dve.wait_ge(turned, b + 1)
                    nc.vector.tensor_copy(c.XT[:, b * S:(b + 1) * S], c.ps_s[:, b, :])
                dve.wait_ge(turned, B + 1)
                nc.vector.tensor_copy(c.CTT[:, :], c.ps_t[:, 0, 0:B * KC])


SPLIT_OPS = 5
STORES = 4


def split_parts(nc, dve, chain, full, part):
    chain.inc(nc.vector.tensor_copy(part(0), full))
    chain.wait(dve)
    for i in (1, 2):
        chain.inc(nc.vector.tensor_tensor(full, full, part(i - 1), ALU.subtract))
        chain.wait(dve)
        chain.inc(nc.vector.tensor_copy(part(i), full))
        chain.wait(dve)


def stacks(c, ctx):
    c.QX = c.sb("QX", [P, 2 * H, S], BF16, ctx)
    c.KX = c.sb("KX", [P, 2 * H, S], BF16, ctx)


def zero_rows(c, engine, stack, s_rows):
    nc = c.nc
    for slot in range(2):
        rows = stack[64:P, slot * H:(slot + 1) * H, :]
        if stack is c.QX:
            nc.gpsimd.memset(rows, 0.0).then_inc(s_rows, 1)
            engine.wait_ge(s_rows, slot + 1)
        else:
            some = c.neghalf[64:P, 0:1].rearrange("p (a b) -> p a b", a=1).broadcast_to([P - 64, H, S])
            nc.scalar.activation(rows, some, ACT.Copy, scale=0.0).then_inc(s_rows, 1)


class Beside(NamedTuple):
    load: Callable
    pool: Callable
    tensor: Callable
    vector: Callable
    scalar: Callable = None
    s_rows: tuple = None


def narrow_projections(c, tag, own, scratch, QX, KX, s_qx, wq, wk, wv, bq=None, bk=None, bv=None, qscale=1.0,
                       beside=None):
    nc = c.nc
    W = c.sb(f"{tag}_W", [P, 3, P], F32, own)
    BQK = c.sb(f"{tag}_BQK", [P, 2], F32, own)
    BV = c.sb(f"{tag}_BV", [P, P], F32, own)
    FULL = c.sb(f"{tag}_FULL", [P, 2, S], F32, own)
    PARTS = c.sb(f"{tag}_PARTS", [P, STORES, NPART, S], BF16, own)
    kinds = [0] if wk is None else [0, 1]
    items = [(b, w) for b in range(B) for w in kinds]
    s_w, s_bias, s_proj, s_full, s_split, s_v, s_vn = (
        c.sem(f"{tag}_p{n}") for n in ("w", "bias", "proj", "full", "split", "v", "vn"))
    s_store = [c.sem(f"{tag}_store{i}") for i in range(STORES)]
    weights = [w for w in (wq, wk, wv) if w is not None]
    biases = [w for w in (bq, bk, bv) if w is not None]

    with nc.Block() as block:
        @block.sync
        def _(sp):
            for i, w in enumerate((wq, wk, wv)):
                if w is not None:
                    sp.dma_start(W[:, i, :], w).then_inc(s_w, 16)
            for i, v in enumerate((bq, bk)):
                if v is not None:
                    sp.dma_start(BQK[:, i:i + 1], col(v)).then_inc(s_w, 16)
            if bv is not None:
                sp.dma_start(BV[:, :], row(bv)).then_inc(s_w, 16)
            if beside:
                beside.load(sp)
            for i, (b, w) in enumerate(items):
                sp.wait_ge(s_split, SPLIT_OPS * (i + 1))
                sp.dma_start(scratch[b, w], PARTS[:, i % STORES]).then_inc(s_store[i % STORES], 16)
                if w == kinds[-1] and b == 1:
                    for k in range(len(kinds)):
                        sp.wait_ge(s_store[k], 16)
                    if beside and beside.s_rows:
                        for rows in beside.s_rows:
                            sp.wait_ge(rows, 2)
                    load_stacks(nc, sp, scratch, 0, QX, KX, s_qx)
            for i in range(STORES):
                sp.wait_ge(s_store[i], 16 * (len(items) // STORES))

        @block.gpsimd
        def _(pool):
            if beside:
                beside.pool(pool)

        @block.tensor
        def _(pe):
            pe.wait_ge(s_w, 16 * (len(weights) + len(biases)))
            for i, (b, w) in enumerate(items):
                if i >= 2:
                    pe.wait_ge(s_full, i - 1)
                nc.tensor.matmul(c.ps_s[:, i % 2, :], W[:, w, :], c.XT[:, b * S:(b + 1) * S],
                                 start=True, stop=True).then_inc(s_proj, 1)
                if w == 0 and wv is not None:
                    if b >= 2:
                        pe.wait_ge(s_vn, b - 1)
                    for m in range(QT):
                        n = b * QT + m
                        last = nc.tensor.matmul(c.ps_t[:, b % 2, m * P:(m + 1) * P], c.XT[:, n * P:(n + 1) * P],
                                                W[:, 2, :], start=True, stop=True)
                    last.then_inc(s_v, 1)
            if beside:
                beside.tensor(pe)

        @block.scalar
        def _(act):
            if beside and beside.scalar:
                beside.scalar(act)
            if bq is not None:
                act.wait_ge(s_bias, 1)
            for i, (b, w) in enumerate(items):
                act.wait_ge(s_proj, i + 1)
                if i >= 2:
                    act.wait_ge(s_split, SPLIT_OPS * (i - 1))
                scale = qscale if w == 0 else 1.0
                if (bq, bk)[w] is None:
                    ins = nc.scalar.activation(FULL[:, i % 2, :], c.ps_s[:, i % 2, :], ACT.Copy, scale=scale)
                else:
                    ins = nc.scalar.activation(FULL[:, i % 2, :], c.ps_s[:, i % 2, :], ACT.Identity,
                                               bias=BQK[:, w:w + 1], scale=scale)
                ins.then_inc(s_full, 1)

        @block.vector
        def _(dve):
            if beside and beside.scalar:
                beside.vector(dve)
            chain = Chain(s_split)
            dve.wait_ge(s_w, 16 * (len(weights) + len(biases)))
            if bq is not None:
                nc.vector.tensor_scalar(BQK[:, 0:1], BQK[:, 0:1], qscale, None, ALU.mult).then_inc(s_bias, 1)
            for i, (b, w) in enumerate(items):
                dve.wait_ge(s_full, i + 1)
                if i >= STORES:
                    dve.wait_ge(s_store[i % STORES], 16 * (i // STORES))
                part = lambda j: PARTS[:, i % STORES, j, :]
                split_parts(nc, dve, chain, FULL[:, i % 2, :], part)
                if w == 0 and wv is not None:
                    dve.wait_ge(s_v, b + 1)
                    dst = c.VN[:, b * QT:(b + 1) * QT, :]
                    src = c.ps_t[:, b % 2, :].rearrange("p (m d) -> p m d", m=QT)
                    if bv is None:
                        nc.vector.tensor_copy(dst, src).then_inc(s_vn, 1)
                    else:
                        nc.vector.tensor_tensor(dst, src, BV[:, :].rearrange("p (a d) -> p a d", a=1).broadcast_to([P, QT, P]),
                                                ALU.add).then_inc(s_vn, 1)
            if beside and not beside.scalar:
                beside.vector(dve)


STACK_LOADS = NPART * NPART


def load_stacks(nc, sp, scratch, b, QX, KX, sem):
    slot = slice((b % 2) * H, (b % 2 + 1) * H)
    for i in range(NPART):
        for j in range(NPART):
            r = HD8 * (NPART * i + j)
            for w, part, stack in ((0, i, QX), (1, j, KX)):
                if stack is not None:
                    sp.dma_start(stack[r:r + HD8, slot, :],
                                 scratch[b, w, :, part, :].rearrange("(h d) t -> d h t", d=HD8)).then_inc(sem, 16)


def gather_values(c, pool, t, first, s_pv, s_vg, cross_values=None, per_group=1):
    nc = c.nc
    if not first:
        pool.wait_ge(s_pv, per_group * t)
    if cross_values is None:
        for kt in range(QT):
            src = c.VN[:, bass.ds((t // GROUPS) * QT + kt, 1), bass.ds((t % GROUPS) * GH * HD8, GH * HD8)]
            last = nc.gpsimd.tensor_copy(c.VG[:, kt, :, 0:HD8], src.rearrange("p a (h d) -> p (a h) d", d=HD8))
    else:
        last = nc.gpsimd.tensor_copy(c.VG[0:SROWS, 0, 0:1, 0:HD8], cross_values[:, bass.ds(t // GROUPS, 1), :])
    last.then_inc(s_vg, 1)


def group_end_act(c, act, t, s_pv, s_ct, s_ftr, CT4, first=False, per_group=1):
    act.wait_ge(s_pv, per_group * (t + 1))
    if not first:
        act.wait_ge(s_ftr, t)
    c.nc.scalar.activation(CT4[:, :], c.ps_v[:, :], ACT.Copy).then_inc(s_ct, 1)


def group_end_pe(c, pe, t, s_ct, s_ctx, s_ftr, CT4, first=False):
    pe.wait_ge(s_ct, t + 1)
    if not first:
        pe.wait_ge(s_ctx, t)
    for i in range(QT):
        last = c.nc.tensor.transpose(c.ps_f[:, i * P:(i + 1) * P], CT4[:, i * P:(i + 1) * P], c.ident[:, :])
    last.then_inc(s_ftr, 1)


def group_end_dve(c, dve, t, s_ftr, s_rden, s_ctx, RDEN):
    nc = c.nc
    dve.wait_ge(s_ftr, t + 1)
    sums = c.ps_f[:, :].rearrange("p (q h w) -> p q h w", q=QT, h=GH)
    nc.vector.reciprocal(RDEN[:, :, :], sums[:, :, :, HD8]).then_inc(s_rden, 1)
    dve.wait_ge(s_rden, t + 1)
    out = c.CTX[:, bass.ds((t // GROUPS) * QT, QT), bass.ds((t % GROUPS) * GH * HD8, GH * HD8)]
    nc.vector.tensor_tensor(out.rearrange("p q (h d) -> p q h d", d=HD8), sums[:, :, :, 0:HD8],
                            RDEN[:, :, :].rearrange("p q (h a) -> p q h a", a=1).broadcast_to([P, QT, GH, HD8]),
                            ALU.mult).then_inc(s_ctx, 1)


def narrow_full_attention(c, tag, own, QX, KX, scratch, s_qx):
    nc = c.nc
    NM = c.sb(f"{tag}_NM", [P, QT, GH], F32, own)
    MP = c.sb(f"{tag}_MP", [P, QT, NPART, GH], BF16, own)
    MX = c.sb(f"{tag}_MX", [GH * NPART, S], BF16, own)
    IB = c.sb(f"{tag}_IB", [P, P], BF16, own)
    PT = c.sb(f"{tag}_PT", [P, 2, GH, 2, S], F32, own)
    CT4 = c.sb(f"{tag}_CT4", [P, S], F32, own)
    RDEN = c.sb(f"{tag}_RDEN", [P, QT, GH], F32, own)
    (scores, maxed, parted, mturned, s_mx, s_mload, s_ib, st, exped, products, s_vg, s_ct, s_ftr, s_rden, s_ctx) = (
        c.sem(f"{tag}_{n}") for n in ("scores", "maxed", "parted", "mturned", "mx", "mload", "ib", "st", "exped",
                                      "products", "vg", "ct", "ftr", "rden", "ctx"))
    NF = c.sb(f"{tag}_NF", [P, QT, GH], F32, own)
    PART_OPS = SPLIT_OPS + 1
    QUARTERS = ((), (0,), (1,), (2, 3))
    AHEAD = 2
    TILES = GH * QT

    def slot(u):
        return (u % (2 * GROUPS)) * GH

    def score(pe, u, i, first):
        n = u * TILES + i
        if i == 0:
            pe.wait_ge(s_qx, (u // GROUPS + 1) * 2 * STACK_LOADS * 16)
        if not (first and i < 2):
            pe.wait_ge(maxed, n - 1)
        qt = i % QT
        head = slot(u) + i // QT
        nc.tensor.matmul(c.ps_t[:, i % 2, :], QX[0:SROWS, bass.ds(head, 1), qt * P:(qt + 1) * P],
                         KX[0:SROWS, bass.ds(head, 1), :], start=True, stop=True).then_inc(scores, 1)

    def turn_maxima(pe, u, early=False):
        pe.wait_ge(parted, PART_OPS * (u + 1))
        if not early:
            pe.wait_ge(s_ctx, u - 2)
        for qt in range(QT):
            mm = nc.tensor.matmul(c.ps_f[0:GH * NPART, qt * P:(qt + 1) * P], MP[:, qt, :, :].rearrange("p i h -> p (i h)"),
                                  IB[:, :], start=True, stop=True)
        mm.then_inc(mturned, 1)

    def score_by_key(pe, t, half, j, first):
        m = (2 * t + half) * GH + j
        if half == 0 and j == 0:
            pe.wait_ge(s_mload, NPART * 16 * (t + 1))
        if not (first and half == 0 and j < 2):
            pe.wait_ge(exped, m - 1)
        head = slot(t) + j
        for k in range(2):
            kt = 2 * half + k
            mm = nc.tensor.matmul(c.ps_s[:, 2 * (j % 2) + k, :], KX[:, bass.ds(head, 1), kt * P:(kt + 1) * P],
                                  QX[:, bass.ds(head, 1), :], start=True, stop=True)
        mm.then_inc(st, 1)

    def value_products(pe, t, half, part, first):
        k, side = divmod(part, 2)
        kt = 2 * half + k
        q = slice(side * S // 2, (side + 1) * S // 2)
        if half == 0 and part == 0:
            pe.wait_ge(s_vg, t + 1)
            if not first:
                pe.wait_ge(s_ct, t)
        if part == 0:
            pe.wait_ge(exped, (2 * t + half + 1) * GH)
        for j in range(GH):
            mm = nc.tensor.matmul(c.ps_v[j * CW:(j + 1) * CW, q], c.VG[:, kt, j, :], PT[:, half, j, k, q],
                                  start=(kt == 0 and side == 0), stop=(kt == QT - 1 and side == 1))
        if part == 3:
            mm.then_inc(products, 1)

    with nc.Block() as block:
        @block.sync
        def _(sp):
            def load_maxima(u):
                sp.wait_ge(s_mx, u + 1)
                for i in range(NPART):
                    sp.dma_start(QX[SROWS + i:SROWS + i + 1, bass.ds(slot(u), GH), :],
                                 MX[i * GH:(i + 1) * GH, :]).then_inc(s_mload, 16)

            def load_batch(b):
                sp.wait_ge(s_qx, b * 2 * STACK_LOADS * 16)
                if b >= 2:
                    sp.wait_ge(products, 2 * GROUPS * (b - 1))
                load_stacks(nc, sp, scratch, b, QX, KX, s_qx)

            load_batch(1)
            done = 0
            for b in range(2, B):
                with sp.Fori(done, GROUPS * (b - 1) + 2) as u:
                    load_maxima(u)
                done = GROUPS * (b - 1) + 2
                load_batch(b)
            with sp.Fori(done, STEPS) as u:
                load_maxima(u)

        @block.gpsimd
        def _(pool):
            def step(t, first, last):
                gather_values(c, pool, t, first, products, s_vg, per_group=2)
            peeled(pool, STEPS, step)

        @block.tensor
        def _(pe):
            pe.wait_ge(s_ib, 1)
            for u in range(AHEAD):
                for i in range(TILES):
                    score(pe, u, i, u == 0)
            turn_maxima(pe, 0, True)

            def step(t, first, last, ahead=True):
                for half in range(2):
                    for j in range(GH):
                        if ahead:
                            score(pe, t + AHEAD, 8 * half + 2 * j, False)
                        score_by_key(pe, t, half, j, first)
                        if ahead:
                            score(pe, t + AHEAD, 8 * half + 2 * j + 1, False)
                        if half:
                            for part in QUARTERS[j]:
                                value_products(pe, t, 0, part, first)
                        elif not first:
                            for part in QUARTERS[j]:
                                value_products(pe, t - 1, 1, part, False)
                        if half == 0 and j == 2 and not last:
                            if first:
                                pe.wait_ge(s_mx, 1)
                            turn_maxima(pe, t + 1, first)
                        if half == 1 and j == 1 and not first:
                            if not last:
                                pe.wait_ge(s_mx, t + 2)
                            group_end_pe(c, pe, t - 1, s_ct, s_ctx, s_ftr, CT4)
            step(0, True, False)
            with pe.Fori(1, STEPS - AHEAD) as t:
                step(t, False, False)
            step(STEPS - 2, False, False, ahead=False)
            step(STEPS - 1, False, True, ahead=False)
            for part in range(4):
                value_products(pe, STEPS - 1, 1, part, False)
            group_end_pe(c, pe, STEPS - 1, s_ct, s_ctx, s_ftr, CT4)

        @block.vector
        def _(dve):
            def maxima(u, i):
                dve.wait_ge(scores, u * TILES + i + 1)
                j, qt = i // QT, i % QT
                nc.vector.tensor_reduce(NM[:, qt, j:j + 1], c.ps_t[:, i % 2, :], AX.X, ALU.max,
                                        negate=True).then_inc(maxed, 1)

            def part_op(u, i):
                n = PART_OPS * u + i
                if i == 0:
                    dve.wait_ge(maxed, TILES * (u + 1))
                wait(dve, parted, n)
                part = lambda k: MP[:, :, k, :]
                if i == 0:
                    ins = nc.vector.tensor_copy(NF[:, :, :], NM[:, :, :])
                elif i % 2:
                    ins = nc.vector.tensor_copy(part(i // 2), NF[:, :, :])
                else:
                    ins = nc.vector.tensor_tensor(NF[:, :, :], NF[:, :, :], part(i // 2 - 1), ALU.subtract)
                ins.then_inc(parted, 1)

            nc.vector.tensor_copy(IB[:, :], c.ident[:, :]).then_inc(s_ib, 1)
            for u in range(AHEAD):
                for i in range(TILES):
                    maxima(u, i)
                for i in range(PART_OPS if u == 0 else 1):
                    part_op(u, i)

            def step(t, first, last, ahead=True):
                if not last:
                    dve.wait_ge(mturned, t + 1)
                    dve.wait_ge(parted, PART_OPS * (t + 1) + 1)
                for i in range(TILES):
                    if ahead:
                        maxima(t + AHEAD, i)
                    if i + 1 < PART_OPS and not last:
                        part_op(t + 1, i + 1)
                    if i == 12 and not first:
                        group_end_dve(c, dve, t - 1, s_ftr, s_rden, s_ctx, RDEN)
                if ahead:
                    part_op(t + AHEAD, 0)
            step(0, True, False)
            with dve.Fori(1, STEPS - AHEAD) as t:
                step(t, False, False)
            step(STEPS - 2, False, False, ahead=False)
            step(STEPS - 1, False, True, ahead=False)
            group_end_dve(c, dve, STEPS - 1, s_ftr, s_rden, s_ctx, RDEN)

        @block.scalar
        def _(act):
            def take_maxima(u, first):
                act.wait_ge(mturned, u + 1)
                if not first:
                    act.wait_ge(s_mload, NPART * 16 * u)
                nc.scalar.activation(MX[:, :], c.ps_f[0:GH * NPART, :], ACT.Copy).then_inc(s_mx, 1)

            take_maxima(0, True)

            def step(t, first, last):
                for half in range(2):
                    n = 2 * t + half
                    if not first:
                        act.wait_ge(products, n - 1)
                    for j in range(GH):
                        act.wait_ge(st, n * GH + j + 1)
                        nc.scalar.activation(PT[:, half, j, :, :], c.ps_s[:, 2 * (j % 2):2 * (j % 2) + 2, :],
                                             ACT.Exp).then_inc(exped, 1)
                        if half == 0 and j == 2 and not last:
                            take_maxima(t + 1, False)
                    if half == 0 and not first:
                        group_end_act(c, act, t - 1, products, s_ct, s_ftr, CT4, per_group=2)
            peeled(act, STEPS, step)
            group_end_act(c, act, STEPS - 1, products, s_ct, s_ftr, CT4, per_group=2)


def narrow_causal_attention(c, tag, own, QX, KX, scratch, s_qx, causal):
    nc = c.nc
    PR = c.sb(f"{tag}_PR", [P, 2, QT, S], F32, own)
    PT = c.sb(f"{tag}_PT", [P, 2, GH, QT, S], F32, own)
    CT4 = c.sb(f"{tag}_CT4", [P, S], F32, own)
    NM = c.sb(f"{tag}_NM", [P, 2, QT], F32, own)
    M1 = c.sb(f"{tag}_M1", [P, QT], F32, own)
    M2 = c.sb(f"{tag}_M2", [P, QT], F32, own)
    RDEN = c.sb(f"{tag}_RDEN", [P, QT, GH], F32, own)
    (scores, maxed, exped, turned, out_dve, out_act, products, s_vg, s_ct, s_ftr, s_rden, s_ctx, s_rel) = (
        c.sem(f"{tag}_{n}") for n in ("scores", "maxed", "exped", "turned", "out_dve", "out_act", "products",
                                      "vg", "ct", "ftr", "rden", "ctx", "rel"))
    keys = lambda qt: (qt + 1) * P

    def score_pair(pe, t, j, pair, first):
        n = t * GH + j
        if pair == 0 and j == 0:
            pe.wait_ge(s_qx, (t // GROUPS + 1) * 2 * STACK_LOADS * 16)
        if not first:
            pe.wait_ge(maxed, 2 * (n - 1) + pair + 1)
        head = (t % (2 * GROUPS)) * GH + j
        for qt in (2 * pair, 2 * pair + 1):
            last = nc.tensor.matmul(c.ps_s[:, qt, 0:keys(qt)], QX[:, bass.ds(head, 1), qt * P:(qt + 1) * P],
                                    KX[:, bass.ds(head, 1), 0:keys(qt)], start=True, stop=True)
        last.then_inc(scores, 1)

    def turn(pe, t, j, qt, first):
        n = t * GH + j
        pe.wait_ge(exped, QT * n + qt + 1)
        if not (first and qt < 2):
            before, m = (qt - 2, n) if qt >= 2 else (qt + 2, n - 1)
            if before == 0:
                pe.wait_ge(out_dve, m + 1)
            else:
                pe.wait_ge(out_act, (QT - 1) * m + before)
        for kt in range(keys(qt) // P):
            last = nc.tensor.transpose(c.ps_t[:, qt % 2, kt * P:(kt + 1) * P], PR[:, j % 2, qt, kt * P:(kt + 1) * P],
                                       c.ident[:, :])
        last.then_inc(turned, 1)

    def take(engine, t, side, j, qt, first):
        n = t * GH + j
        engine.wait_ge(turned, QT * n + qt + 1)
        if j == 0 and not first:
            engine.wait_ge(products, t - 1)
        k = keys(qt) // P
        dst = PT[:, side, j, 0:k, qt * P:(qt + 1) * P]
        src = c.ps_t[:, qt % 2, 0:k * P].rearrange("p (k q) -> p k q", q=P)
        if qt:
            nc.scalar.activation(dst, src, ACT.Copy).then_inc(out_act, 1)
        else:
            nc.vector.tensor_copy(dst, src).then_inc(out_dve, 1)

    def value_products(pe, t, side, kt):
        if kt == 0:
            pe.wait_ge(out_dve, GH * (t + 1))
            pe.wait_ge(out_act, (QT - 1) * GH * (t + 1))
            pe.wait_ge(s_vg, t + 1)
            if not (isinstance(t, int) and t == 0):
                pe.wait_ge(s_ct, t)
        for j in range(GH):
            mm = nc.tensor.matmul(c.ps_v[j * CW:(j + 1) * CW, kt * P:S], c.VG[:, kt, j, :],
                                  PT[:, side, j, kt, kt * P:S], start=(kt == 0), stop=(kt == QT - 1))
        if kt == QT - 1:
            mm.then_inc(products, 1)

    def maxima(dve, t, j, meanwhile=None):
        n = t * GH + j
        TAB, MASK = causal
        own_ops = Chain(s_rel)
        dve.sem_clear(s_rel)

        def diagonals(pair):
            dve.wait_ge(scores, 2 * n + pair + 1)
            step = QT + 1
            first = 2 * pair * step
            both = lambda t: t.rearrange("p q (n k) -> p (q n) k", k=P)[:, first:first + step + 1:step, :]
            own_ops.inc(nc.vector.tensor_tensor(
                both(PR[:, j % 2]), both(c.ps_s[:, :, :]),
                TAB[:, 3 * P:4 * P].rearrange("p (a k) -> p a k", a=1).broadcast_to([P, 2, P]), ALU.mult))
            return own_ops.value()

        def masked(qt, after):
            dve.wait_ge(s_rel, after)
            d = slice(qt * P, (qt + 1) * P)
            own_ops.inc(nc.vector.tensor_tensor_reduce(
                out=PR[:, j % 2, qt, d], in0=PR[:, j % 2, qt, d], in1=MASK[:, :], scale=1.0, scalar=LOWEST,
                op0=ALU.add, op1=ALU.max, accum_out=(M1 if qt else M2)[:, qt:qt + 1]))
            return own_ops.value()

        def left(qt, after):
            dve.wait_ge(s_rel, after)
            d = slice(0, qt * P)
            own_ops.inc(nc.vector.tensor_tensor_reduce(
                out=PR[:, j % 2, qt, d], in0=c.ps_s[:, qt, d], in1=TAB[:, (3 - qt) * P:3 * P], scale=1.0,
                scalar=M1[:, qt:qt + 1], op0=ALU.mult, op1=ALU.max, accum_out=M2[:, qt:qt + 1]))
            return own_ops.value()

        def negated(pair, after):
            dve.wait_ge(s_rel, after)
            nc.vector.tensor_scalar(NM[:, j % 2, 2 * pair:2 * pair + 2], M2[:, 2 * pair:2 * pair + 2], -1.0, None,
                                    ALU.mult).then_inc(maxed, 1)

        at = diagonals(0)
        if meanwhile:
            meanwhile()
        one = masked(1, at)
        masked(0, at)
        one = left(1, one)
        at = diagonals(1)
        negated(0, one)
        two, three = masked(2, at), masked(3, at)
        left(2, two)
        negated(1, left(3, three))

    def probabilities(act, t, j, qt):
        n = t * GH + j
        act.wait_ge(maxed, 2 * n + qt // 2 + 1)
        k = keys(qt)
        nc.scalar.activation(PR[:, j % 2, qt, 0:k], PR[:, j % 2, qt, 0:k], ACT.Exp, bias=NM[:, j % 2, qt:qt + 1]).then_inc(exped, 1)

    def after(t, j):
        return (t, j + 1) if j + 1 < GH else (t + 1, 0)

    with nc.Block() as block:
        @block.sync
        def _(sp):
            for b in range(1, B):
                sp.wait_ge(s_qx, b * 2 * STACK_LOADS * 16)
                if b >= 2:
                    sp.wait_ge(scores, 2 * H * (b - 1))
                load_stacks(nc, sp, scratch, b, QX, KX, s_qx)

        @block.gpsimd
        def _(pool):
            def step(t, first, last):
                gather_values(c, pool, t, first, products, s_vg)
            peeled(pool, STEPS, step)

        @block.tensor
        def _(pe):
            score_pair(pe, 0, 0, 0, True)
            score_pair(pe, 0, 0, 1, True)

            def step(t, side, place):
                for j in range(GH):
                    for pair in range(2):
                        if not (place == -1 and j == GH - 1):
                            score_pair(pe, *after(t, j), pair, False)
                        turn(pe, t, j, 2 * pair, place == 0 and j == 0)
                        turn(pe, t, j, 2 * pair + 1, place == 0 and j == 0)
                    if j == 0 and place not in (0, 1):
                        group_end_pe(c, pe, t - 2, s_ct, s_ctx, s_ftr, CT4)
                    if j < 3 and place != 0:
                        for kt in ((0,), (1,), (2, 3))[j]:
                            value_products(pe, t - 1, 1 - side, kt)
            steps(pe, step)
            group_end_pe(c, pe, STEPS - 2, s_ct, s_ctx, s_ftr, CT4)
            for kt in range(QT):
                value_products(pe, STEPS - 1, 1, kt)
            group_end_pe(c, pe, STEPS - 1, s_ct, s_ctx, s_ftr, CT4)

        @block.vector
        def _(dve):
            maxima(dve, 0, 0)

            def step(t, side, place):
                for j in range(GH):
                    take_first = lambda: take(dve, t, side, j, 0, place in (0, 1))
                    if place == -1 and j == GH - 1:
                        take_first()
                    else:
                        maxima(dve, *after(t, j), take_first)
                    if j == 1 and place not in (0, 1):
                        group_end_dve(c, dve, t - 2, s_ftr, s_rden, s_ctx, RDEN)
            steps(dve, step)
            for t in (STEPS - 2, STEPS - 1):
                group_end_dve(c, dve, t, s_ftr, s_rden, s_ctx, RDEN)

        @block.scalar
        def _(act):
            for qt in range(QT):
                probabilities(act, 0, 0, qt)

            def step(t, side, place):
                for j in range(GH):
                    for pair in range(2):
                        for qt in (2 * pair, 2 * pair + 1):
                            if qt:
                                take(act, t, side, j, qt, place in (0, 1))
                        if not (place == -1 and j == GH - 1):
                            ahead = after(t, j)
                            probabilities(act, *ahead, 2 * pair)
                            probabilities(act, *ahead, 2 * pair + 1)
                    if j == 3 and place != 0:
                        group_end_act(c, act, t - 1, products, s_ct, s_ftr, CT4, first=(place == 1))
            steps(act, step)
            group_end_act(c, act, STEPS - 1, products, s_ct, s_ftr, CT4)


def norm_stats(nc, R, ST, MV, chain, dve, s_stats):
    for i in range(QT):
        chain.inc(nc.vector.bn_stats(ST[:, i, :], R[:, i, :]))
    chain.wait(dve)
    for i in range(QT):
        last = nc.vector.bn_aggr(MV[:, i, :], ST[:, i, :])
    last.then_inc(s_stats, 1)


def norm_scales(c, pool, MV, RS, s_stats, s_rstd, n):
    nc = c.nc
    pool.wait_ge(s_stats, n + 1)
    nc.gpsimd.tensor_scalar(RS[:, :], MV[:, :, 1], EPS, None, ALU.add).then_inc(s_rstd, 1)
    pool.wait_ge(s_rstd, 2 * n + 1)
    nc.gpsimd.tensor_tensor(RS[:, :], RS[:, :], c.neghalf[:, :], ALU.pow).then_inc(s_rstd, 1)


def norm_apply(nc, dve, R, dst, MV, RS, done, s_rstd, n):
    dve.wait_ge(s_rstd, 2 * (n + 1))
    for i in range(QT):
        done.inc(nc.vector.tensor_scalar(dst[:, i, :], R[:, i, :], MV[:, i, 0:1], RS[:, i:i + 1],
                                         ALU.subtract, ALU.mult))


def norm_order(norms):
    if norms == 1:
        return [(0, "stats", 0)] + [s for b in range(B) for s in
                                    ([(0, "stats", b + 1)] if b + 1 < B else []) + [(0, "apply", b)]]
    return [step for b in range(0, B, 2) for step in
            [(0, "stats", b), (0, "stats", b + 1), (0, "apply", b), (1, "stats", b), (0, "apply", b + 1),
             (1, "stats", b + 1), (1, "apply", b), (1, "apply", b + 1)]]


def finish(c, tag, source, wo=None, bias=None, mode="post", pre=None, out=None, OT=None):
    nc = c.nc
    with ExitStack() as own:
        W = c.sb(f"{tag}_fW", [P, P], F32, own)
        BO = c.sb(f"{tag}_fBO", [P, P], F32, own)
        WB = c.sb(f"{tag}_fWB", [P, 2], F32, own)
        CT = c.sb(f"{tag}_fCT", [P, 2, QT, P], F32, own)
        R = c.sb(f"{tag}_fR", [P, 2, QT, P], F32, own)
        R2 = c.sb(f"{tag}_fR2", [P, 2, QT, P], F32, own)
        ST = c.sb(f"{tag}_fST", [P, 2, QT, 6], F32, own)
        MV = c.sb(f"{tag}_fMV", [P, 2, QT, 2], F32, own)
        RS = c.sb(f"{tag}_fRS", [P, 2, QT], F32, own)
        s_w, s_t1, s_ct, s_o, s_sum, s_chain, s_stats, s_rstd, s_n, s_t2, s_xt, s_out = (
            c.sem(f"{tag}_f{n}") for n in ("w", "t1", "ct", "o", "sum", "chain", "stats", "rstd", "n", "t2", "xt", "out"))
        n_w = 16 * ((wo is not None) + (bias is not None) + 2 * (pre is not None))
        norms = 1 if (mode == "inner" or pre is None) else 2
        with nc.Block() as block:
            @block.sync
            def _(sp):
                if wo is not None:
                    sp.dma_start(W[:, :], wo).then_inc(s_w, 16)
                if bias is not None:
                    sp.dma_start(BO[:, :], row(bias)).then_inc(s_w, 16)
                if pre is not None:
                    sp.dma_start(WB[:, 0:1], col(pre[0])).then_inc(s_w, 16)
                    sp.dma_start(WB[:, 1:2], col(pre[1])).then_inc(s_w, 16)
                if out is not None:
                    for b in range(B):
                        sp.wait_ge(s_n, QT * (b + 1))
                        sp.dma_start(out[b].rearrange("(n p) d -> p n d", p=P),
                                     c.X[:, b * QT:(b + 1) * QT, :]).then_inc(s_out, 16)
                    sp.wait_ge(s_out, 16 * B)

            @block.gpsimd
            def _(pool):
                for n in range(norms * B):
                    norm_scales(c, pool, MV[:, n % 2], RS[:, n % 2], s_stats, s_rstd, n)

            @block.tensor
            def _(pe):
                if n_w:
                    pe.wait_ge(s_w, n_w)

                def before(b):
                    if source == "x":
                        return
                    src = c.CTX[:, b * QT:(b + 1) * QT, :] if source == "ctx" else OT[:, b, :].rearrange("p (i t) -> p i t", i=QT)
                    if source == "ctx":
                        if b >= 2:
                            pe.wait_ge(s_ct, b - 1)
                        for i in range(QT):
                            last = nc.tensor.transpose(c.ps_s[:, b % 2, i * P:(i + 1) * P], src[:, i, :], c.ident[:, :])
                        last.then_inc(s_t1, 1)
                        pe.wait_ge(s_ct, b + 1)
                    if b >= 2:
                        pe.wait_ge(s_sum, b - 1)
                    for i in range(QT):
                        dst = c.ps_s[:, 2 + b % 2, i * P:(i + 1) * P]
                        if source == "ctx":
                            last = nc.tensor.matmul(dst, CT[:, b % 2, i, :], W[:, :], start=True, stop=True)
                        else:
                            last = nc.tensor.transpose(dst, src[:, i, :], c.ident[:, :])
                    last.then_inc(s_o, 1)

                def behind(b):
                    if out is not None:
                        return
                    pe.wait_ge(s_n, QT * (b + 1))
                    if b >= 2:
                        pe.wait_ge(s_xt, b - 1)
                    for i in range(QT):
                        src = c.X[:, b * QT + i, :] if (mode == "post" and pre is None) else R2[:, b % 2, i, :]
                        last = nc.tensor.transpose(c.ps_t[:, b % 2, i * P:(i + 1) * P], src, c.ident[:, :])
                    last.then_inc(s_t2, 1)

                for b in range(B):
                    before(b)
                for b in range(B):
                    behind(b)

            @block.scalar
            def _(act):
                def before(b):
                    if source == "ctx":
                        act.wait_ge(s_t1, b + 1)
                        if b >= 2:
                            act.wait_ge(s_o, b - 1)
                        nc.scalar.activation(CT[:, b % 2, :, :], c.ps_s[:, b % 2, :].rearrange("p (i t) -> p i t", i=QT),
                                             ACT.Copy).then_inc(s_ct, 1)

                def behind(b):
                    if out is not None:
                        return
                    act.wait_ge(s_t2, b + 1)
                    dst, src = c.XT[:, b * S:(b + 1) * S], c.ps_t[:, b % 2, :]
                    if pre is None:
                        nc.scalar.activation(dst, src, ACT.Copy).then_inc(s_xt, 1)
                    else:
                        nc.scalar.activation(dst, src, ACT.Identity, bias=WB[:, 1:2], scale=WB[:, 0:1]).then_inc(s_xt, 1)
                if n_w:
                    act.wait_ge(s_w, n_w)
                for b in range(B):
                    before(b)
                for b in range(B):
                    behind(b)

            @block.vector
            def _(dve):
                chain, done = Chain(s_chain), Chain(s_n)
                if n_w:
                    dve.wait_ge(s_w, n_w)

                def summed(b, x):
                    if source == "x":
                        return x
                    dve.wait_ge(s_o, b + 1)
                    if b >= 2:
                        (done if norms == 1 else chain).wait(dve)
                    o = c.ps_s[:, 2 + b % 2, :].rearrange("p (i t) -> p i t", i=QT)
                    r = R[:, b % 2]
                    nc.vector.tensor_tensor(r, x, o, ALU.add).then_inc(s_sum, 1)
                    dve.wait_ge(s_sum, b + 1)
                    if bias is not None:
                        chain.inc(nc.vector.tensor_tensor(
                            r, r, BO[:, :].rearrange("p (a d) -> p a d", a=1).broadcast_to([P, QT, P]), ALU.add))
                        chain.wait(dve)
                    return r

                place, count = {}, 0
                for norm, what, b in norm_order(norms):
                    x = c.X[:, b * QT:(b + 1) * QT, :]
                    r = x if norm == 1 or source == "x" else R[:, b % 2]
                    if what == "stats":
                        if norm == 0:
                            r = summed(b, x)
                            if mode == "inner":
                                chain.inc(nc.vector.tensor_tensor(x, x, r, ALU.add))
                        else:
                            chain.wait(dve)
                        place[norm, b] = count
                        norm_stats(nc, r, ST[:, count % 2], MV[:, count % 2], chain, dve, s_stats)
                        count += 1
                    else:
                        final = norm == norms - 1
                        to_x = mode != "inner" and not (norms == 2 and final)
                        if not to_x and b >= 2:
                            dve.wait_ge(s_t2, b - 1)
                        n = place[norm, b]
                        norm_apply(nc, dve, r, x if to_x else R2[:, b % 2], MV[:, n % 2], RS[:, n % 2],
                                   done if final else chain, s_rstd, n)
                done.wait(dve)


def distance_tables(c, rel, TAB, MASK, own):
    nc = c.nc
    near = QT * P - P - CLIP
    DI = c.sb("rel_DI", [P, QT * P - near], mybir.dt.int32, own)
    D = c.sb("rel_D", [P, QT * P - near], F32, own)
    T = c.sb("rel_T", [P, QT * P - near], F32, own)
    E = c.sb("rel_E", [P, CLIP + 1], F32, own)
    s_e, s_iota, s_chain = (c.sem(f"rel_{n}") for n in ("e", "iota", "chain"))
    s_rows = c.sem("rel_query_rows"), c.sem("rel_key_rows")

    def load(sp):
        sp.dma_start(E[:, :], row(rel)).then_inc(s_e, 16)

    def pool_part(pool):
        nc.gpsimd.iota(DI[:, :], pattern=[[-1, QT * P - near]], base=(QT - 1) * P - near, channel_multiplier=1)\
            .then_inc(s_iota, 1)
        nc.gpsimd.memset(MASK[:, :], 0.0).then_inc(s_iota, 1)
        pool.wait_ge(s_iota, 2)
        nc.gpsimd.affine_select(out=MASK[:, :], in_=MASK[:, :], compare_op=ALU.is_ge, fill=MASKED,
                                base=0, pattern=[[-1, P]], channel_multiplier=1).then_inc(s_iota, 1)
        pool.wait_ge(s_iota, 3)
        zero_rows(c, pool, c.QX, s_rows[0])

    def vector_part(dve):
        chain = Chain(s_chain)
        dve.wait_ge(s_e, 16)
        dve.wait_ge(s_iota, 1)
        chain.inc(nc.vector.tensor_scalar(E[:, :], E[:, :], ISQ8, None, ALU.mult))
        chain.inc(nc.vector.tensor_copy(D[:, :], DI[:, :]))
        chain.wait(dve)
        chain.inc(nc.vector.tensor_copy(TAB[:, 0:near], E[:, CLIP:CLIP + 1].broadcast_to([P, near])))
        chain.inc(nc.vector.tensor_scalar(TAB[:, near:], D[:, :], float(CLIP), E[:, CLIP:CLIP + 1], ALU.is_ge, ALU.mult))
        chain.wait(dve)
        for r in range(CLIP):
            chain.inc(nc.vector.tensor_scalar(T[:, :], D[:, :], float(r), E[:, r:r + 1], ALU.is_equal, ALU.mult))
            chain.wait(dve)
            chain.inc(nc.vector.tensor_tensor(TAB[:, near:], TAB[:, near:], T[:, :], ALU.add))
            chain.wait(dve)

    return Beside(load, pool_part, lambda pe: None, vector_part,
                  lambda act: zero_rows(c, act, c.KX, s_rows[1]), s_rows)


def narrow_self_attention(c, tag, wq, wk, wv, scratch, bq=None, bk=None, bv=None, qscale=1.0, rel=None):
    with ExitStack() as own:
        QX, KX = c.QX, c.KX
        c.VN = c.sb(f"{tag}_VN", [P, NT, P], F32, own)
        s_qx = c.sem(f"{tag}_qx")
        causal = None
        if rel is not None:
            TAB = c.sb(f"{tag}_TAB", [P, QT * P], F32, own)
            MASK = c.sb(f"{tag}_MASK", [P, P], F32, own)
            causal = (TAB, MASK)
        with ExitStack() as brief:
            tables = distance_tables(c, rel, *causal, brief) if causal else None
            narrow_projections(c, tag, brief, scratch, QX, KX, s_qx, wq, wk, wv, bq, bk, bv, qscale, beside=tables)
        if causal:
            narrow_causal_attention(c, tag, own, QX, KX, scratch, s_qx, causal)
        else:
            narrow_full_attention(c, tag, own, QX, KX, scratch, s_qx)


def cross_operands(c, tag, own, wk, bk, wv, bv, KX, VB):
    nc = c.nc
    GR = SROWS // HD8
    WK = c.sb(f"{tag}_WK", [P, HD8], F32, own)
    WKR = c.sb(f"{tag}_WKR", [P, SROWS], F32, own)
    BK = c.sb(f"{tag}_BK", [SROWS, 1], F32, own)
    WV = c.sb(f"{tag}_oWV", [P, HD8], F32, own)
    BV = c.sb(f"{tag}_oBV", [KC, HD8], F32, own)
    G = c.sb(f"{tag}_G", [SROWS, GR], F32, own)
    MK = c.sb(f"{tag}_MK", [SROWS, NPART], F32, own)
    FULL = c.sb(f"{tag}_KF", [SROWS, B * KC], F32, own)
    PARTS = c.sb(f"{tag}_KP", [SROWS, NPART, B * KC], BF16, own)
    s_w, s_g, s_ops, s_k, s_v, s_split = (c.sem(f"{tag}_o{n}") for n in ("w", "g", "ops", "k", "v", "split"))

    def load(sp):
        sp.dma_start(WK[:, :], wk).then_inc(s_w, 16)
        sp.dma_start(WV[:, :], wv).then_inc(s_w, 16)
        sp.dma_start(BV[:, :], row(bv, KC)).then_inc(s_w, 16)
        for g in range(NPART * NPART):
            sp.dma_start(BK[g * HD8:(g + 1) * HD8, :], col(bk)).then_inc(s_w, 16)

    def pool_part(pool):
        nc.gpsimd.memset(VB[:, :, :], 0.0)
        nc.gpsimd.memset(G[:, :], 1.0).then_inc(s_g, 1)
        pool.wait_ge(s_g, 1)
        nc.gpsimd.affine_select(out=G[:, :], in_=G[:, :], compare_op=ALU.is_ge, fill=0.0, base=0,
                                pattern=[[-HD8, GR]], channel_multiplier=1).then_inc(s_g, 1)
        pool.wait_ge(s_g, 2)
        nc.gpsimd.affine_select(out=G[:, :], in_=G[:, :], compare_op=ALU.is_ge, fill=0.0, base=HD8 - 1,
                                pattern=[[HD8, GR]], channel_multiplier=-1).then_inc(s_g, 1)
        pool.wait_ge(s_g, 3)
        nc.gpsimd.memset(c.KX[SROWS:P, :, :], 1.0)

    def tensor_part(pe):
        pe.wait_ge(s_w, 16 * 12)
        pe.wait_ge(s_ops, 2)
        nc.tensor.matmul(c.ps_s[0:SROWS, 2, 0:B * KC], WKR[:, :], c.CTT[:, :], start=True, stop=True).then_inc(s_k, 1)
        for b in range(B):
            last = nc.tensor.matmul(c.ps_t[0:KC, 0, b * HD8:(b + 1) * HD8], c.CTT[:, b * KC:(b + 1) * KC], WV[:, :],
                                    start=True, stop=True)
        last.then_inc(s_v, 1)

    def vector_part(dve):
        ops, split = Chain(s_ops), Chain(s_split)
        dve.wait_ge(s_w, 16 * 12)
        ops.inc(nc.vector.memset(WKR[:, NPART * NPART * HD8:], 0.0))
        ops.inc(nc.vector.tensor_copy(
            WKR[:, 0:NPART * NPART * HD8].rearrange("p (g d) -> p g d", d=HD8),
            WK[:, :].rearrange("p (a d) -> p a d", a=1).broadcast_to([P, NPART * NPART, HD8])))
        dve.wait_ge(s_g, 3)
        g = G[:, 0:NPART * NPART].rearrange("p (i j) -> p j i", j=NPART)
        ops.inc(nc.vector.reduce_sum(MK[:, :], g, AX.X))
        dve.wait_ge(s_k, 1)
        rows = NPART * NPART * HD8
        ops.inc(nc.vector.tensor_copy(FULL[:, :], c.ps_s[0:SROWS, 2, 0:B * KC]))
        ops.wait(dve)
        ops.inc(nc.vector.tensor_scalar(FULL[0:rows, :], FULL[0:rows, :], BK[0:rows, :], None, ALU.add))
        ops.wait(dve)
        split_parts(nc, dve, split, FULL[:, :], lambda i: PARTS[:, i, :])
        kx = KX[:, :, :].rearrange("p b k -> p (b k)")
        ops.inc(nc.vector.tensor_scalar(kx, PARTS[:, 0, :], MK[:, 0:1], None, ALU.mult))
        for i in (1, 2):
            ops.wait(dve)
            ops.inc(nc.vector.scalar_tensor_tensor(kx, PARTS[:, i, :], MK[:, i:i + 1], kx, ALU.mult, ALU.add))
        dve.wait_ge(s_v, 1)
        nc.vector.tensor_tensor(VB[0:KC, :, :], c.ps_t[0:KC, 0, 0:B * HD8].rearrange("p (b d) -> p b d", b=B),
                                BV[:, :].rearrange("p (a d) -> p a d", a=1).broadcast_to([KC, B, HD8]), ALU.add)

    return Beside(load, pool_part, tensor_part, vector_part)


def narrow_cross(c, tag, own, QX, KX, VB, scratch, s_qx):
    nc = c.nc
    SC = c.sb(f"{tag}_SC", [P, 2, QT, KC], F32, own)
    PR = c.sb(f"{tag}_PR", [P, 2, QT, KC], F32, own)
    PT = c.sb(f"{tag}_PT", [SROWS, 2, GH, S], F32, own)
    CT4 = c.sb(f"{tag}_CT4", [P, S], F32, own)
    M = c.sb(f"{tag}_M", [P, 2, QT], F32, own)
    RDEN = c.sb(f"{tag}_RDEN", [P, QT, GH], F32, own)
    (scores, maxed, lessened, exped, turned, taken, products, s_vg, s_ct, s_ftr, s_rden, s_ctx, s_zero) = (
        c.sem(f"{tag}_{n}") for n in ("scores", "maxed", "lessened", "exped", "turned", "taken", "products",
                                      "vg", "ct", "ftr", "rden", "ctx", "ptzero"))
    NK = GH

    def ahead(t, j, k):
        return (t, j + k) if j + k < GH else (t + 1, j + k - GH)

    def score(pe, t, j, first):
        n = t * GH + j
        if j == 0:
            pe.wait_ge(s_qx, (t // GROUPS + 1) * STACK_LOADS * 16)
        if not first:
            pe.wait_ge(lessened, n - NK + 1)
        head = (t % (2 * GROUPS)) * GH + j
        for qt in range(QT):
            last = nc.tensor.matmul(c.ps_s[:, j, qt * KC:(qt + 1) * KC], QX[0:SROWS, bass.ds(head, 1), qt * P:(qt + 1) * P],
                                    KX[:, bass.ds(t // GROUPS, 1), :], start=True, stop=True)
        last.then_inc(scores, 1)

    with nc.Block() as block:
        @block.sync
        def _(sp):
            for b in range(1, B):
                sp.wait_ge(s_qx, b * STACK_LOADS * 16)
                if b >= 2:
                    sp.wait_ge(scores, H * (b - 1))
                load_stacks(nc, sp, scratch, b, QX, None, s_qx)

        @block.gpsimd
        def _(pool):
            nc.gpsimd.memset(PT[64:SROWS, :, :, :], 0.0).then_inc(s_zero, 1)
            pool.wait_ge(s_zero, 1)

            def step(t, first, last):
                gather_values(c, pool, t, first, products, s_vg, VB)
            peeled(pool, STEPS, step)

        @block.tensor
        def _(pe):
            score(pe, 0, 0, True)
            score(pe, 0, 1, True)

            def value_products(t, side):
                pe.wait_ge(taken, GH * (t + 1))
                pe.wait_ge(s_vg, t + 1)
                if not (isinstance(t, int) and t == 0):
                    pe.wait_ge(s_ct, t)
                for j in range(GH):
                    mm = nc.tensor.matmul(c.ps_v[j * CW:(j + 1) * CW, :], c.VG[0:SROWS, 0, 0, :], PT[:, side, j, :],
                                          start=True, stop=True)
                mm.then_inc(products, 1)

            def step(t, side, place):
                for j in range(GH):
                    n = t * GH + j
                    if not (place == -1 and j >= 2):
                        score(pe, *ahead(t, j, 2), place == 0 and j < 2)
                    pe.wait_ge(exped, n + 1)
                    if not (place == 0 and j < 2):
                        pe.wait_ge(taken, n - 1)
                    for qt in range(QT):
                        mm = nc.tensor.transpose(c.ps_t[0:KC, j % 2, qt * P:(qt + 1) * P], PR[:, j % 2, qt, :], c.ident[:, :])
                    mm.then_inc(turned, 1)
                    if place != 0 and j == 1:
                        value_products(t - 1, 1 - side)
                    if place != 0 and j == 3:
                        group_end_pe(c, pe, t - 1, s_ct, s_ctx, s_ftr, CT4, first=(place == 1))
            steps(pe, step)
            value_products(STEPS - 1, 1)
            group_end_pe(c, pe, STEPS - 1, s_ct, s_ctx, s_ftr, CT4)

        @block.vector
        def _(dve):
            def lessen(t, j):
                n = t * GH + j
                dve.wait_ge(scores, n + 1)
                src = c.ps_s[:, j, 0:QT * KC].rearrange("p (q k) -> p q k", q=QT)
                nc.vector.reduce_max(M[:, j % 2, :], src, AX.X).then_inc(maxed, 1)
                dve.wait_ge(maxed, n + 1)
                nc.vector.tensor_tensor(SC[:, j % 2], src, M[:, j % 2, :].rearrange("p (q a) -> p q a", a=1).broadcast_to([P, QT, KC]),
                                        ALU.subtract).then_inc(lessened, 1)
            lessen(0, 0)
            lessen(0, 1)

            def step(t, side, place):
                for j in range(GH):
                    if not (place == -1 and j >= 2):
                        nt, nj = ahead(t, j, 2)
                        dve.wait_ge(exped, t * GH + j + 1)
                        lessen(nt, nj)
                    if j == 0 and place not in (0, 1):
                        group_end_dve(c, dve, t - 2, s_ftr, s_rden, s_ctx, RDEN)
            steps(dve, step)
            for t in (STEPS - 2, STEPS - 1):
                group_end_dve(c, dve, t, s_ftr, s_rden, s_ctx, RDEN)

        @block.scalar
        def _(act):
            def prob(t, j, first):
                n = t * GH + j
                act.wait_ge(lessened, n + 1)
                if not first:
                    act.wait_ge(turned, n - 1)
                nc.scalar.activation(PR[:, j % 2], SC[:, j % 2], ACT.Exp).then_inc(exped, 1)
            prob(0, 0, True)
            prob(0, 1, True)
            act.wait_ge(s_zero, 1)

            def step(t, side, place):
                for j in range(GH):
                    n = t * GH + j
                    act.wait_ge(turned, n + 1)
                    if j == 0 and place not in (0, 1):
                        act.wait_ge(products, t - 1)
                    nc.scalar.activation(PT[0:KC, side, j, :], c.ps_t[0:KC, j % 2, :], ACT.Copy).then_inc(taken, 1)
                    if not (place == -1 and j >= 2):
                        prob(*ahead(t, j, 2), False)
                    if place != 0 and j == 2:
                        group_end_act(c, act, t - 1, products, s_ct, s_ftr, CT4, first=(place == 1))
            steps(act, step)
            group_end_act(c, act, STEPS - 1, products, s_ct, s_ftr, CT4)


def narrow_cross_attention(c, tag, wq, bq, wk, bk, wv, bv, scratch):
    with ExitStack() as own:
        QX = c.QX
        KX = c.sb(f"{tag}_KX", [SROWS, B, KC], BF16, own)
        VB = c.sb(f"{tag}_VB", [SROWS, B, HD8], F32, own)
        s_qx = c.sem(f"{tag}_qx")
        with ExitStack() as brief:
            operands = cross_operands(c, tag, brief, wk, bk, wv, bv, KX, VB)
            narrow_projections(c, tag, brief, scratch, QX, None, s_qx, wq, None, None, bq=bq, beside=operands)
        narrow_cross(c, tag, own, QX, KX, VB, scratch, s_qx)


def wide_self_attention(c, tag, wq, wk, wv, wo, OT):
    nc = c.nc
    SPAN = 2 * S - P
    TM = QT * H
    with ExitStack() as own:
        WQ, WK, WV = (c.sb(f"{tag}_W{n}", [P, H * HD64], F32, own) for n in "qkv")
        WO = c.sb(f"{tag}_Wo", [P, PAIRS, P], F32, own)
        BH = c.sb(f"{tag}_BH", [P, H, SPAN], F32, own)
        XB = c.sb(f"{tag}_XB", [P, S], F32, own)
        VB = c.sb(f"{tag}_VB", [P, QT, H * HD64], F32, own)
        Q = c.sb(f"{tag}_Q", [P, 2, S], F32, own)
        KZ = c.sb(f"{tag}_KZ", [P, 2, 2, S], F32, own)
        PR = c.sb(f"{tag}_PR", [P, 2, QT, S], F32, own)
        PT = c.sb(f"{tag}_PT", [P, 2, 2, QT, S], F32, own)
        CT = c.sb(f"{tag}_CT", [P, S], F32, own)
        M = c.sb(f"{tag}_M", [P, 2, QT], F32, own)
        NM = c.sb(f"{tag}_NM", [P, 2, QT], F32, own)
        DEN = c.sb(f"{tag}_DEN", [P, 2, QT], F32, own)
        GO = c.sb(f"{tag}_GO", [P, 1], F32, own)
        RDEN = c.sb(f"{tag}_RDEN", [P, 2, QT], F32, own)
        (s_w, s_made, s_iota, s_zero, s_xb, s_vproj, v_act, v_dve, v_pair, v_out, proj, q_out, k_out, scores, biased, negated, exped, inverted,
         normed, turned, taken, products, heads_out, added, s_ot) = (
            c.sem(f"{tag}_{n}") for n in
            ("w", "made", "iota", "zero", "xb", "vproj", "v_act", "v_dve", "v_pair", "v_out", "proj", "q_out", "k_out", "scores", "biased", "negated",
             "exped", "inverted", "normed", "turned", "taken", "products", "heads_out", "added", "ot"))
        ps_q, ps_k, ps_o = c.ps_s[:, 2, :], c.ps_f[:, :], c.ps_s[:, 3, :]

        def ahead(b, i):
            return (b, i + 1) if i + 1 < H else (b + 1, 0)

        def pair_after(b, p):
            return (b, p + 1) if p + 1 < PAIRS else (b + 1, 0)

        def pair_before(b, p):
            return (b, p - 1) if p else (b - 1, PAIRS - 1)

        def values_due(p, first, last):
            return not first if p == 0 else not last

        T = BH[:, H - 1, :]

        def distances(dve, chain):
            dve.wait_ge(s_iota, 1)
            chain.inc(nc.vector.tensor_copy(BH[:, 1, :], BH[:, 0, :].bitcast(mybir.dt.int32)))
            chain.wait(dve)
            chain.inc(nc.vector.tensor_scalar(BH[:, 2, :], BH[:, 1, :], -1.0, None, ALU.mult))
            chain.wait(dve)
            chain.inc(nc.vector.tensor_tensor(T, BH[:, 1, :], BH[:, 2, :], ALU.min))
            chain.wait(dve)

        def head_bias(dve, chain, h):
            if h == H - 1:
                chain.wait(dve)
            chain.inc(nc.vector.tensor_scalar(BH[:, h, :], T, 2.0 ** (-8.0 / (H - h)), None, ALU.mult))

        with nc.Block() as block:
            @block.sync
            def _(sp):
                for dst, src in ((WQ, wq), (WK, wk), (WV, wv)):
                    sp.dma_start(dst[:, :], src).then_inc(s_w, 16)
                sp.dma_start(WO[:, :, :], wo.rearrange("(g p) n -> p g n", p=P)).then_inc(s_w, 16)

            @block.gpsimd
            def _(pool):
                nc.gpsimd.iota(BH[:, 0, :].bitcast(mybir.dt.int32), pattern=[[-1, SPAN]], base=S - P,
                               channel_multiplier=1).then_inc(s_iota, 1)
                nc.gpsimd.memset(KZ[:, :, :, :], 0.0).then_inc(s_zero, 1)

            @block.tensor
            def _(pe):
                pe.wait_ge(s_w, 16 * 4)

                def project(b, p):
                    g = b * PAIRS + p
                    wait(pe, q_out, g)
                    wait(pe, k_out, 2 * g)
                    wait(pe, v_out, min(g - 2, (B - 1) * PAIRS) if isinstance(b, int) else g - 2)
                    w = slice(p * P, (p + 1) * P)
                    x = c.XT[:, bass.ds(b * S, S)]
                    nc.tensor.matmul(ps_q, WQ[:, w], x, start=True, stop=True).then_inc(proj, 1)
                    nc.tensor.matmul(ps_k, WK[:, w], x, start=True, stop=True).then_inc(proj, 1)

                def project_values(b, p):
                    of = (p - 1) % PAIRS
                    wait(pe, s_xb, b + 1 if p == 0 else b + 2)
                    wait(pe, k_out, 2 * (b * PAIRS + p + 2))
                    for kt in range(QT):
                        mm = nc.tensor.matmul(ps_k[:, kt * P:(kt + 1) * P], XB[:, kt * P:(kt + 1) * P],
                                              WV[:, of * P:(of + 1) * P], start=True, stop=True)
                    mm.then_inc(v_pair, 1)

                def score(b, i, qt):
                    m, p = QT * i + qt, i // 2
                    if i % 2 == 0 and qt == 0:
                        wait(pe, q_out, b * PAIRS + p + 1)
                        wait(pe, k_out, b * H + 2 * p + 2)
                    wait(pe, biased, b * TM + m - 1)
                    nc.tensor.matmul(c.ps_s[:, qt % 2, :], Q[:, p % 2, qt * P:(qt + 1) * P], KZ[:, p % 2, i % 2, :],
                                     start=True, stop=True).then_inc(scores, 1)

                def turn(b, i, qt):
                    m = QT * i + qt
                    wait(pe, normed, b * TM + m + 1)
                    wait(pe, taken, b * TM + m - 1)
                    for kt in range(QT):
                        mm = nc.tensor.transpose(c.ps_t[:, qt % 2, kt * P:(kt + 1) * P],
                                                 PR[:, i % 2, qt, kt * P:(kt + 1) * P], c.ident[:, :])
                    mm.then_inc(turned, 1)

                def weigh(b, p):
                    wait(pe, taken, b * TM + 2 * QT * (p + 1))
                    wait(pe, heads_out, b * PAIRS + p)
                    wait(pe, v_out, b * PAIRS + p - (PAIRS - 1))
                    for kt in range(QT):
                        for e in range(2):
                            h = 2 * p + e
                            mm = nc.tensor.matmul(c.ps_v[e * HD64:(e + 1) * HD64, :], VB[:, kt, h * HD64:(h + 1) * HD64],
                                                  PT[:, p % 2, e, kt, :], start=(kt == 0), stop=(kt == QT - 1))
                    mm.then_inc(products, 1)

                def add(b, p):
                    wait(pe, heads_out, b * PAIRS + p + 1)
                    if p == 0:
                        wait(pe, s_ot, b)
                    nc.tensor.matmul(ps_o, WO[:, p, :], CT[:, :], start=(p == 0), stop=(p == PAIRS - 1)).then_inc(added, 1)

                def first_values():
                    pe.wait_ge(s_xb, 1)
                    for g in range(2 * QT):
                        if g >= 2:
                            wait(pe, (v_act, v_dve)[g % 2], g // 2)
                        nc.tensor.matmul(c.ps_t[:, g % 2, :], XB[:, (g // 2) * P:(g // 2 + 1) * P],
                                         WV[:, (g % 2) * 512:(g % 2 + 1) * 512], start=True, stop=True).then_inc(s_vproj, 1)

                def batch(b, first, last):
                    if first:
                        project(b, 0)
                        first_values()
                        for qt in range(QT):
                            score(b, 0, qt)
                        pe.wait_ge(v_act, QT)
                        pe.wait_ge(v_dve, QT)
                    for i in range(H):
                        p = i // 2
                        before = i % 2 == 0 and not (first and p == 0)
                        for qt in range(QT):
                            turn(b, i, qt)
                            if not (last and i == H - 1):
                                score(*ahead(b, i), qt)
                            if before and qt == 0:
                                weigh(*pair_before(b, p))
                            if before and qt == 3:
                                add(*pair_before(b, p))
                            if qt == 1 and i % 2 == 0 and not (last and p == PAIRS - 1):
                                project(*pair_after(b, p))
                            if qt == 1 and i % 2 and values_due(p, first, last):
                                project_values(b, p)
                peeled(pe, B, batch)
                weigh(B - 1, PAIRS - 1)
                add(B - 1, PAIRS - 1)

            @block.vector
            def _(dve):
                made = Chain(s_made)

                def bias(b, h, qt):
                    m = QT * h + qt
                    wait(dve, turned, b * TM + m - 2 * QT + 1)
                    wait(dve, scores, b * TM + m + 1)
                    nc.vector.memset(GO[:, :], 0.0)
                    nc.vector.tensor_tensor_reduce(
                        out=PR[:, h % 2, qt, :], in0=c.ps_s[:, qt % 2, :], in1=BH[:, h, S - P - qt * P:2 * S - P - qt * P],
                        scale=1.0, scalar=LOWEST, op0=ALU.add, op1=ALU.max, accum_out=M[:, h % 2, qt:qt + 1]).then_inc(biased, 1)
                    wait(dve, biased, b * TM + m + 1)
                    nc.vector.tensor_scalar(NM[:, h % 2, qt:qt + 1], M[:, h % 2, qt:qt + 1], -1.0, None,
                                            ALU.mult).then_inc(negated, 1)

                def norm(b, h, qt):
                    m = QT * h + qt
                    wait(dve, exped, b * TM + m + 1)
                    nc.vector.reciprocal(RDEN[:, h % 2, qt:qt + 1], DEN[:, h % 2, qt:qt + 1]).then_inc(inverted, 1)
                    wait(dve, inverted, b * TM + m + 1)
                    nc.vector.tensor_scalar(PR[:, h % 2, qt, :], PR[:, h % 2, qt, :], RDEN[:, h % 2, qt:qt + 1], None,
                                            ALU.mult).then_inc(normed, 1)

                def head(b, h, first, last):
                    making = first and b == 0
                    for qt in range(QT):
                        if making and qt == 0:
                            made.wait(dve)
                        bias(b, h, qt)
                        if qt:
                            norm(b, h, qt - 1)
                        if making and qt == 1 and h + 1 < H:
                            head_bias(dve, made, h + 1)
                        if h == 3 and qt == 0 and not last:
                            columns(b + 1)
                        if h % 2 and qt == 1 and not (first and h == 1):
                            take_heads(*pair_before(b, h // 2))
                        if h % 2 and qt == 2 and not (last and h == H - 1):
                            keys_out(*pair_after(b, h // 2))
                    norm(b, h, QT - 1)

                def columns(b):
                    if isinstance(b, int) and b == 1:
                        dve.wait_ge(s_vproj, 2 * QT)
                    wait(dve, v_pair, (b - 1) * PAIRS)
                    nc.vector.tensor_copy(XB[:, :], c.XT[:, bass.ds(b * S, S)]).then_inc(s_xb, 1)

                def keys_out(b, p):
                    wait(dve, proj, b * H + 2 * p + 2)
                    wait(dve, scores, b * TM + 2 * QT * (p - 1))
                    for e in range(2):
                        r = slice(e * HD64, (e + 1) * HD64)
                        nc.vector.tensor_copy(KZ[r, p % 2, e, :], ps_k[r, :]).then_inc(k_out, 1)

                def take_heads(b, p):
                    wait(dve, products, b * PAIRS + p + 1)
                    wait(dve, added, b * PAIRS + p)
                    nc.vector.tensor_copy(CT[:, :], c.ps_v[:, :]).then_inc(heads_out, 1)

                def batch(b, first, last):
                    if first:
                        nc.vector.tensor_copy(XB[:, :], c.XT[:, 0:S]).then_inc(s_xb, 1)
                        distances(dve, made)
                        head_bias(dve, made, 0)
                        dve.wait_ge(s_zero, 1)
                        keys_out(b, 0)
                        for g in range(1, 2 * QT, 2):
                            dve.wait_ge(s_vproj, g + 1)
                            nc.vector.tensor_copy(VB[:, g // 2, 512:1024], c.ps_t[:, 1, :]).then_inc(v_dve, 1)
                        head(b, 0, first, last)
                    for i in range(H):
                        if not (last and i == H - 1):
                            head(*ahead(b, i), first, last)
                peeled(dve, B, batch)
                take_heads(B - 1, PAIRS - 1)

            @block.scalar
            def _(act):
                def exp(b, h, qt):
                    m = QT * h + qt
                    wait(act, negated, b * TM + m + 1)
                    nc.scalar.activation(PR[:, h % 2, qt, :], PR[:, h % 2, qt, :], ACT.Exp, bias=NM[:, h % 2, qt:qt + 1],
                                         accum_out=DEN[:, h % 2, qt:qt + 1]).then_inc(exped, 1)

                def take(b, i, qt):
                    m = QT * i + qt
                    wait(act, turned, b * TM + m + 1)
                    wait(act, products, b * PAIRS + i // 2 - 1)
                    nc.scalar.activation(PT[:, i // 2 % 2, i % 2, :, qt * P:(qt + 1) * P],
                                         c.ps_t[:, qt % 2, :].rearrange("p (k q) -> p k q", q=P), ACT.Copy).then_inc(taken, 1)

                def queries_out(b, p):
                    wait(act, proj, b * H + 2 * p + 1)
                    wait(act, scores, b * TM + 2 * QT * (p - 1))
                    nc.scalar.activation(Q[:, p % 2, :], ps_q, ACT.Copy, scale=ISQ64).then_inc(q_out, 1)

                def values_out(b, p):
                    of = (p - 1) % PAIRS
                    wait(act, v_pair, b * PAIRS + p)
                    wait(act, products, b * PAIRS + p)
                    nc.scalar.activation(VB[:, :, of * P:(of + 1) * P], ps_k.rearrange("p (k d) -> p k d", k=QT),
                                         ACT.Copy).then_inc(v_out, 1)

                def output_out(b):
                    wait(act, added, b * PAIRS + PAIRS)
                    nc.scalar.activation(OT[:, bass.ds(b, 1), :].rearrange("p a t -> p (a t)"), ps_o, ACT.Copy).then_inc(s_ot, 1)

                def batch(b, first, last):
                    if first:
                        queries_out(b, 0)
                        for g in range(0, 2 * QT, 2):
                            act.wait_ge(s_vproj, g + 1)
                            nc.scalar.activation(VB[:, g // 2, 0:512], c.ps_t[:, 0, :], ACT.Copy).then_inc(v_act, 1)
                        for qt in range(QT):
                            exp(b, 0, qt)
                    for i in range(H):
                        p = i // 2
                        for qt in range(QT):
                            take(b, i, qt)
                            if not (last and i == H - 1):
                                exp(*ahead(b, i), qt)
                            if qt == 2 and i % 2 == 0 and not (last and p == PAIRS - 1):
                                queries_out(*pair_after(b, p))
                            if qt == 2 and i % 2 and values_due(p, first, last):
                                values_out(b, p)
                            if qt == 0 and i == 1 and not first:
                                output_out(b - 1)
                peeled(act, B, batch)
                output_out(B - 1)


def wide_cross_attention(c, tag, wq, bq, wk, bk, wv, bv, wo, bo, OT):
    nc = c.nc
    with ExitStack() as own:
        WQ, WK, WV = (c.sb(f"{tag}_W{n}", [P, H * HD64], F32, own) for n in "qkv")
        WO = c.sb(f"{tag}_Wo", [P, PAIRS, P], F32, own)
        BQ = c.sb(f"{tag}_BQ", [P, PAIRS], F32, own)
        BK = c.sb(f"{tag}_BK", [P, PAIRS], F32, own)
        BV = c.sb(f"{tag}_BV", [KC, H * HD64], F32, own)
        BO = c.sb(f"{tag}_BO", [P, 1], F32, own)
        KB = c.sb(f"{tag}_KB", [P, PAIRS, B, 2, KC], F32, own)
        VA = c.sb(f"{tag}_VA", [SROWS, B, H * HD64], F32, own)
        VB = c.sb(f"{tag}_VB", [SROWS, H * HD64], F32, own)
        Q = c.sb(f"{tag}_Q", [P, 2, S], F32, own)
        SC = c.sb(f"{tag}_SC", [P, 2, 2 * QT, KC], F32, own)
        PR = c.sb(f"{tag}_PR", [P, 2, 2 * QT, KC], F32, own)
        PT = c.sb(f"{tag}_PT", [SROWS, 2, S], F32, own)
        CT = c.sb(f"{tag}_CT", [P, S], F32, own)
        M = c.sb(f"{tag}_M", [P, 2 * QT], F32, own)
        DEN = c.sb(f"{tag}_DEN", [P, 2 * QT], F32, own)
        RDEN = c.sb(f"{tag}_RDEN", [P, 2 * QT], F32, own)
        (s_w, s_zero, s_scaled, s_kproj, s_kout, s_vproj, s_vout, s_vb, proj, q_out, scores, maxed, lessened, exped, summed,
         inverted, normed, turned, taken, products, heads_out, added, s_ot) = (
            c.sem(f"{tag}_{n}") for n in
            ("w", "zero", "scaled", "kproj", "kout", "vproj", "vout", "vb", "proj", "q_out", "scores", "maxed", "lessened",
             "exped", "summed", "inverted", "normed", "turned", "taken", "products", "heads_out", "added", "ot"))
        N_W = 16 * 8

        with nc.Block() as block:
            @block.sync
            def _(sp):
                for dst, src in ((WQ, wq), (WK, wk), (WV, wv)):
                    sp.dma_start(dst[:, :], src.rearrange("m h d -> m (h d)")).then_inc(s_w, 16)
                sp.dma_start(WO[:, :, :], wo.rearrange("(g e) d n -> (e d) g n", e=2)).then_inc(s_w, 16)
                sp.dma_start(BQ[:, :], bq.rearrange("(g e) d -> (e d) g", e=2),
                             allow_slow_non_contiguous=True).then_inc(s_w, 16)
                sp.dma_start(BK[:, :], bk.rearrange("(g e) d -> (e d) g", e=2),
                             allow_slow_non_contiguous=True).then_inc(s_w, 16)
                sp.dma_start(BV[:, :], row(bv.rearrange("h d -> (h d)"), KC)).then_inc(s_w, 16)
                sp.dma_start(BO[:, :], col(bo)).then_inc(s_w, 16)

            @block.gpsimd
            def _(pool):
                nc.gpsimd.memset(KB[:, :, :, :, :], 0.0).then_inc(s_zero, 1)
                pool.wait_ge(s_zero, 1)
                nc.gpsimd.memset(VA[64:SROWS, :, :], 0.0).then_inc(s_zero, 1)
                pool.wait_ge(s_zero, 2)
                nc.gpsimd.memset(PT[64:SROWS, :, :], 0.0)

            @block.tensor
            def _(pe):
                pe.wait_ge(s_w, N_W)
                for p in range(PAIRS):
                    if p >= 2:
                        pe.wait_ge(s_kout, 2 * (p - 1))
                    nc.tensor.matmul(c.ps_s[:, p % 2, 0:B * KC], WK[:, p * P:(p + 1) * P], c.CTT[:, :],
                                     start=True, stop=True).then_inc(s_kproj, 1)
                    b, half = p // 2, p % 2
                    if p >= 2:
                        pe.wait_ge(s_vout, p - 1)
                    nc.tensor.matmul(c.ps_t[0:KC, half, :], c.CTT[:, b * KC:(b + 1) * KC], WV[:, half * 512:(half + 1) * 512],
                                     start=True, stop=True).then_inc(s_vproj, 1)

            @block.vector
            def _(dve):
                dve.wait_ge(s_w, N_W)
                nc.vector.tensor_scalar(BQ[:, :], BQ[:, :], ISQ64, None, ALU.mult).then_inc(s_scaled, 1)
                dve.wait_ge(s_zero, 2)
                for p in range(PAIRS):
                    dve.wait_ge(s_kproj, p + 1)
                    for e in range(2):
                        r = slice(e * HD64, (e + 1) * HD64)
                        nc.vector.tensor_scalar(KB[r, p, :, e, :], c.ps_s[r, p % 2, 0:B * KC].rearrange("p (b k) -> p b k", b=B),
                                                BK[r, p:p + 1], None, ALU.add).then_inc(s_kout, 1)
                    b, half = p // 2, p % 2
                    dve.wait_ge(s_vproj, p + 1)
                    v = slice(half * 512, (half + 1) * 512)
                    nc.vector.tensor_tensor(VA[0:KC, b, v], c.ps_t[0:KC, half, :], BV[:, v], ALU.add).then_inc(s_vout, 1)

        def ahead(b, p, k):
            return (b, p + k) if p + k < PAIRS else (b + 1, p + k - PAIRS)

        def more(p, k, last):
            return not last or p + k < PAIRS

        with nc.Block() as block:
            @block.tensor
            def _(pe):
                def project(b, p):
                    wait(pe, q_out, b * PAIRS + p)
                    nc.tensor.matmul(c.ps_s[:, 2, :], WQ[:, p * P:(p + 1) * P], c.XT[:, bass.ds(b * S, S)],
                                     start=True, stop=True).then_inc(proj, 1)

                def score(b, p):
                    wait(pe, q_out, b * PAIRS + p + 1)
                    wait(pe, lessened, b * PAIRS + p)
                    for qt in range(QT):
                        mm = nc.tensor.matmul(c.ps_s[:, qt // 2, (qt % 2) * 2 * KC:(qt % 2 + 1) * 2 * KC],
                                              Q[:, p % 2, qt * P:(qt + 1) * P],
                                              KB[:, p, bass.ds(b, 1), :, :].rearrange("p a e k -> p (a e k)"),
                                              start=True, stop=True)
                    mm.then_inc(scores, 1)

                def turn(b, p):
                    wait(pe, normed, b * PAIRS + p + 1)
                    wait(pe, taken, b * PAIRS + p)
                    for e in range(2):
                        for qt in range(QT):
                            mm = nc.tensor.transpose(c.ps_t[0:KC, e, qt * P:(qt + 1) * P], PR[:, p % 2, 2 * qt + e, :],
                                                     c.ident[:, :])
                    mm.then_inc(turned, 1)

                def weigh(b, p):
                    if p == 0:
                        wait(pe, s_vb, b + 1)
                    wait(pe, taken, b * PAIRS + p + 1)
                    wait(pe, heads_out, b * PAIRS + p)
                    for e in range(2):
                        h = 2 * p + e
                        mm = nc.tensor.matmul(c.ps_v[e * HD64:(e + 1) * HD64, :], VB[:, h * HD64:(h + 1) * HD64], PT[:, e, :],
                                              start=True, stop=True)
                    mm.then_inc(products, 1)

                def add(b, p):
                    wait(pe, heads_out, b * PAIRS + p + 1)
                    if p == 0:
                        wait(pe, s_ot, b)
                    nc.tensor.matmul(c.ps_f[:, :], WO[:, p, :], CT[:, :], start=(p == 0), stop=(p == PAIRS - 1)).then_inc(added, 1)

                def batch(b, first, last):
                    if first:
                        project(b, 0)
                        project(b, 1)
                        score(b, 0)
                        project(b, 2)
                        score(b, 1)
                    for p in range(PAIRS):
                        if more(p, 2, last):
                            score(*ahead(b, p, 2))
                        turn(b, p)
                        if more(p, 3, last):
                            project(*ahead(b, p, 3))
                        if not (first and p == 0):
                            add(*((b, p - 1) if p else (b - 1, PAIRS - 1)))
                        weigh(b, p)
                peeled(pe, B, batch)
                add(B - 1, PAIRS - 1)

            @block.vector
            def _(dve):
                def lessen(b, p):
                    n = b * PAIRS + p
                    src = c.ps_s[:, 0:2, 0:4 * KC].rearrange("p a (m k) -> p a m k", k=KC)
                    dve.wait_ge(scores, n + 1)
                    nc.vector.reduce_max(M[:, :].rearrange("p (a m) -> p a m", a=2), src, AX.X).then_inc(maxed, 1)
                    dve.wait_ge(maxed, n + 1)
                    wait(dve, exped, n - 1)
                    nc.vector.tensor_tensor(SC[:, p % 2].rearrange("p (a m) k -> p a m k", a=2), src,
                                            M[:, :].rearrange("p (a m b) -> p a m b", a=2, b=1).broadcast_to([P, 2, 4, KC]),
                                            ALU.subtract).then_inc(lessened, 1)

                def norm(b, p):
                    n = b * PAIRS + p
                    dve.wait_ge(exped, n + 1)
                    nc.vector.reduce_sum(DEN[:, :], PR[:, p % 2], AX.X).then_inc(summed, 1)
                    dve.wait_ge(summed, n + 1)
                    nc.vector.reciprocal(RDEN[:, :], DEN[:, :]).then_inc(inverted, 1)
                    dve.wait_ge(inverted, n + 1)
                    nc.vector.tensor_tensor(PR[:, p % 2], PR[:, p % 2],
                                            RDEN[:, :].rearrange("p (m a) -> p m a", a=1).broadcast_to([P, 2 * QT, KC]),
                                            ALU.mult).then_inc(normed, 1)

                def take_heads(b, p):
                    n = b * PAIRS + p
                    dve.wait_ge(products, n + 1)
                    dve.wait_ge(added, n)
                    nc.vector.tensor_copy(CT[:, :], c.ps_v[:, :]).then_inc(heads_out, 1)

                def batch(b, first, last):
                    wait(dve, products, b * PAIRS)
                    nc.vector.tensor_copy(VB[:, :], VA[:, bass.ds(b, 1), :].rearrange("p a n -> p (a n)")).then_inc(s_vb, 1)
                    if first:
                        lessen(b, 0)
                        norm(b, 0)
                        lessen(b, 1)
                    for p in range(PAIRS):
                        if more(p, 2, last):
                            lessen(*ahead(b, p, 2))
                        if more(p, 1, last):
                            norm(*ahead(b, p, 1))
                        take_heads(b, p)
                peeled(dve, B, batch)

            @block.scalar
            def _(act):
                def exp(b, p):
                    n = b * PAIRS + p
                    act.wait_ge(lessened, n + 1)
                    wait(act, turned, n - 1)
                    nc.scalar.activation(PR[:, p % 2], SC[:, p % 2], ACT.Exp).then_inc(exped, 1)

                def queries_out(b, p):
                    n = b * PAIRS + p
                    act.wait_ge(proj, n + 1)
                    wait(act, scores, n - 1)
                    nc.scalar.activation(Q[:, p % 2, :], c.ps_s[:, 2, :], ACT.Identity, bias=BQ[:, p:p + 1],
                                         scale=ISQ64).then_inc(q_out, 1)

                def output_out(b):
                    wait(act, added, b * PAIRS + PAIRS)
                    nc.scalar.activation(OT[:, bass.ds(b, 1), :].rearrange("p a t -> p (a t)"), c.ps_f[:, :], ACT.Identity,
                                         bias=BO[:, 0:1]).then_inc(s_ot, 1)

                def batch(b, first, last):
                    if first:
                        queries_out(b, 0)
                        queries_out(b, 1)
                        exp(b, 0)
                        queries_out(b, 2)
                        exp(b, 1)
                    for p in range(PAIRS):
                        act.wait_ge(turned, b * PAIRS + p + 1)
                        wait(act, products, b * PAIRS + p)
                        nc.scalar.activation(PT[0:KC, :, :], c.ps_t[0:KC, :, :], ACT.Copy).then_inc(taken, 1)
                        if more(p, 2, last):
                            exp(*ahead(b, p, 2))
                        if more(p, 3, last):
                            queries_out(*ahead(b, p, 3))
                        if p == 0 and not first:
                            output_out(b - 1)
                peeled(act, B, batch)
                output_out(B - 1)


def gates(c, tag, own, wg, GATE):
    nc = c.nc
    WG = c.sb(f"{tag}_WG", [P, NE], F32, own)
    L = c.sb(f"{tag}_L", [P, NT, NE], F32, own)
    E = c.sb(f"{tag}_E", [P, NT, NE], F32, own)
    C1 = c.sb(f"{tag}_C1", [P, NT, NE, NE], F32, own)
    C2 = c.sb(f"{tag}_C2", [P, NT, NE, NE], F32, own)
    LOW = c.sb(f"{tag}_LOW", [P, NE, NE], F32, own)
    RK = c.sb(f"{tag}_RK", [P, NT, NE], F32, own)
    M = c.sb(f"{tag}_GM", [P, NT], F32, own)
    s_w, s_low, s_logits, s_chain, s_exp, s_shared = (
        c.sem(f"{tag}_g{n}") for n in ("w", "low", "logits", "chain", "exp", "shared"))

    def load(sp):
        sp.dma_start(WG[:, :], wg).then_inc(s_w, 16)

    def pool_part(pool):
        nc.gpsimd.memset(LOW[:, :, :], 1.0).then_inc(s_low, 1)
        pool.wait_ge(s_low, 1)
        nc.gpsimd.affine_select(out=LOW[:, :, :], in_=LOW[:, :, :], compare_op=ALU.is_gt, fill=0.0, base=0,
                                pattern=[[1, NE], [-1, NE]], channel_multiplier=0).then_inc(s_low, 1)

    def tensor_part(pe):
        pe.wait_ge(s_w, 16)
        for n in range(NT):
            last = nc.tensor.matmul(c.ps_f[:, n * NE:(n + 1) * NE], c.XT[:, n * P:(n + 1) * P], WG[:, :],
                                    start=True, stop=True)
        last.then_inc(s_logits, 1)

    def scalar_part(act):
        act.wait_ge(s_chain, 3)
        nc.scalar.activation(E[:, :, :], E[:, :, :], ACT.Exp).then_inc(s_exp, 1)

    def vector_part(dve):
        chain = Chain(s_chain)
        if GATE.shape[2] > NE:
            nc.vector.memset(GATE[:, :, NE:], 1.0).then_inc(s_shared, 1)
            dve.wait_ge(s_shared, 1)
        dve.wait_ge(s_logits, 1)
        chain.inc(nc.vector.tensor_copy(L[:, :, :], c.ps_f[:, 0:NT * NE].rearrange("p (n e) -> p n e", e=NE)))
        chain.wait(dve)
        chain.inc(nc.vector.reduce_max(M[:, :], L[:, :, :], AX.X))
        chain.wait(dve)
        by_tile = M[:, :].rearrange("p (n a) -> p n a", a=1).broadcast_to([P, NT, NE])
        chain.inc(nc.vector.tensor_tensor(E[:, :, :], L[:, :, :], by_tile, ALU.subtract))
        of_e = L[:, :, :].rearrange("p n (e a) -> p n e a", a=1).broadcast_to([P, NT, NE, NE])
        of_j = L[:, :, :].rearrange("p n (a j) -> p n a j", a=1).broadcast_to([P, NT, NE, NE])
        chain.inc(nc.vector.tensor_tensor(C1[:, :, :, :], of_j, of_e, ALU.is_gt))
        chain.inc(nc.vector.tensor_tensor(C2[:, :, :, :], of_j, of_e, ALU.is_equal))
        chain.wait(dve)
        dve.wait_ge(s_low, 2)
        c2 = C2[:, :, :, :].rearrange("p n e j -> p n (e j)")
        chain.inc(nc.vector.tensor_tensor(
            c2, c2, LOW[:, :, :].rearrange("p (a e) j -> p a (e j)", a=1).broadcast_to([P, NT, NE * NE]), ALU.mult))
        chain.wait(dve)
        chain.inc(nc.vector.tensor_tensor(C1[:, :, :, :], C1[:, :, :, :], C2[:, :, :, :], ALU.add))
        chain.wait(dve)
        chain.inc(nc.vector.reduce_sum(RK[:, :, :], C1[:, :, :, :], AX.X))
        chain.wait(dve)
        dve.wait_ge(s_exp, 1)
        gate = GATE[:, :, 0:NE]
        chain.inc(nc.vector.scalar_tensor_tensor(gate, RK[:, :, :], 2.0, E[:, :, :], ALU.is_lt, ALU.mult))
        chain.wait(dve)
        chain.inc(nc.vector.reduce_sum(M[:, :], gate, AX.X))
        chain.wait(dve)
        chain.inc(nc.vector.reciprocal(M[:, :], M[:, :]))
        chain.wait(dve)
        chain.inc(nc.vector.tensor_tensor(gate, gate, by_tile, ALU.mult))
        chain.wait(dve)

    return Beside(load, pool_part, tensor_part, vector_part, scalar_part)


def experts(c, tag, wg, GATE, w1, w2, w3=None, b1=None, b2=None, shared=None):
    nc = c.nc
    hid = w1.shape[2]
    CH = hid // P
    gated = w3 is not None
    total = NE + (shared is not None)
    with ExitStack() as own:
        W1 = [c.sb(f"{tag}_W1{i}", [P, hid], F32, own) for i in range(2)]
        W3 = [c.sb(f"{tag}_W3{i}", [P, hid], F32, own) for i in range(2)] if gated else None
        W2 = [c.sb(f"{tag}_W2{i}", [P, CH, P], F32, own) for i in range(2)]
        HT = c.sb(f"{tag}_HT", [P, 2, CH, S], F32, own)
        GT = c.sb(f"{tag}_GT", [P, 2, CH, S], F32, own) if gated else None
        B1 = c.sb(f"{tag}_B1", [P, NE, CH], F32, own) if not gated else None
        BE = c.sb(f"{tag}_BE", [P, 2, CH], F32, own) if not gated else None
        B2 = c.sb(f"{tag}_B2", [P, NE, P], F32, own) if not gated else None
        s_w = [c.sem(f"{tag}_w{i}") for i in range(2)]
        s_b, s_be, s_first, s_act, s_hidden, s_second, s_added = (
            c.sem(f"{tag}_{n}") for n in ("bias", "be", "first", "act", "hidden", "second", "added"))
        N_W = 16 * (3 if gated else 2)
        ADDS = QT if gated else 2 * QT
        sources = (w1, w2) + ((w3,) if gated else ())

        def load(sp, e, i, shared_too=False):
            if shared_too:
                srcs = ((W1[i][:, :], shared[0]), (W3[i][:, :], shared[1]),
                        (W2[i][:, :, :], shared[2].rearrange("(c p) n -> p c n", p=P)))
            else:
                srcs = ((W1[i][:, :], w1[e]), (W2[i][:, :, :], w2[e].rearrange("(c p) n -> p c n", p=P)))
                if gated:
                    srcs += ((W3[i][:, :], w3[e]),)
            for dst, src in srcs:
                sp.dma_start(dst, src).then_inc(s_w[i], 16)

        def run(engine, one):
            def pair(t, first, last):
                for i in range(2):
                    one(t, i, first and i == 0, last and i == 1 and total % 2 == 0)
            if total % 2:
                pair(0, True, False)
                with engine.Fori(1, total // 2) as t:
                    pair(t, False, False)
                one(total // 2, 0, False, True)
            else:
                peeled(engine, total // 2, pair)

        gating = gates(c, tag, own, wg, GATE)

        with nc.Block() as block:
            @block.gpsimd
            def _(pool):
                gating.pool(pool)

            @block.sync
            def _(sp):
                gating.load(sp)
                if not gated:
                    sp.dma_start(B1[:, :, :], b1.rearrange("e (c p) -> p e c", p=P), allow_slow_non_contiguous=True).then_inc(s_b, 16)
                    sp.dma_start(B2[:, :, :].rearrange("p e n -> p (e n)"), row(b2.rearrange("e n -> (e n)"))).then_inc(s_b, 16)
                load(sp, 0, 0)
                load(sp, 1, 1)
                for e in range(2, NE):
                    sp.wait_ge(s_second, (e - 1) * B)
                    sp.wait_ge(s_w[e % 2], e // 2 * N_W)
                    load(sp, e, e % 2)
                if shared is not None:
                    sp.wait_ge(s_second, (NE - 1) * B)
                    sp.wait_ge(s_w[0], NE // 2 * N_W)
                    load(sp, None, 0, True)

            @block.tensor
            def _(pe):
                gating.tensor(pe)

                def first_products(t, i, b, first):
                    k = (2 * t + i) * B + b
                    if b == 0:
                        pe.wait_ge(s_w[i], (t + 1) * N_W)
                    for ch in range(2 * CH if gated else CH):
                        if not first:
                            if gated and ch >= CH:
                                pe.wait_ge(s_hidden, (k - 1) * CH + ch - CH + 1)
                            else:
                                pe.wait_ge(s_act, (k - 1) * CH + ch + 1)
                        W = W3[i] if gated and ch >= CH else W1[i]
                        nc.tensor.matmul(c.ps_s[:, ch, :], W[:, (ch % CH) * P:(ch % CH + 1) * P], c.XT[:, b * S:(b + 1) * S],
                                         start=True, stop=True).then_inc(s_first, 1)

                def second_products(t, i, b, first):
                    k = (2 * t + i) * B + b
                    pe.wait_ge(s_hidden if gated else s_act, (k + 1) * CH)
                    if not (first and b < 2):
                        pe.wait_ge(s_added, (k - 1) * ADDS)
                    for q in range(QT):
                        for ch in range(CH):
                            mm = nc.tensor.matmul(c.ps_t[:, b % 2, q * P:(q + 1) * P], HT[:, b % 2, ch, q * P:(q + 1) * P],
                                                  W2[i][:, ch, :], start=(ch == 0), stop=(ch == CH - 1))
                    mm.then_inc(s_second, 1)

                def one(t, i, first, last):
                    for b in range(B):
                        if b + 1 < B:
                            first_products(t, i, b + 1, False)
                        elif not last:
                            first_products(t + i, 1 - i, 0, False)
                        second_products(t, i, b, first)
                first_products(0, 0, 0, True)
                run(pe, one)

            @block.scalar
            def _(act):
                gating.scalar(act)
                if not gated:
                    act.wait_ge(s_b, 32)

                def one(t, i, first, last):
                    if not gated:
                        nc.scalar.activation(BE[:, i, :], B1[:, bass.ds(2 * t + i, 1), :].rearrange("p a c -> p (a c)"),
                                             ACT.Copy).then_inc(s_be, 1)
                        act.wait_ge(s_be, 2 * t + i + 1)
                    for b in range(B):
                        k = (2 * t + i) * B + b
                        for ch in range(CH):
                            act.wait_ge(s_first, k * (2 * CH if gated else CH) + ch + 1)
                            if not (first and b < 2):
                                if gated:
                                    act.wait_ge(s_hidden, (k - 2) * CH + ch + 1)
                                else:
                                    act.wait_ge(s_second, k - 1)
                            if gated:
                                nc.scalar.activation(GT[:, b % 2, ch, :], c.ps_s[:, ch, :], ACT.Silu).then_inc(s_act, 1)
                            else:
                                nc.scalar.activation(HT[:, b % 2, ch, :], c.ps_s[:, ch, :], ACT.Gelu_apprx_tanh,
                                                     bias=BE[:, i, ch:ch + 1]).then_inc(s_act, 1)
                run(act, one)

            @block.vector
            def _(dve):
                gating.vector(dve)
                if not gated:
                    dve.wait_ge(s_b, 32)

                def hidden(t, i, b, first):
                    k = (2 * t + i) * B + b
                    for ch in range(CH):
                        dve.wait_ge(s_first, k * 2 * CH + CH + ch + 1)
                        dve.wait_ge(s_act, k * CH + ch + 1)
                        if not (first and b < 2):
                            dve.wait_ge(s_second, k - 1)
                        nc.vector.tensor_tensor(HT[:, b % 2, ch, :], GT[:, b % 2, ch, :], c.ps_s[:, CH + ch, :],
                                                ALU.mult).then_inc(s_hidden, 1)

                def add(t, i, b, first):
                    k = (2 * t + i) * B + b
                    e = 2 * t + i
                    if not gated:
                        if not (first and b == 0):
                            dve.wait_ge(s_added, k * ADDS)
                        for q in range(QT):
                            x = c.X[:, b * QT + q, :]
                            gate = GATE[:, b * QT + q, bass.ds(e, 1)]
                            nc.vector.scalar_tensor_tensor(x, B2[:, bass.ds(e, 1), :].rearrange("p a n -> p (a n)"), gate, x,
                                                           ALU.mult, ALU.add).then_inc(s_added, 1)
                        dve.wait_ge(s_added, k * ADDS + QT)
                    elif not (first and b == 0):
                        dve.wait_ge(s_added, k * ADDS)
                    dve.wait_ge(s_second, k + 1)
                    for q in range(QT):
                        x = c.X[:, b * QT + q, :]
                        gate = GATE[:, b * QT + q, bass.ds(e, 1)]
                        nc.vector.scalar_tensor_tensor(x, c.ps_t[:, b % 2, q * P:(q + 1) * P], gate, x,
                                                       ALU.mult, ALU.add).then_inc(s_added, 1)

                def one(t, i, first, last):
                    for b in range(B):
                        if gated:
                            if b + 1 < B:
                                hidden(t, i, b + 1, first)
                            elif not last:
                                hidden(t + i, 1 - i, 0, False)
                        add(t, i, b, first)
                if gated:
                    hidden(0, 0, 0, True)
                run(dve, one)


def decoder(nc, a, out):
    scratch = nc.dram_tensor("split_parts", (B, 2, P, NPART, S), BF16, kind="Internal").ap()
    with ExitStack() as ctx:
        c = Core(nc, ctx)
        setup(c, a["x"], a["ctx_1024"])

        with ExitStack() as narrow:
            stacks(c, narrow)
            narrow_self_attention(c, "a", a["L0_attn_Wq"], a["L0_attn_Wk"], a["L0_attn_Wv"], scratch, rel=a["L0_attn_rel_emb"])
            finish(c, "a", "ctx", wo=a["L0_attn_Wo"], bias=a["L0_attn_bo"])
            narrow_cross_attention(c, "b", a["L0_xattn_Wq"], a["L0_xattn_bq"], a["L0_xattn_Wk"], a["L0_xattn_bk"],
                                   a["L0_xattn_Wv"], a["L0_xattn_bv"], scratch)
            finish(c, "b", "ctx", wo=a["L0_xattn_Wo"], bias=a["L0_xattn_bo"], pre=(a["L0_ffn_ln1_w"], a["L0_ffn_ln1_b"]))
            q, k, v = (slice(i * P, (i + 1) * P) for i in range(3))
            w, b = a["L0_ffn_w_qkv"], a["L0_ffn_b_qkv"]
            narrow_self_attention(c, "c", w[:, q], w[:, k], w[:, v], scratch, b[q], b[k], b[v], qscale=ISQ8)
            finish(c, "c", "ctx", wo=a["L0_ffn_w_o"], bias=a["L0_ffn_b_o"], mode="inner",
                   pre=(a["L0_ffn_ln2_w"], a["L0_ffn_ln2_b"]))
        with ExitStack() as own:
            GATE = c.sb("GATE0", [P, NT, NE], F32, own)
            experts(c, "f", a["L0_ffn_w_gate"], GATE, a["L0_ffn_w1"], a["L0_ffn_w2"], b1=a["L0_ffn_b1"], b2=a["L0_ffn_b2"])
        finish(c, "f", "x", pre=(a["L1_attn_ln_gamma"], a["L1_attn_ln_beta"]))
        c.recycle_semaphores()
        with ExitStack() as own:
            OT = c.sb("OT_d", [P, B, S], F32, own)
            wide_self_attention(c, "d", a["L1_attn_Wq"], a["L1_attn_Wk"], a["L1_attn_Wv"], a["L1_attn_Wo"], OT)
            finish(c, "d", "dm", OT=OT)
        with ExitStack() as own:
            OT = c.sb("OT_e", [P, B, S], F32, own)
            wide_cross_attention(c, "e", *(a[f"L1_xattn_{n}"] for n in ("Wq", "bq", "Wk", "bk", "Wv", "bv", "Wo", "bo")), OT)
            finish(c, "e", "dm", OT=OT)
        with ExitStack() as own:
            GATE = c.sb("GATE1", [P, NT, NE + 1], F32, own)
            experts(c, "g", a["L1_ffn_w_router"], GATE, a["L1_ffn_w1"], a["L1_ffn_w2"], w3=a["L1_ffn_w3"],
                    shared=(a["L1_ffn_sw1"], a["L1_ffn_sw3"], a["L1_ffn_sw2"]))
        finish(c, "g", "x", out=out)


_NAMES = ["x", "ctx_1024"] \
    + [f"L0_attn_{n}" for n in ("Wq", "Wk", "Wv", "Wo", "bo", "rel_emb")] \
    + [f"L0_xattn_{n}" for n in ("Wq", "bq", "Wk", "bk", "Wv", "bv", "Wo", "bo")] \
    + [f"L0_ffn_{n}" for n in ("ln1_w", "ln1_b", "ln2_w", "ln2_b", "w_qkv", "b_qkv", "w_o", "b_o", "w_gate",
                               "w1", "b1", "w2", "b2")] \
    + [f"L1_attn_{n}" for n in ("ln_gamma", "ln_beta", "Wq", "Wk", "Wv", "Wo")] \
    + [f"L1_xattn_{n}" for n in ("Wq", "bq", "Wk", "bk", "Wv", "bv", "Wo", "bo")] \
    + [f"L1_ffn_{n}" for n in ("w_router", "w1", "w3", "w2", "sw1", "sw3", "sw2")]


def kernel(**inputs):
    import numpy as np
    import concourse.bacc as bacc
    from concourse.bass_utils import run_bass_kernel_spmd

    nc = bacc.Bacc("TRN2", target_bir_lowering=False, num_devices=1)
    arrays, aps = {}, {}
    for name in _NAMES:
        array = np.ascontiguousarray(inputs[name])
        arrays[f"in_{name}"] = array
        aps[name] = nc.dram_tensor(f"in_{name}", array.shape, mybir.dt.from_np(array.dtype), kind="ExternalInput").ap()
    out = nc.dram_tensor("out", (B, S, P), F32, kind="ExternalOutput").ap()
    decoder(nc, aps, out)
    result = run_bass_kernel_spmd(nc, [arrays], core_ids=[0])
    return result.results[0]["out"]
```
